# Optimizing a Trainium2 kernel written in Bass

```python
import numpy as np
import jax
import jax.numpy as jnp

def _softmax(x, axis=-1):
    return jax.nn.softmax(x, axis=axis)

def _gelu(x):
    return jax.nn.gelu(x, approximate=True)

def _silu(x):
    return jax.nn.silu(x)

def _sigmoid(x):
    return jax.nn.sigmoid(x)

def _layernorm(x, axis=-1, eps=1e-05):
    m = jnp.mean(x, axis=axis, keepdims=True)
    v = jnp.var(x, axis=axis, keepdims=True)
    return (x - m) / jnp.sqrt(v + eps)

def _scatter_add(tgt, idx, src, axis=0):
    return tgt.at[idx].add(src)

def _segment_sum(src, seg, n):
    return jax.ops.segment_sum(src, seg, n)
kernel_name = 'mk_gnn_preln_d2_gnn_r8_348419'

def setup_inputs(seed: int=0):
    np.random.seed(seed)
    _w = jnp.asarray

    def _rec_inputs():
        import jax
        import jax.numpy as jnp
        _gk = jax.random.key(seed)
        x = -6.415e-05 + 1 * jax.random.normal(jax.random.fold_in(_gk, 1), (1250, 512), jnp.float32)
        _s = jax.random.randint(jax.random.fold_in(_gk, 2), (10000,), 0, 1250, jnp.int32)
        _d = jax.random.randint(jax.random.fold_in(_gk, 3), (10000,), 0, 1250, jnp.int32)
        _loop = jnp.arange(1250, dtype=jnp.int32)
        src = jnp.concatenate([_s, _d, _loop])
        dst = jnp.concatenate([_d, _s, _loop])
        _o = jnp.argsort(dst, stable=True)
        src = src[_o]
        dst = dst[_o]
        edge_attr_64 = 0.000279952 + 1.00013 * jax.random.normal(jax.random.fold_in(_gk, 12), (21250, 64), jnp.float32)
        edge_type_32 = jax.random.randint(jax.random.fold_in(_gk, 14), (21250,), 0, 32, jnp.int32)
        edge_weight1 = jax.random.uniform(jax.random.fold_in(_gk, 15), (21250, 1), jnp.float32, 0.0, 0.999996)
        return (x, src, dst, edge_attr_64, edge_type_32, edge_weight1)
    x, src, dst, edge_attr_64, edge_type_32, edge_weight1 = _rec_inputs()

    def _L0_gnn_setup():
        import jax, jax.numpy as jnp
        import numpy as np
        N_NODES = 2500
        N_EDGES = 40000
        IN_FEAT = 512
        OUT_FEAT = 512
        NUM_RELS = 32
        NUM_BASES = 8
        key = jax.random.key(seed)
        ks = jax.random.split(key, 8)
        x = jax.random.normal(ks[0], (N_NODES, IN_FEAT), dtype=jnp.float32)
        bases = jax.random.normal(ks[1], (NUM_BASES, IN_FEAT, OUT_FEAT), dtype=jnp.float32) * (1.0 / np.sqrt(IN_FEAT))
        w_comp = jax.random.normal(ks[2], (NUM_RELS, NUM_BASES), dtype=jnp.float32) * (1.0 / np.sqrt(NUM_BASES))
        h_bias = jnp.zeros((OUT_FEAT,), dtype=jnp.float32)
        norm = jax.random.uniform(ks[3], (N_EDGES, 1), dtype=jnp.float32)
        src = jax.random.randint(ks[4], (N_EDGES,), 0, N_NODES, dtype=jnp.int32)
        dst = jax.random.randint(ks[5], (N_EDGES,), 0, N_NODES, dtype=jnp.int32)
        etype = jnp.sort(jax.random.randint(ks[6], (N_EDGES,), 0, NUM_RELS, dtype=jnp.int32))
        return {'x': x, 'bases': bases, 'w_comp': w_comp, 'h_bias': h_bias, 'norm': norm, 'src': src, 'dst': dst, 'etype': etype}
    _L0_gnn_all = _L0_gnn_setup()
    _L0_gnn_in = {k: v for k, v in _L0_gnn_all.items() if k in ('bases', 'w_comp', 'h_bias')}
    del _L0_gnn_all

    def _L1_gnn_setup():
        import jax, jax.numpy as jnp
        import numpy as np
        N_NODES = 2500
        N_EDGES = 40000
        HIDDEN = 512
        EDGE_DIM = 64
        LN_EPS = 1e-05

        def mish(x):
            return x * jnp.tanh(jax.nn.softplus(x))
        key = jax.random.key(seed)
        ks = jax.random.split(key, 8)
        s = lambda fan_in: 1.0 / np.sqrt(fan_in)
        return {'x': jax.random.normal(ks[0], (N_NODES, HIDDEN), dtype=jnp.float32), 'edge_index': jax.random.randint(ks[1], (2, N_EDGES), 0, N_NODES, dtype=jnp.int64), 'edge_attr': jax.random.normal(ks[2], (N_EDGES, EDGE_DIM), dtype=jnp.float32), 'W1': jax.random.normal(ks[3], (2 * HIDDEN + EDGE_DIM, HIDDEN), dtype=jnp.float32) * s(2 * HIDDEN + EDGE_DIM), 'b1': jnp.zeros((HIDDEN,), dtype=jnp.float32), 'W2': jax.random.normal(ks[4], (HIDDEN, HIDDEN), dtype=jnp.float32) * s(HIDDEN), 'b2': jnp.zeros((HIDDEN,), dtype=jnp.float32), 'W3': jax.random.normal(ks[5], (2 * HIDDEN, HIDDEN), dtype=jnp.float32) * s(2 * HIDDEN), 'b3': jnp.zeros((HIDDEN,), dtype=jnp.float32), 'W4': jax.random.normal(ks[6], (HIDDEN, HIDDEN), dtype=jnp.float32) * s(HIDDEN), 'b4': jnp.zeros((HIDDEN,), dtype=jnp.float32), 'gamma': jnp.ones((HIDDEN,), dtype=jnp.float32), 'beta': jnp.zeros((HIDDEN,), dtype=jnp.float32)}
    _L1_gnn_all = _L1_gnn_setup()
    _L1_gnn_in = {k: v for k, v in _L1_gnn_all.items() if k in ('W1', 'b1', 'W2', 'b2', 'W3', 'b3', 'W4', 'b4', 'gamma', 'beta')}
    del _L1_gnn_all
    return {'x': x, 'src': src, 'dst': dst, 'edge_attr_64': edge_attr_64, 'edge_type_32': edge_type_32, 'edge_weight1': edge_weight1, 'L0_gnn_bases': _L0_gnn_in['bases'], 'L0_gnn_w_comp': _L0_gnn_in['w_comp'], 'L0_gnn_h_bias': _L0_gnn_in['h_bias'], 'L1_gnn_W1': _L1_gnn_in['W1'], 'L1_gnn_b1': _L1_gnn_in['b1'], 'L1_gnn_W2': _L1_gnn_in['W2'], 'L1_gnn_b2': _L1_gnn_in['b2'], 'L1_gnn_W3': _L1_gnn_in['W3'], 'L1_gnn_b3': _L1_gnn_in['b3'], 'L1_gnn_W4': _L1_gnn_in['W4'], 'L1_gnn_b4': _L1_gnn_in['b4'], 'L1_gnn_gamma': _L1_gnn_in['gamma'], 'L1_gnn_beta': _L1_gnn_in['beta']}

def reference(x, src, dst, edge_attr_64, edge_type_32, edge_weight1, L0_gnn_bases, L0_gnn_w_comp, L0_gnn_h_bias, L1_gnn_W1, L1_gnn_b1, L1_gnn_W2, L1_gnn_b2, L1_gnn_W3, L1_gnn_b3, L1_gnn_W4, L1_gnn_b4, L1_gnn_gamma, L1_gnn_beta):
    import jax
    import jax.numpy as jnp

    def _L0_gnn_ref(x, bases, w_comp, h_bias, norm, src, dst, etype):
        import jax, jax.numpy as jnp
        import numpy as np
        N_NODES = 2500
        N_EDGES = 40000
        IN_FEAT = 512
        OUT_FEAT = 512
        NUM_RELS = 32
        NUM_BASES = 8
        n_nodes = x.shape[0]
        weight = jnp.einsum('rb,bio->rio', w_comp, bases)
        h_rel = jnp.einsum('ni,rio->rno', x, weight)
        msg = h_rel[etype, src] * norm
        out = jax.ops.segment_sum(msg, dst, num_segments=n_nodes)
        out = out + h_bias
        return out

    def _L1_gnn_ref(x, edge_index, edge_attr, W1, b1, W2, b2, W3, b3, W4, b4, gamma, beta):
        import jax, jax.numpy as jnp
        import numpy as np
        N_NODES = 2500
        N_EDGES = 40000
        HIDDEN = 512
        EDGE_DIM = 64
        LN_EPS = 1e-05

        def mish(x):
            return x * jnp.tanh(jax.nn.softplus(x))
        src, dst = (edge_index[0], edge_index[1])
        edge_feat = jnp.concatenate([x[src], x[dst], edge_attr], axis=-1)
        h = mish(edge_feat @ W1 + b1)
        messages = mish(h @ W2 + b2)
        agg = jax.ops.segment_sum(messages, dst, num_segments=x.shape[0])
        u = mish(jnp.concatenate([x, agg], axis=-1) @ W3 + b3)
        out = u @ W4 + b4
        y = x + out
        mu = jnp.mean(y, axis=-1, keepdims=True)
        var = jnp.mean(jnp.square(y - mu), axis=-1, keepdims=True)
        return (y - mu) * jax.lax.rsqrt(var + LN_EPS) * gamma + beta
    edge_index = jnp.stack([src, dst])
    h = jnp.maximum(_layernorm(x, axis=-1), 0.0)
    x = x + _L0_gnn_ref(h, L0_gnn_bases, L0_gnn_w_comp, L0_gnn_h_bias, edge_weight1, src, dst, edge_type_32)
    h = jnp.maximum(_layernorm(x, axis=-1), 0.0)
    x = x + _L1_gnn_ref(h, edge_index, edge_attr_64, L1_gnn_W1, L1_gnn_b1, L1_gnn_W2, L1_gnn_b2, L1_gnn_W3, L1_gnn_b3, L1_gnn_W4, L1_gnn_b4, L1_gnn_gamma, L1_gnn_beta)
    return x

_drawn_inputs = setup_inputs


def setup_inputs(seed=0):
    import zlib

    import numpy as np

    out = dict(_drawn_inputs(seed))
    spreads = {'L0_gnn_h_bias': (0.0, 0.1),
     'L1_gnn_b1': (0.0, 0.1),
     'L1_gnn_b2': (0.0, 0.1),
     'L1_gnn_b3': (0.0, 0.567),
     'L1_gnn_b4': (0.0, 0.404),
     'L1_gnn_gamma': (1.0, 0.2),
     'L1_gnn_beta': (0.0, 0.1)}
    factors = {}
    for name, (base, spread) in spreads.items():
        noise = np.random.default_rng([zlib.crc32(name.encode()), seed]).standard_normal(out[name].shape)
        drawn = base * np.exp(spread * noise) if base else spread * noise
        out[name] = jnp.asarray(drawn.astype(out[name].dtype))
    for name, factor in factors.items():
        out[name] = (out[name] * factor).astype(out[name].dtype)
    return out
```

```python
from contextlib import ExitStack

import concourse.bass as bass
from concourse import mybir

F32 = mybir.dt.float32
F32R = mybir.dt.float32r
I32 = mybir.dt.int32
ALU = mybir.AluOpType
ACT = mybir.ActivationFunctionType
AX_X = mybir.AxisListType.X

P = 128
N = 1250
E = 21250
D = 512
KC = D // P
ED = 64
R = 32
NB = 8
NP = 125
NT = N // NP
TG = 4
GROUPS = -(-E // (P * TG * 2)) * 2
T = GROUPS * TG
EPAD = T * P
FULL = E // P
REST = E - FULL * P
WN = 16
WINDOWS = -(-N // WN)
NPAD = N + WN
ROWS = 8
BANKS = 4
TCH = 21
CHUNKS = T // TCH
U_MAX = 1e18
EPS = 1e-5


def wait(eng, sem, value):
    if not (isinstance(value, int) and value <= 0):
        eng.wait_ge(sem, value)


def carrier(eng, turns):
    return lambda: eng.sem_inc(turns, 1)


def gnn_kernel(nc, x, src_t, dst_t, etype, norm_t, edge_attr, bases, w_comp, h_bias, w1, b1, w2, b2,
               w3, b3, w4, b4, gamma, beta, out):
    h0_rows = nc.dram_tensor("h0_rows", [N, D], F32, kind="Internal").ap()
    xa_rows = nc.dram_tensor("xa_rows", [N, D], F32, kind="Internal").ap()
    xb_rows = nc.dram_tensor("xb_rows", [N, D], F32, kind="Internal").ap()
    by_tile = "(t p) f -> p t f"
    x_v = x.rearrange(by_tile, p=NP)
    out_v = out.rearrange(by_tile, p=NP)
    h0_v = h0_rows.rearrange(by_tile, p=NP)
    xa_v = xa_rows.rearrange(by_tile, p=NP)
    xb_v = xb_rows.rearrange(by_tile, p=NP)

    def row_over_partitions(v, parts):
        return v.rearrange("(a f) -> a f", a=1).partition_broadcast(parts) if 0 else v.partition_broadcast(parts)

    with ExitStack() as whole:
        def sbuf(stack, name, shape, dt=F32):
            return stack.enter_context(nc.sbuf_tensor(name, shape, dt))

        def psum(stack, name, shape):
            return stack.enter_context(nc.psum_tensor(name, shape, F32))

        def sem(stack, name):
            return stack.enter_context(nc.semaphore(name))

        src_idx = sbuf(whole, "src_idx", [P, T], I32)
        dst_idx = sbuf(whole, "dst_idx", [P, T], I32)
        dst_row = sbuf(whole, "dst_row", [P, T], I32)
        dst_rel = sbuf(whole, "dst_rel", [P, T + TG])
        wide = sbuf(whole, "wide", [1, 1], I32)
        iota = sbuf(whole, "iota", [P, WN])
        ident = sbuf(whole, "ident", [P, P])
        x1 = sbuf(whole, "x1", [NP, NT, D])

        layer0 = whole.enter_context(ExitStack())
        coef = sbuf(layer0, "coef", [P, T + TG, NB])
        with ExitStack() as st:
            norm_sb = sbuf(st, "norm_sb", [P, T])
            wc = sbuf(st, "wc", [R, NB])
            etype_b = sbuf(st, "etype_b", [R, 2, TCH * P], I32)
            type_hot = sbuf(st, "type_hot", [R, 2, TCH * P])
            rel_id_i = sbuf(st, "rel_id_i", [R, 1], I32)
            rel_id = sbuf(st, "rel_id", [R, 1])
            ones = sbuf(st, "ones", [1, P])
            base_f = sbuf(st, "base_f", [1, T])
            off = sbuf(st, "off", [P, T])
            far = sbuf(st, "far", [P, 2])
            far1 = sbuf(st, "far1", [P, 1])
            wide_f = sbuf(st, "wide_f", [1, 2])
            stats = sbuf(st, "stats", [NP, NT, 6])
            mv = sbuf(st, "mv", [NP, NT, 2])
            std = sbuf(st, "std", [NP, NT])
            rstd = sbuf(st, "rstd", [NP, NT])
            eps = sbuf(st, "eps", [NP, 1])
            h0 = sbuf(st, "h0", [NP, NT, D])
            base_ps = psum(st, "base_ps", [P, 512])
            far_ps = psum(st, "far_ps", [P, 512])
            coef_ps = psum(st, "coef_ps", [P, 2, 512])

            idx_in = sem(st, "idx_in")
            x_in = sem(st, "x_in")
            type_in = [sem(st, f"type_in{i}") for i in range(2)]
            made = sem(st, "made")
            pads = sem(st, "pads")
            consts = sem(st, "consts")
            base_done = sem(st, "base_done")
            base_at = sem(st, "base_at")
            check = sem(st, "check")
            far_t = sem(st, "far_t")
            flag_at = sem(st, "flag_at")
            hot = sem(st, "hot")
            coef_mm = sem(st, "coef_mm")
            coef_at = sem(st, "coef_at")
            stat = sem(st, "stat")
            std_at = sem(st, "std_at")
            norm_at = sem(st, "norm_at")
            h_at = sem(st, "h_at")
            h_out = sem(st, "h_out")
            with nc.Block() as block:
                @block.sync
                def _(eng):
                    eng.dma_start(dst_idx[:, :], dst_t).then_inc(idx_in, 16)
                    eng.dma_start(x1[:, :, :], x_v).then_inc(x_in, 16)
                    eng.dma_start(src_idx[:, :], src_t).then_inc(idx_in, 16)
                    eng.dma_start(norm_sb[:, :], norm_t).then_inc(idx_in, 16)
                    eng.dma_start(wc[:, :], w_comp).then_inc(idx_in, 16)
                    for c in range(CHUNKS):
                        wait(eng, hot, c - 1)
                        eng.dma_start(etype_b[:, c % 2, :],
                                      etype[c * TCH * P:(c + 1) * TCH * P].partition_broadcast(R))\
                            .then_inc(type_in[c % 2], 16)
                    eng.wait_ge(h_at, NT)
                    eng.dma_start(h0_v, h0[:, :, :]).then_inc(h_out, 16)
                    eng.wait_ge(h_out, 16)

                @block.gpsimd
                def _(eng):
                    eng.memset(ident[:, :], 0.0).then_inc(made, 1)
                    eng.wait_ge(made, 1)
                    eng.affine_select(out=ident[:, :], in_=ident[:, :], compare_op=ALU.not_equal,
                                      fill=1.0, base=0, pattern=[[-1, P]], channel_multiplier=1)\
                        .then_inc(made, 1)
                    eng.iota(iota[:, :], [[1, WN]], base=0, channel_multiplier=0,
                             allow_small_or_imprecise_dtypes=True).then_inc(made, 1)
                    eng.iota(rel_id_i[:, :], [[0, 1]], base=0, channel_multiplier=1).then_inc(made, 1)

                @block.vector
                def _(eng):
                    eng.memset(ones[:, :], 1.0).then_inc(consts, 1)
                    eng.memset(dst_rel[:, T:T + TG], -1.0).then_inc(consts, 1)
                    eng.memset(coef[:, T:T + TG, :], 0.0).then_inc(consts, 1)
                    eng.memset(far[:, :], 0.0).then_inc(consts, 1)
                    eng.memset(eps[:, :], EPS).then_inc(consts, 1)
                    eng.wait_ge(idx_in, 64)
                    eng.tensor_scalar(dst_row[:, :], dst_idx[:, :], 0.0, None, ALU.max)\
                        .then_inc(base_done, 1)
                    eng.wait_ge(base_done, 1)
                    eng.tensor_copy(base_f[:, :], dst_row[0:1, :]).then_inc(base_done, 1)
                    eng.wait_ge(made, 4)
                    eng.tensor_copy(rel_id[:, :], rel_id_i[:, :]).then_inc(base_done, 1)
                    eng.wait_ge(x_in, 16)
                    for t in range(NT):
                        eng.bn_stats(stats[:, t, :], x1[:, t, :]).then_inc(stat, 1)
                    for t in range(NT):
                        eng.wait_ge(stat, t + 1)
                        eng.bn_aggr(mv[:, t, :], stats[:, t, :]).then_inc(stat, 1)
                    eng.wait_ge(base_at, 1)
                    eng.tensor_tensor(dst_rel[:, 0:T], dst_idx[:, :], base_ps[:, 0:T], ALU.subtract)\
                        .then_inc(check, 1)
                    eng.wait_ge(check, 1)
                    eng.tensor_scalar(off[:, :], dst_rel[:, 0:T], -(WN - 1) / 2, None, ALU.add)\
                        .then_inc(check, 1)
                    eng.wait_ge(check, 2)
                    eng.tensor_tensor(off[:, :], off[:, :], off[:, :], ALU.mult).then_inc(check, 1)
                    eng.wait_ge(check, 3)
                    eng.wait_ge(consts, 5)
                    eng.reduce_max(far[:, 0:1], off[:, 0:FULL], axis=AX_X).then_inc(check, 1)
                    if REST:
                        eng.reduce_max(far[0:REST, 1:2], off[0:REST, FULL:FULL + 1], axis=AX_X)\
                            .then_inc(check, 1)
                    eng.wait_ge(check, 4 + (REST > 0))
                    eng.reduce_max(far1[:, :], far[:, :], axis=AX_X).then_inc(check, 1)
                    eng.wait_ge(far_t, 1)
                    eng.reduce_max(wide_f[:, 0:1], far_ps[0:1, 0:P], axis=AX_X).then_inc(flag_at, 1)
                    eng.wait_ge(flag_at, 1)
                    eng.tensor_scalar(wide[:, :], wide_f[:, 0:1], (WN / 2) ** 2, None, ALU.is_ge)\
                        .then_inc(flag_at, 1)
                    eng.wait_ge(std_at, 1)
                    eng.reciprocal(rstd[:, :], std[:, :]).then_inc(norm_at, 1)
                    eng.wait_ge(norm_at, 1)
                    for t in range(NT):
                        eng.tensor_scalar(h0[:, t, :], x1[:, t, :], mv[:, t, 0:1], rstd[:, t:t + 1],
                                          ALU.subtract, ALU.mult).then_inc(norm_at, 1)
                    for t in range(NT):
                        eng.wait_ge(norm_at, 2 + t)
                        eng.tensor_scalar(h0[:, t, :], h0[:, t, :], 0.0, None, ALU.max)\
                            .then_inc(h_at, 1)
                    for c in range(CHUNKS + 1):
                        if c < CHUNKS:
                            eng.wait_ge(type_in[c % 2], 16 * (c // 2 + 1))
                            wait(eng, coef_mm, c - 1)
                            eng.tensor_scalar(type_hot[:, c % 2, :], etype_b[:, c % 2, :],
                                              rel_id[:, :], None, ALU.is_equal).then_inc(hot, 1)
                        if c > 0:
                            eng.wait_ge(coef_mm, c)
                            t0 = (c - 1) * TCH
                            eng.tensor_tensor(
                                coef[:, t0:t0 + TCH, :],
                                coef_ps[:, (c - 1) % 2, 0:TCH * NB].rearrange("p (t b) -> p t b", b=NB),
                                norm_sb[:, t0:t0 + TCH].unsqueeze(2).to_broadcast([P, TCH, NB]),
                                ALU.mult).then_inc(coef_at, 1)

                @block.tensor
                def _(eng):
                    eng.wait_ge(base_done, 2)
                    eng.wait_ge(consts, 1)
                    eng.matmul(base_ps[:, 0:T], ones[:, :], base_f[:, :], start=True, stop=True)\
                        .then_inc(base_at, 1)
                    eng.wait_ge(check, 5 + (REST > 0))
                    eng.wait_ge(made, 2)
                    eng.transpose(far_ps[0:1, 0:P], far1[:, :], ident[:, :]).then_inc(far_t, 1)
                    for c in range(CHUNKS):
                        eng.wait_ge(hot, c + 1)
                        wait(eng, coef_at, c - 1)
                        for t in range(TCH):
                            mm = eng.matmul(coef_ps[:, c % 2, t * NB:(t + 1) * NB],
                                            type_hot[:, c % 2, t * P:(t + 1) * P], wc[:, :],
                                            start=True, stop=True)
                        mm.then_inc(coef_mm, 1)

                @block.scalar
                def _(eng):
                    eng.wait_ge(stat, 2 * NT)
                    eng.wait_ge(consts, 5)
                    eng.activation(std[:, :], mv[:, :, 1:2].squeeze(2), ACT.Sqrt, bias=eps[:, :])\
                        .then_inc(std_at, 1)

        with ExitStack() as st:
            G = sbuf(st, "G", [P, KC, NB, NPAD])
            with ExitStack() as st2:
                scatter_layer0(nc, st2, sbuf, psum, sem, G, h0_rows, src_idx, dst_idx, dst_row,
                               dst_rel, coef, iota, wide)
            with ExitStack() as st2:
                apply_bases(nc, st2, sbuf, psum, sem, G, bases, h_bias, x1)
        layer0.close()

        with ExitStack() as st:
            h1 = sbuf(st, "h1", [NP, NT, D])
            h1t = sbuf(st, "h1t", [P, KC, N])
            with ExitStack() as st2:
                node_products(nc, st2, sbuf, psum, sem, x1, h1, h1t, ident, w1, b1, xa_v, xb_v)
            aggt = sbuf(st, "aggt", [P, KC, NPAD])
            with ExitStack() as st2:
                edge_mlp(nc, st2, sbuf, psum, sem, aggt, xa_rows, xb_rows, edge_attr, w1, w2, b2,
                         src_idx, dst_idx, dst_row, dst_rel, iota, ident, wide)
            with ExitStack() as st2:
                node_mlp(nc, st2, sbuf, psum, sem, x1, h1, h1t, aggt, ident, w3, b3, w4, b4, gamma,
                         beta, out_v)


def gather_ahead(eng, idx_sem, slot, table, first):
    eng.tensor_copy(slot, table[:, bass.ds(first, TG)]).then_inc(idx_sem, 1)


def scatter_layer0(nc, st, sbuf, psum, sem, G, h0_rows, src_idx, dst_idx, dst_row, dst_rel, coef,
                   iota, wide):
    rows = sbuf(st, "rows", [P, ROWS, D])
    idx = sbuf(st, "l0_idx", [P, ROWS], I32)
    S = sbuf(st, "S", [P, ROWS, NB, WN])
    ps = psum(st, "l0_ps", [P, BANKS, KC * NB * WN])
    rows_in = [sem(st, f"rows_in{i}") for i in range(ROWS)]
    idx_at = sem(st, "l0_idx_at")
    s_at = sem(st, "s_at")
    mm_done = sem(st, "mm_done")
    added = sem(st, "added")
    w_s = sem(st, "w_s")
    w_mm = sem(st, "w_mm")
    w_add = sem(st, "w_add")
    w_node = sem(st, "w_node")
    pool_turns = sem(st, "l0_pool_turns")
    pe_turns = sem(st, "l0_pe_turns")
    node = sbuf(st, "l0_node", [P, 1])

    def gather(eng, i, q, rows_free, per_tile, carry):
        if q % TG == 0:
            half = slice(q, q + TG)
            for k in range(q, q + TG):
                wait(eng, rows_in[k], 16 * i)
            eng.tensor_copy(idx[:, half], src_idx[:, bass.ds(ROWS * i + q, TG)]).then_inc(idx_at, 1)
            eng.wait_ge(idx_at, 2 * i + q // TG + 1)
        eng.wait_ge(rows_free, (ROWS * i + q + 1) * per_tile)
        carry()
        eng.indirect_dma_start(rows[:, q, :], None, h0_rows,
                               bass.IndirectOffsetOnAxis(ap=idx[:, q:q + 1], axis=0))\
            .then_inc(rows_in[q], 16)

    def gathers(eng, rows_free, per_tile):
        carry = carrier(eng, pool_turns)
        for q in range(ROWS):
            gather(eng, 0, q, rows_free, per_tile, carry)
        with eng.Fori(1, T // ROWS, 1) as i:
            for q in range(ROWS):
                gather(eng, i, q, rows_free, per_tile, carry)

    def products(eng, q, bank):
        for c in range(KC):
            mm = eng.matmul(ps[:, bank, c * NB * WN:(c + 1) * NB * WN],
                            rows[:, q, c * P:(c + 1) * P],
                            S[:, q, :, :].rearrange("p b n -> p (b n)"), start=True, stop=True)
        return mm

    def build_s(eng, t, q, node):
        return eng.scalar_tensor_tensor(
            S[:, q, :, :], iota[:, :].unsqueeze(1).to_broadcast([P, NB, WN]), node,
            coef[:, bass.ds(t, 1), :].squeeze(1).unsqueeze(2).to_broadcast([P, NB, WN]),
            ALU.is_equal, ALU.mult)

    def add_to_g(eng, base, bank):
        window = G[:, :, :, bass.ds(base, WN)].rearrange("p c b n -> p (c b) n")
        return eng.tensor_tensor(window, window,
                                 ps[:, bank, :].rearrange("p (m n) -> p m n", n=WN), ALU.add)

    with nc.Block() as block:
        @block.gpsimd
        def _(eng):
            general = eng.value_load(wide[0:1, 0:1], min_val=0, max_val=1)
            with eng.If(general == 0):
                gathers(eng, mm_done, 1)
            with eng.Else():
                gathers(eng, w_mm, WINDOWS)

        @block.tensor
        def _(eng):
            general = eng.value_load(wide[0:1, 0:1], min_val=0, max_val=1)
            with eng.If(general == 0):
                eng.sem_inc(mm_done, ROWS)
                with eng.Fori(0, T // ROWS, 1) as i:
                    for q in range(ROWS):
                        t = ROWS * i + q
                        eng.wait_ge(rows_in[q], 16 * i + 16)
                        eng.wait_ge(s_at, t + 1)
                        eng.wait_ge(added, t + 1)
                        products(eng, q, q % BANKS).then_inc(mm_done, 1)
            with eng.Else():
                eng.sem_inc(w_mm, ROWS * WINDOWS)
                carry = carrier(eng, pe_turns)
                with eng.Fori(0, T // ROWS, 1) as i:
                    for q in range(ROWS):
                        eng.wait_ge(rows_in[q], 16 * i + 16)
                        carry()
                        with eng.Fori(0, WINDOWS, 1) as w:
                            n = (ROWS * i + q) * WINDOWS + w
                            eng.wait_ge(w_s, n + 1)
                            eng.wait_ge(w_add, n + 1)
                            products(eng, q, 0).then_inc(w_mm, 1)

        @block.vector
        def _(eng):
            general = eng.value_load(wide[0:1, 0:1], min_val=0, max_val=1)
            with eng.If(general == 0):
                starts = [eng.alloc_register(f"l0_start{k}") for k in range(TG)]
                eng.memset(G[:, :, :, :].rearrange("p c b n -> p (c b n)"), 0.0).then_inc(added, BANKS)
                for k in range(TG):
                    build_s(eng, k, k, dst_rel[:, k:k + 1]).then_inc(s_at, 1)
                with eng.Fori(0, T // ROWS, 1) as i:
                    for half in range(2):
                        t0 = ROWS * i + half * TG
                        eng.reg_load(starts, dst_row[0:1, bass.ds(t0, TG)])
                        eng.wait_ge(mm_done, ROWS + t0)
                        for k in range(TG):
                            t = t0 + TG + k
                            build_s(eng, t, (1 - half) * TG + k, dst_rel[:, bass.ds(t, 1)])\
                                .then_inc(s_at, 1)
                        for k in range(TG):
                            eng.wait_ge(mm_done, ROWS + t0 + k + 1)
                            eng.wait_ge(added, BANKS + t0 + k)
                            start = eng.snap(starts[k], min_val=0, max_val=N - 1)
                            add_to_g(eng, start, k).then_inc(added, 1)
            with eng.Else():
                eng.memset(G[:, :, :, :].rearrange("p c b n -> p (c b n)"), 0.0).then_inc(w_add, 1)
                with eng.Fori(0, T // ROWS, 1) as i:
                    for q in range(ROWS):
                        t = ROWS * i + q
                        eng.wait_ge(w_add, t * WINDOWS + 1)
                        eng.tensor_copy(node[:, :], dst_idx[:, bass.ds(t, 1)]).then_inc(w_node, 1)
                        with eng.Fori(0, WINDOWS, 1) as w:
                            n = t * WINDOWS + w
                            eng.wait_ge(w_node, n + t + 1)
                            build_s(eng, t, q, node[:, :]).then_inc(w_s, 1)
                            eng.wait_ge(w_s, n + 1)
                            eng.tensor_scalar(node[:, :], node[:, :], -float(WN), None, ALU.add)\
                                .then_inc(w_node, 1)
                            eng.wait_ge(w_mm, ROWS * WINDOWS + n + 1)
                            add_to_g(eng, w * WN, 0).then_inc(w_add, 1)


def apply_bases(nc, st, sbuf, psum, sem, G, bases, h_bias, x1):
    RING = 4
    ROUND = NT // 2
    wb = sbuf(st, "wb", [P, RING, D])
    bias = sbuf(st, "bias0", [NP, D])
    ps = psum(st, "b_ps", [P, 8, D])
    wb_in = [sem(st, f"wb_in{i}") for i in range(RING)]
    bias_in = sem(st, "bias0_in")
    used = sem(st, "wb_used")
    summed = sem(st, "summed")
    got = sem(st, "got")
    x1_at = sem(st, "x1_at")
    pieces = NB * KC
    with nc.Block() as block:
        @block.sync
        def _(eng):
            for m in range(2 * pieces):
                b, c = divmod(m % pieces, KC)
                wait(eng, used, m - RING + 1)
                eng.dma_start(wb[:, m % RING, :], bases[b, c * P:(c + 1) * P, :])\
                    .then_inc(wb_in[m % RING], 16)

        @block.scalar
        def _(eng):
            eng.dma_start(bias[:, :], h_bias.partition_broadcast(NP)).then_inc(bias_in, 16)

        @block.tensor
        def _(eng):
            for m in range(2 * pieces):
                r = m // pieces
                b, c = divmod(m % pieces, KC)
                eng.wait_ge(wb_in[m % RING], 16 * (m // RING + 1))
                for k in range(ROUND):
                    t = r * ROUND + k
                    if m % pieces == 0 and t >= 8:
                        eng.wait_ge(got, t - 8 + 1)
                    mm = eng.matmul(ps[0:NP, t % 8, :], G[:, c, b, t * NP:(t + 1) * NP],
                                    wb[:, m % RING, :], start=(m % pieces == 0),
                                    stop=(m % pieces == pieces - 1))
                mm.then_inc(used, 1)

        @block.vector
        def _(eng):
            eng.wait_ge(bias_in, 16)
            for t in range(NT):
                eng.wait_ge(used, pieces * (t // ROUND + 1))
                eng.tensor_tensor(x1[:, t, :], x1[:, t, :], ps[0:NP, t % 8, :], ALU.add)\
                    .then_inc(got, 1)
                eng.wait_ge(got, t + 1)
                eng.tensor_tensor(x1[:, t, :], x1[:, t, :], bias[:, :], ALU.add).then_inc(x1_at, 1)


def node_products(nc, st, sbuf, psum, sem, x1, h1, h1t, ident, w1, b1, xa_v, xb_v):
    w1ab = sbuf(st, "w1ab", [P, 2, KC, D])
    b1b = sbuf(st, "b1b", [NP, D])
    stats = sbuf(st, "stats1", [NP, NT, 6])
    mv = sbuf(st, "mv1", [NP, NT, 2])
    std = sbuf(st, "std1", [NP, NT])
    rstd = sbuf(st, "rstd1", [NP, NT])
    eps = sbuf(st, "eps1", [NP, 1])
    rows_ab = sbuf(st, "rows_ab", [NP, 2, 2, D])
    tp = psum(st, "tp1", [P, 2, D])
    ps = psum(st, "ab_ps", [P, 4, D])
    w_in = sem(st, "w1_in")
    eps_at = sem(st, "eps1_at")
    stat = sem(st, "stat1")
    std_at = sem(st, "std1_at")
    norm_at = sem(st, "norm1_at")
    h_at = sem(st, "h1_at")
    tp_done = sem(st, "tp1_done")
    ht_at = sem(st, "h1t_at")
    ab_mm = sem(st, "ab_mm")
    ab_at = sem(st, "ab_at")
    ab_out = [sem(st, f"ab_out{i}") for i in range(2)]
    with nc.Block() as block:
        @block.sync
        def _(eng):
            for a in range(2):
                eng.dma_start(w1ab[:, a, :, :],
                              w1[a * D:(a + 1) * D, :].rearrange("(c p) n -> p c n", p=P))\
                    .then_inc(w_in, 16)
            eng.dma_start(b1b[:, :], b1.partition_broadcast(NP)).then_inc(w_in, 16)
            for t in range(NT):
                eng.wait_ge(ab_at, 2 * t + 2)
                eng.dma_start(xa_v[:, t, :], rows_ab[:, t % 2, 0, :]).then_inc(ab_out[t % 2], 16)
                eng.dma_start(xb_v[:, t, :], rows_ab[:, t % 2, 1, :]).then_inc(ab_out[t % 2], 16)
            for s in range(2):
                eng.wait_ge(ab_out[s], 32 * (NT // 2))

        @block.vector
        def _(eng):
            eng.memset(eps[:, :], EPS).then_inc(eps_at, 1)
            for t in range(NT):
                eng.bn_stats(stats[:, t, :], x1[:, t, :]).then_inc(stat, 1)
            for t in range(NT):
                eng.wait_ge(stat, t + 1)
                eng.bn_aggr(mv[:, t, :], stats[:, t, :]).then_inc(stat, 1)
            eng.wait_ge(std_at, 1)
            eng.reciprocal(rstd[:, :], std[:, :]).then_inc(norm_at, 1)
            eng.wait_ge(norm_at, 1)
            for t in range(NT):
                eng.tensor_scalar(h1[:, t, :], x1[:, t, :], mv[:, t, 0:1], rstd[:, t:t + 1],
                                  ALU.subtract, ALU.mult).then_inc(norm_at, 1)
                eng.wait_ge(norm_at, 2 + t)
                eng.tensor_scalar(h1[:, t, :], h1[:, t, :], 0.0, None, ALU.max).then_inc(h_at, 1)
            eng.wait_ge(w_in, 48)
            for t in range(NT):
                eng.wait_ge(ab_mm, 2 * t + 2)
                if t >= 2:
                    eng.wait_ge(ab_out[t % 2], 32 * (t // 2))
                eng.tensor_copy(rows_ab[:, t % 2, 0, :], ps[0:NP, 2 * (t % 2), :]).then_inc(ab_at, 1)
                eng.tensor_tensor(rows_ab[:, t % 2, 1, :], ps[0:NP, 2 * (t % 2) + 1, :], b1b[:, :],
                                  ALU.add).then_inc(ab_at, 1)

        @block.scalar
        def _(eng):
            eng.wait_ge(stat, 2 * NT)
            eng.wait_ge(eps_at, 1)
            eng.activation(std[:, :], mv[:, :, 1:2].squeeze(2), ACT.Sqrt, bias=eps[:, :])\
                .then_inc(std_at, 1)
            for t in range(NT):
                eng.wait_ge(tp_done, t + 1)
                eng.activation(h1t[:, :, t * NP:(t + 1) * NP],
                               tp[:, t % 2, 0:KC * P].rearrange("p (c n) -> p c n", c=KC)[:, :, 0:NP],
                               ACT.Copy).then_inc(ht_at, 1)

        @block.tensor
        def _(eng):
            def transposes(t):
                eng.wait_ge(h_at, t + 1)
                wait(eng, ht_at, t - 1)
                for c in range(KC):
                    mm = eng.transpose(tp[:, t % 2, c * P:c * P + NP], h1[:, t, c * P:(c + 1) * P],
                                       ident[0:NP, 0:NP])
                mm.then_inc(tp_done, 1)

            transposes(0)
            eng.wait_ge(w_in, 48)
            for t in range(NT):
                if t + 1 < NT:
                    transposes(t + 1)
                eng.wait_ge(ht_at, t + 1)
                for a in range(2):
                    if a == 0:
                        wait(eng, ab_at, 2 * (t - 1))
                    for c in range(KC):
                        mm = eng.matmul(ps[0:NP, 2 * (t % 2) + a, :], h1t[:, c, t * NP:(t + 1) * NP],
                                        w1ab[:, a, c, :], start=(c == 0), stop=(c == KC - 1))
                    mm.then_inc(ab_mm, 1)


def edge_mlp(nc, st, sbuf, psum, sem, aggt, xa_rows, xb_rows, edge_attr, w1, w2, b2, src_idx,
             dst_idx, dst_row, dst_rel, iota, ident, wide):
    GF = TG * D
    X = sbuf(st, "X", [P, 2, GF])
    XB = sbuf(st, "XB", [P, 2, GF])
    U1 = sbuf(st, "U1", [P, 2, GF])
    X2 = sbuf(st, "X2", [P, 2, GF])
    U2 = sbuf(st, "U2", [P, 2, GF])
    h_hi = sbuf(st, "h_hi", [P, 2, D], F32R)
    h_lo = sbuf(st, "h_lo", [P, 2, D], F32R)
    w2_hi = sbuf(st, "w2_hi", [P, KC, D], F32R)
    w2_lo = sbuf(st, "w2_lo", [P, KC, D], F32R)
    wc_hi = sbuf(st, "wc_hi", [P, D], F32R)
    wc_lo = sbuf(st, "wc_lo", [P, D], F32R)
    ea = sbuf(st, "ea", [P, 2, TG * P])
    ea_s = sbuf(st, "ea_s", [P, 2, TG * P], F32R)
    b2b = sbuf(st, "b2b", [P, D])
    one = sbuf(st, "one", [P, 2, TG, WN])
    idx_a = sbuf(st, "idx_a", [P, 2, TG], I32)
    idx_b = sbuf(st, "idx_b", [P, 2, TG], I32)
    pz1 = psum(st, "pz1", [P, 2, D])
    pt = psum(st, "pt", [P, 2, D])
    pz2 = psum(st, "pz2", [P, 2, D])
    pg = psum(st, "pg", [P, 2, D])

    w_in = sem(st, "w2_in")
    w_split = sem(st, "w_split")
    ea_in = [sem(st, f"ea_in{i}") for i in range(2)]
    a_in = [sem(st, f"a_in{i}") for i in range(2)]
    b_in = [sem(st, f"b_in{i}") for i in range(2)]
    ia_at = sem(st, "ia_at")
    ib_at = sem(st, "ib_at")
    ea_at = sem(st, "ea_at")
    xb_at = sem(st, "xb_at")
    z1_mm = sem(st, "z1_mm")
    z1_at = sem(st, "z1_at")
    exp1 = sem(st, "exp1")
    cut1 = sem(st, "cut1")
    ln1 = sem(st, "ln1")
    tanh1 = sem(st, "tanh1")
    hid = sem(st, "hid")
    exp2 = sem(st, "exp2")
    cut2 = sem(st, "cut2")
    ln2 = sem(st, "ln2")
    tanh2 = sem(st, "tanh2")
    msg = sem(st, "msg")
    t_mm = sem(st, "t_mm")
    hi_at = sem(st, "hi_at")
    lo_at = sem(st, "lo_at")
    z2_mm = sem(st, "z2_mm")
    z2_at = sem(st, "z2_at")
    one_at = sem(st, "one_at")
    sum_mm = sem(st, "sum_mm")
    sum_at = sem(st, "sum_at")
    g_one = sem(st, "g_one")
    g_mm = sem(st, "g_mm")
    g_at = sem(st, "g_at")
    g_node = sem(st, "g_node")
    pool_turns = sem(st, "l1_pool_turns")
    pe_turns = sem(st, "l1_pe_turns")
    node = sbuf(st, "l1_node", [P, 1])

    def grp(i, d):
        return 2 * i + d

    def tile(i, d, k):
        return 2 * TG * i + TG * d + k

    def count(i, d, per=16):
        return per * i + per * (d // 2 + 1)

    def steps(eng, step, first, last):
        lo, hi = 1, GROUPS - 4
        hi -= (hi - lo + 1) % 2
        for j in range(first, lo):
            step(0, j, j)
        with eng.Fori(0, (hi - lo + 1) // 2, 1) as i:
            for p in range(2):
                step(i, lo + p, None)
        for j in range(hi + 1, last + 1):
            step(0, j, j)

    def there(j, d):
        return j is None or 0 <= j + d < GROUPS

    def pe_program(eng, general):
        carry = carrier(eng, pe_turns)

        def edge_products(i, d, k):
            s = d % 2
            if k == 0:
                eng.wait_ge(ea_at, 2 * grp(i, d) + 2)
            wait(eng, z1_at, tile(i, d, k) - 1)
            lhs = ea_s[:, s, k * P:(k + 1) * P]
            eng.matmul(pz1[:, k % 2, :], lhs, wc_hi[:, :], start=True, stop=False)
            eng.matmul(pz1[:, k % 2, :], lhs, wc_lo[:, :], start=False, stop=True).then_inc(z1_mm, 1)

        def transposes(i, d, k):
            if k == 0:
                eng.wait_ge(hid, grp(i, d) + 1)
            wait(eng, lo_at, tile(i, d, k) - 1)
            for c in range(KC):
                mm = eng.transpose(pt[:, k % 2, c * P:(c + 1) * P],
                                   U1[:, d % 2, k * D + c * P:k * D + (c + 1) * P], ident[:, :])
            mm.then_inc(t_mm, 1)

        def hidden_products(i, d, k):
            eng.wait_ge(lo_at, tile(i, d, k) + 1)
            wait(eng, z2_at, tile(i, d, k) - 1)
            n = 0
            for c in range(KC):
                for part, w in ((h_hi, w2_hi), (h_hi, w2_lo), (h_lo, w2_hi)):
                    mm = eng.matmul(pz2[:, k % 2, :], part[:, k % 2, c * P:(c + 1) * P], w[:, c, :],
                                    start=(n == 0), stop=(n == 3 * KC - 1))
                    n += 1
            mm.then_inc(z2_mm, 1)

        def window_products(s, k):
            for c in range(KC):
                mm = eng.matmul(pg[:, k % 2, c * WN:(c + 1) * WN], U2[:, s, k * D + c * P:k * D + (c + 1) * P],
                                one[:, s, k, :], start=True, stop=True)
            return mm

        def sum_products(i, d, k):
            if k == 0:
                eng.wait_ge(msg, grp(i, d) + 1)
            t = tile(i, d, k)
            if not general:
                eng.wait_ge(one_at, t + 1)
                eng.wait_ge(sum_at, t + 1)
                window_products(d % 2, k).then_inc(sum_mm, 1)
            else:
                carry()
                with eng.Fori(0, WINDOWS, 1) as w:
                    eng.wait_ge(g_one, t * WINDOWS + w + 1)
                    window_products(d % 2, k).then_inc(g_mm, 1)

        def step(i, d, j):
            for k in range(TG):
                if there(j, 1):
                    transposes(i, d + 1, k)
                if k == 0 and there(j, 0):
                    hidden_products(i, d, TG - 1)
                if k > 0 and there(j, 1):
                    hidden_products(i, d + 1, k - 1)
                if k >= 2 and there(j, -1):
                    sum_products(i, d - 1, 2 * k - 4)
                    sum_products(i, d - 1, 2 * k - 3)
                if k >= 2 and there(j, 3):
                    edge_products(i, d + 3, 2 * k - 4)
                    edge_products(i, d + 3, 2 * k - 3)

        eng.wait_ge(w_split, 6)
        steps(eng, step, -3, GROUPS)

    def act_program(eng, general):
        def act(func, u, group, s, source=None, bias=0.0):
            return eng.activation(u[:, s, :], (u if source is None else source)[:, s, :], func, bias=bias)

        def hi_part(i, d, k):
            t = tile(i, d, k)
            eng.wait_ge(t_mm, t + 1)
            wait(eng, z2_mm, t - 1)
            eng.activation(h_hi[:, k % 2, :], pt[:, k % 2, :], ACT.Copy).then_inc(hi_at, 1)

        def step(i, d, j):
            if there(j, 1):
                eng.wait_ge(ln1, grp(i, d + 1) + 1)
                act(ACT.Tanh, U1, None, (d + 1) % 2).then_inc(tanh1, 1)
            if there(j, -1):
                eng.wait_ge(ln2, grp(i, d - 1) + 1)
                act(ACT.Tanh, U2, None, (d - 1) % 2).then_inc(tanh2, 1)
            if there(j, 1):
                hi_part(i, d + 1, 0)
            if there(j, 2):
                eng.wait_ge(z1_at, tile(i, d + 2, TG))
                wait(eng, t_mm, tile(i, d + 1, 0))
                act(ACT.Exp, U1, None, d % 2, X).then_inc(exp1, 1)
            if there(j, 1):
                hi_part(i, d + 1, 1)
            if there(j, 0):
                eng.wait_ge(z2_at, tile(i, d, TG))
                if not (j is not None and j - 2 < 0):
                    eng.wait_ge(sum_mm, tile(i, d - 1, 0))
                act(ACT.Exp, U2, None, d % 2, X2).then_inc(exp2, 1)
            if there(j, 2):
                eng.wait_ge(cut1, grp(i, d + 2) + 1)
                act(ACT.Ln, U1, None, d % 2, bias=1.0).then_inc(ln1, 1)
            if there(j, 1):
                hi_part(i, d + 1, 2)
            if there(j, 0):
                eng.wait_ge(cut2, grp(i, d) + 1)
                act(ACT.Ln, U2, None, d % 2, bias=1.0).then_inc(ln2, 1)
            if there(j, 1):
                hi_part(i, d + 1, 3)

        steps(eng, step, -2, GROUPS)

    def dve_program(eng, general):
        starts = [eng.alloc_register(f"l1_start{general}{k}") for k in range(TG)]

        def split_attributes(i, d):
            s = d % 2
            eng.wait_ge(ea_in[s], count(i, d, 32))
            wait(eng, z1_mm, tile(i, d - 1, 0))
            eng.tensor_copy(ea_s[:, s, :], ea[:, s, :]).then_inc(ea_at, 1)
            eng.wait_ge(ea_at, 2 * grp(i, d) + 1)
            eng.tensor_tensor(ea_s[ED:P, s, :], ea[ED:P, s, :], ea_s[ED:P, s, :].bitcast(F32),
                              ALU.subtract).then_inc(ea_at, 1)

        def preactivation(i, d, k):
            if k == 0:
                eng.wait_ge(xb_at, grp(i, d) + 1)
            eng.wait_ge(z1_mm, tile(i, d, k) + 1)
            own = X[:, d % 2, k * D:(k + 1) * D]
            eng.tensor_tensor(own, own, pz1[:, k % 2, :], ALU.add).then_inc(z1_at, 1)

        def cut(u, i, d, exp, done):
            eng.wait_ge(exp, grp(i, d) + 1)
            eng.tensor_scalar(u[:, d % 2, :], u[:, d % 2, :], U_MAX, None, ALU.min).then_inc(done, 1)

        def times(u, z, i, d, tanh, done):
            eng.wait_ge(tanh, grp(i, d) + 1)
            eng.tensor_tensor(u[:, d % 2, :], u[:, d % 2, :], z[:, d % 2, :], ALU.mult)\
                .then_inc(done, 1)

        def lo_part(i, d, k):
            eng.wait_ge(hi_at, tile(i, d, k) + 1)
            eng.tensor_tensor(h_lo[:, k % 2, :], pt[:, k % 2, :], h_hi[:, k % 2, :].bitcast(F32),
                              ALU.subtract).then_inc(lo_at, 1)

        def second_preactivation(i, d, k):
            t = tile(i, d, k)
            if k == 0:
                wait(eng, msg, grp(i, d - 1))
            eng.wait_ge(z2_mm, t + 1)
            eng.tensor_tensor(X2[:, d % 2, k * D:(k + 1) * D], pz2[:, k % 2, :], b2b[:, :], ALU.add)\
                .then_inc(z2_at, 1)

        def one_hots(i, d):
            wait(eng, sum_mm, tile(i, d - 1, 0))
            for k in range(TG):
                t = tile(i, d, k)
                eng.tensor_scalar(one[:, d % 2, k, :], iota[:, :], dst_rel[:, bass.ds(t, 1)],
                                  None, ALU.is_equal).then_inc(one_at, 1)

        def add_window(k, base):
            window = aggt[:, :, bass.ds(base, WN)]
            return eng.tensor_tensor(window, window,
                                     pg[:, k % 2, 0:KC * WN].rearrange("p (c n) -> p c n", c=KC),
                                     ALU.add)

        def sum_up(i, d, k):
            t = tile(i, d, k)
            s = d % 2
            if not general:
                eng.wait_ge(sum_mm, t + 1)
                eng.wait_ge(sum_at, 2 + t)
                start = eng.snap(starts[k], min_val=0, max_val=N - 1)
                add_window(k, start).then_inc(sum_at, 1)
            else:
                eng.wait_ge(g_at, t * WINDOWS + 1)
                eng.tensor_copy(node[:, :], dst_idx[:, bass.ds(t, 1)]).then_inc(g_node, 1)
                with eng.Fori(0, WINDOWS, 1) as w:
                    n = t * WINDOWS + w
                    eng.wait_ge(g_node, n + t + 1)
                    eng.tensor_scalar(one[:, s, k, :], iota[:, :], node[:, :], None,
                                      ALU.is_equal).then_inc(g_one, 1)
                    eng.wait_ge(g_one, n + 1)
                    eng.tensor_scalar(node[:, :], node[:, :], -float(WN), None, ALU.add)\
                        .then_inc(g_node, 1)
                    eng.wait_ge(g_mm, n + 1)
                    add_window(k, w * WN).then_inc(g_at, 1)
                eng.sem_inc(sum_mm, 1)

        def step(i, d, j):
            if there(j, -1) and not general:
                eng.reg_load(starts, dst_row[0:1, bass.ds(tile(i, d - 1, 0), TG)])
            if there(j, 1):
                times(U1, X, i, d + 1, tanh1, hid)
            if there(j, 2):
                for k in range(TG):
                    preactivation(i, d + 2, k)
            if there(j, 3):
                split_attributes(i, d + 3)
            if there(j, 0):
                second_preactivation(i, d, TG - 1)
            if there(j, 1):
                lo_part(i, d + 1, 0)
            if there(j, -1):
                times(U2, X2, i, d - 1, tanh2, msg)
            if there(j, 1):
                lo_part(i, d + 1, 1)
                second_preactivation(i, d + 1, 0)
            if there(j, 2):
                cut(U1, i, d + 2, exp1, cut1)
            if there(j, 1):
                lo_part(i, d + 1, 2)
                second_preactivation(i, d + 1, 1)
            if there(j, 0):
                cut(U2, i, d, exp2, cut2)
            if there(j, -1):
                sum_up(i, d - 1, 0)
                sum_up(i, d - 1, 1)
            if there(j, 1):
                lo_part(i, d + 1, 3)
                second_preactivation(i, d + 1, 2)
            if there(j, -1):
                sum_up(i, d - 1, 2)
                sum_up(i, d - 1, 3)
            if there(j, 0) and not general:
                one_hots(i, d)

        eng.memset(aggt[:, :, :].rearrange("p c n -> p (c n)"), 0.0)\
            .then_inc(g_at if general else sum_at, 1 if general else 2)
        eng.wait_ge(w_in, 64)
        raw2 = U2[:, 0, :].rearrange("p (c n) -> p c n", c=KC)
        rawc = U2[:, 1, 0:D]
        eng.tensor_copy(w2_hi[:, :, :], raw2).then_inc(w_split, 1)
        eng.tensor_copy(wc_hi[:, :], rawc).then_inc(w_split, 1)
        eng.wait_ge(w_split, 2)
        eng.tensor_tensor(w2_lo[:, :, :], raw2, w2_hi[:, :, :].bitcast(F32), ALU.subtract)\
            .then_inc(w_split, 2)
        eng.tensor_tensor(wc_lo[:, :], rawc, wc_hi[:, :].bitcast(F32), ALU.subtract)\
            .then_inc(w_split, 2)
        steps(eng, step, -3, GROUPS)

    def pool_program(eng):
        carry = carrier(eng, pool_turns)

        def rows_of(i, d, slot, idx, table, rows, done, idx_sem):
            s = d % 2
            if not isinstance(i, int) or d >= 2:
                eng.wait_ge(done[s], count(i, d - 2, 64))
            eng.tensor_copy(idx[:, s, :], table[:, bass.ds(tile(i, d, 0), TG)]).then_inc(idx_sem, 1)
            eng.wait_ge(idx_sem, grp(i, d) + 1)
            carry()
            for k in range(TG):
                eng.indirect_dma_start(slot[:, s, k * D:(k + 1) * D], None, rows,
                                       bass.IndirectOffsetOnAxis(ap=idx[:, s, k:k + 1], axis=0))\
                    .then_inc(done[s], 16)

        def rows_a(i, d):
            wait(eng, hid, grp(i, d) - 1)
            rows_of(i, d, X, idx_a, src_idx, xa_rows, a_in, ia_at)

        def rows_b(i, d):
            wait(eng, xb_at, grp(i, d) - 1)
            rows_of(i, d, XB, idx_b, dst_row, xb_rows, b_in, ib_at)

        def add_b(i, d):
            s = d % 2
            eng.wait_ge(a_in[s], count(i, d, 64))
            eng.wait_ge(b_in[s], count(i, d, 64))
            eng.tensor_tensor(X[:, s, :], X[:, s, :], XB[:, s, :], ALU.add).then_inc(xb_at, 1)

        rows_b(0, 0)
        for d in range(3):
            rows_a(0, d)
            rows_b(0, d + 1)
            add_b(0, d)
        with eng.Fori(0, (GROUPS - 4) // 2, 1) as i:
            for d in (3, 4):
                rows_a(i, d)
                rows_b(i, d + 1)
                add_b(i, d)
        rows_a(0, GROUPS - 1)
        add_b(0, GROUPS - 1)

    def branch(eng, program):
        general = eng.value_load(wide[0:1, 0:1], min_val=0, max_val=1)
        with eng.If(general == 0):
            program(eng, 0)
        with eng.Else():
            program(eng, 1)

    with nc.Block() as block:
        @block.sync
        def _(eng):
            eng.dma_start(U2[:, 0, :].rearrange("p (c n) -> p c n", c=KC),
                          w2.rearrange("(c p) n -> p c n", p=P)).then_inc(w_in, 16)
            eng.dma_start(b2b[:, :], b2.partition_broadcast(P)).then_inc(w_in, 16)
            for half in range(2):
                eng.dma_start(U2[half * ED:(half + 1) * ED, 1, 0:D], w1[2 * D:2 * D + ED, :])\
                    .then_inc(w_in, 16)

            def attributes(i, d):
                s = d % 2
                wait(eng, ea_at, 2 * grp(i, d - 1))
                for half in range(2):
                    eng.dma_start(ea[half * ED:(half + 1) * ED, s, :],
                                  edge_attr[:, bass.ds(tile(i, d, 0) * P, TG * P)])\
                        .then_inc(ea_in[s], 16)

            attributes(0, 0)
            attributes(0, 1)
            with eng.Fori(0, GROUPS // 2 - 1, 1) as i:
                attributes(i, 2)
                attributes(i, 3)

        @block.gpsimd
        def _(eng):
            pool_program(eng)

        @block.tensor
        def _(eng):
            branch(eng, pe_program)

        @block.scalar
        def _(eng):
            act_program(eng, 0)

        @block.vector
        def _(eng):
            branch(eng, dve_program)


def node_mlp(nc, st, sbuf, psum, sem, x1, h1, h1t, aggt, ident, w3, b3, w4, b4, gamma, beta, out_v):
    w3s = sbuf(st, "w3s", [P, 2 * KC, D])
    w4s = sbuf(st, "w4s", [P, KC, D])
    rows = sbuf(st, "rows5", [NP, 4, D])
    Z = sbuf(st, "Z", [NP, 2, D])
    U = sbuf(st, "U", [NP, 2, D])
    ut = sbuf(st, "ut", [P, 2, D])
    stats = sbuf(st, "stats2", [NP, NT, 6])
    mv = sbuf(st, "mv2", [NP, NT, 2])
    std = sbuf(st, "std2", [NP, NT])
    rstd = sbuf(st, "rstd2", [NP, NT])
    eps = sbuf(st, "eps2", [NP, 1])
    p3 = psum(st, "p3", [P, 2, D])
    pt = psum(st, "pt3", [P, 2, D])
    p4 = psum(st, "p4", [P, 2, D])
    w_in = sem(st, "w34_in")
    eps_at = sem(st, "eps2_at")
    mm3 = sem(st, "mm3")
    z_at = sem(st, "z_at")
    e_at = sem(st, "e_at")
    cut = sem(st, "cut")
    l_at = sem(st, "l_at")
    t_at = sem(st, "t_at")
    u_at = sem(st, "u_at")
    tp = sem(st, "tp3")
    ut_at = sem(st, "ut_at")
    mm4 = sem(st, "mm4")
    y_a = sem(st, "y_a")
    y_at = sem(st, "y_at")
    stat = sem(st, "stat2")
    std_at = sem(st, "std2_at")
    r_at = sem(st, "r_at")
    f1 = sem(st, "f1")
    f2 = sem(st, "f2")
    f3 = sem(st, "f3")
    f4 = sem(st, "f4")
    stored = sem(st, "stored")
    with nc.Block() as block:
        @block.sync
        def _(eng):
            eng.dma_start(w3s[:, :, :], w3.rearrange("(c p) n -> p c n", p=P)).then_inc(w_in, 16)
            eng.dma_start(w4s[:, :, :], w4.rearrange("(c p) n -> p c n", p=P)).then_inc(w_in, 16)
            for n, v in enumerate((b3, b4, gamma, beta)):
                eng.dma_start(rows[:, n, :], v.partition_broadcast(NP)).then_inc(w_in, 16)
            for t in range(NT):
                eng.wait_ge(f4, t + 1)
                eng.dma_start(out_v[:, t, :], x1[:, t, :]).then_inc(stored, 16)
            eng.wait_ge(stored, 16 * NT)

        @block.tensor
        def _(eng):
            eng.wait_ge(w_in, 96)

            def first(t):
                wait(eng, z_at, t - 1)
                for c in range(2 * KC):
                    lhs = (h1t if c < KC else aggt)[:, c % KC, t * NP:(t + 1) * NP]
                    mm = eng.matmul(p3[0:NP, t % 2, :], lhs, w3s[:, c, :], start=(c == 0),
                                    stop=(c == 2 * KC - 1))
                mm.then_inc(mm3, 1)

            def second(t):
                eng.wait_ge(u_at, t + 1)
                wait(eng, ut_at, t - 1)
                for c in range(KC):
                    mm = eng.transpose(pt[:, t % 2, c * P:c * P + NP],
                                       U[:, t % 2, c * P:(c + 1) * P], ident[0:NP, 0:NP])
                mm.then_inc(tp, 1)
                eng.wait_ge(ut_at, t + 1)
                wait(eng, y_a, t - 1)
                for c in range(KC):
                    mm = eng.matmul(p4[0:NP, t % 2, :], ut[:, t % 2, c * P:c * P + NP], w4s[:, c, :],
                                    start=(c == 0), stop=(c == KC - 1))
                mm.then_inc(mm4, 1)

            first(0)
            for t in range(NT):
                if t + 1 < NT:
                    first(t + 1)
                second(t)

        @block.scalar
        def _(eng):
            for t in range(NT):
                s = t % 2
                eng.wait_ge(z_at, t + 1)
                wait(eng, tp, t - 1)
                eng.activation(U[:, s, :], Z[:, s, :], ACT.Exp).then_inc(e_at, 1)
                eng.wait_ge(cut, t + 1)
                eng.activation(U[:, s, :], U[:, s, :], ACT.Ln, bias=1.0).then_inc(l_at, 1)
                eng.wait_ge(l_at, t + 1)
                eng.activation(U[:, s, :], U[:, s, :], ACT.Tanh).then_inc(t_at, 1)
                eng.wait_ge(tp, t + 1)
                wait(eng, mm4, t - 1)
                view = "p (c n) -> p c n"
                eng.activation(ut[:, s, :].rearrange(view, c=KC)[:, :, 0:NP],
                               pt[:, s, :].rearrange(view, c=KC)[:, :, 0:NP], ACT.Copy)\
                    .then_inc(ut_at, 1)
            eng.wait_ge(stat, 2 * NT)
            eng.wait_ge(eps_at, 1)
            eng.activation(std[:, :], mv[:, :, 1:2].squeeze(2), ACT.Sqrt, bias=eps[:, :])\
                .then_inc(std_at, 1)

        @block.vector
        def _(eng):
            eng.memset(eps[:, :], EPS).then_inc(eps_at, 1)
            eng.wait_ge(w_in, 96)

            def z_part(t):
                s = t % 2
                eng.wait_ge(mm3, t + 1)
                wait(eng, u_at, t - 1)
                eng.tensor_tensor(Z[:, s, :], p3[0:NP, s, :], rows[:, 0, :], ALU.add)\
                    .then_inc(z_at, 1)
                eng.wait_ge(e_at, t + 1)
                eng.tensor_scalar(U[:, s, :], U[:, s, :], U_MAX, None, ALU.min).then_inc(cut, 1)

            def y_part(t):
                eng.wait_ge(mm4, t + 1)
                eng.tensor_tensor(h1[:, t, :], h1[:, t, :], p4[0:NP, t % 2, :], ALU.add)\
                    .then_inc(y_a, 1)
                eng.wait_ge(y_a, t + 1)
                eng.tensor_tensor(h1[:, t, :], h1[:, t, :], rows[:, 1, :], ALU.add)\
                    .then_inc(y_at, 1)
                eng.wait_ge(y_at, t + 1)
                eng.bn_stats(stats[:, t, :], h1[:, t, :]).then_inc(stat, 1)

            for t in range(NT):
                z_part(t)
                if t > 0:
                    y_part(t - 1)
                eng.wait_ge(t_at, t + 1)
                eng.tensor_tensor(U[:, t % 2, :], U[:, t % 2, :], Z[:, t % 2, :], ALU.mult)\
                    .then_inc(u_at, 1)
            y_part(NT - 1)
            for t in range(NT):
                eng.wait_ge(stat, t + 1)
                eng.bn_aggr(mv[:, t, :], stats[:, t, :]).then_inc(stat, 1)
            eng.wait_ge(std_at, 1)
            eng.reciprocal(rstd[:, :], std[:, :]).then_inc(r_at, 1)
            eng.wait_ge(r_at, 1)
            for t in range(NT):
                eng.tensor_scalar(h1[:, t, :], h1[:, t, :], mv[:, t, 0:1], rstd[:, t:t + 1],
                                  ALU.subtract, ALU.mult).then_inc(f1, 1)
                eng.wait_ge(f1, t + 1)
                eng.tensor_tensor(h1[:, t, :], h1[:, t, :], rows[:, 2, :], ALU.mult).then_inc(f2, 1)
                eng.tensor_tensor(x1[:, t, :], x1[:, t, :], rows[:, 3, :], ALU.add).then_inc(f3, 1)
                eng.wait_ge(f2, t + 1)
                eng.wait_ge(f3, t + 1)
                eng.tensor_tensor(x1[:, t, :], x1[:, t, :], h1[:, t, :], ALU.add).then_inc(f4, 1)


def kernel(x, src, dst, edge_attr_64, edge_type_32, edge_weight1, L0_gnn_bases, L0_gnn_w_comp,
           L0_gnn_h_bias, L1_gnn_W1, L1_gnn_b1, L1_gnn_W2, L1_gnn_b2, L1_gnn_W3, L1_gnn_b3,
           L1_gnn_W4, L1_gnn_b4, L1_gnn_gamma, L1_gnn_beta):
    import numpy as np
    import concourse.bacc as bacc
    from concourse.bass_utils import run_bass_kernel_spmd

    def padded(a, fill):
        a = np.asarray(a).reshape(E)
        return np.concatenate([a, np.full(EPAD - E, fill, a.dtype)])

    def by_tile(a, fill):
        return np.ascontiguousarray(padded(a, fill).reshape(T, P).T)

    attr = np.zeros((ED, EPAD), np.asarray(edge_attr_64).dtype)
    attr[:, :E] = np.asarray(edge_attr_64).T
    given = {
        "x": x, "src_t": by_tile(src, 0), "dst_t": by_tile(dst, -1), "etype": padded(edge_type_32, 0),
        "norm_t": by_tile(edge_weight1, 0), "edge_attr": attr, "bases": L0_gnn_bases,
        "w_comp": L0_gnn_w_comp, "h_bias": L0_gnn_h_bias, "w1": L1_gnn_W1, "b1": L1_gnn_b1,
        "w2": L1_gnn_W2, "b2": L1_gnn_b2, "w3": L1_gnn_W3, "b3": L1_gnn_b3, "w4": L1_gnn_W4,
        "b4": L1_gnn_b4, "gamma": L1_gnn_gamma, "beta": L1_gnn_beta,
    }
    nc = bacc.Bacc("TRN2", target_bir_lowering=False, num_devices=1)
    arrays, args = {}, []
    for name, a in given.items():
        a = np.ascontiguousarray(a)
        arrays[f"in_{name}"] = a
        args.append(nc.dram_tensor(f"in_{name}", a.shape, mybir.dt.from_np(a.dtype),
                                   kind="ExternalInput").ap())
    args.append(nc.dram_tensor("out_0", (N, D), F32, kind="ExternalOutput").ap())
    gnn_kernel(nc, *args)
    r = run_bass_kernel_spmd(nc, [arrays], core_ids=[0])
    return r.results[0]["out_0"]
```

```python
from contextlib import ExitStack

import concourse.bass as bass
from concourse import mybir

F32 = mybir.dt.float32
F32R = mybir.dt.float32r
I32 = mybir.dt.int32
ALU = mybir.AluOpType
ACT = mybir.ActivationFunctionType
AX_X = mybir.AxisListType.X

P = 128
N = 1250
E = 21250
D = 512
KC = D // P
ED = 64
R = 32
NB = 8
NP = 125
NT = N // NP
TG = 4
GROUPS = -(-E // (P * TG * 2)) * 2
T = GROUPS * TG
EPAD = T * P
FULL = E // P
REST = E - FULL * P
WN = 16
WINDOWS = -(-N // WN)
NPAD = N + WN
BR = ED
ROWS = 8
BANKS = 4
QT = P // R
TQ = T // QT
TCH = 21
CHUNKS = TQ // TCH
HALF = 512 // (QT * NB)
U_MAX = 1e18
EPS = 1e-5


def wait(eng, sem, value):
    if not (isinstance(value, int) and value <= 0):
        eng.wait_ge(sem, value)


def carrier(eng, turns):
    return lambda: eng.sem_inc(turns, 1)


def gnn_kernel(nc, x, src_t, dst_t, dst_e, etype, norm_t, edge_attr, bases, w_comp, h_bias, w1, b1, w2, b2,
               w3, b3, w4, b4, gamma, beta, out):
    h0_rows = nc.dram_tensor("h0_rows", [N, D], F32, kind="Internal").ap()
    xa_rows = nc.dram_tensor("xa_rows", [N, D], F32, kind="Internal").ap()
    xb_parts = nc.dram_tensor("xb_parts", [NPAD, 2, D], F32, kind="Internal").ap()
    by_tile = "(t p) f -> p t f"
    x_v = x.rearrange(by_tile, p=NP)
    out_v = out.rearrange(by_tile, p=NP)
    h0_v = h0_rows.rearrange(by_tile, p=NP)
    xa_v = xa_rows.rearrange(by_tile, p=NP)
    xb_v = xb_parts[0:N, :, :].rearrange("(t p) h f -> p t h f", p=NP)

    with ExitStack() as whole:
        def sbuf(stack, name, shape, dt=F32):
            return stack.enter_context(nc.sbuf_tensor(name, shape, dt))

        def psum(stack, name, shape):
            return stack.enter_context(nc.psum_tensor(name, shape, F32))

        def sem(stack, name):
            return stack.enter_context(nc.semaphore(name))

        src_idx = sbuf(whole, "src_idx", [P, T], I32)
        dst_idx = sbuf(whole, "dst_idx", [P, T], I32)
        dst_row = sbuf(whole, "dst_row", [P, T], I32)
        dst_rel = sbuf(whole, "dst_rel", [P, T + TG])
        wide = sbuf(whole, "wide", [1, 1], I32)
        win_node = sbuf(whole, "win_node", [P, T])
        iota = sbuf(whole, "iota", [P, WN])
        ident = sbuf(whole, "ident", [P, P])
        x1 = sbuf(whole, "x1", [NP, NT, D])

        layer0 = whole.enter_context(ExitStack())
        coef = sbuf(layer0, "coef", [P, T + TG, NB])
        with ExitStack() as st:
            norm_sb = sbuf(st, "norm_sb", [P, T])
            wc = sbuf(st, "wc", [P, QT, NB])
            etype_b = sbuf(st, "etype_b", [P, CHUNKS, TCH * P], I32)
            type_hot = sbuf(st, "type_hot", [P, CHUNKS, TCH * P])
            rel_id_i = sbuf(st, "rel_id_i", [P, 1], I32)
            rel_id = sbuf(st, "rel_id", [P, 1])
            half_i = sbuf(st, "half_i", [P, 1], I32)
            half_f = sbuf(st, "half_f", [P, 1])
            ones = sbuf(st, "ones", [1, P])
            base_f = sbuf(st, "base_f", [1, T])
            off = sbuf(st, "off", [P, T])
            far = sbuf(st, "far", [P, 2])
            far1 = sbuf(st, "far1", [P, 1])
            wide_f = sbuf(st, "wide_f", [1, 2])
            stats = sbuf(st, "stats", [NP, NT, 6])
            mv = sbuf(st, "mv", [NP, NT, 2])
            std = sbuf(st, "std", [NP, NT])
            rstd = sbuf(st, "rstd", [NP, NT])
            eps = sbuf(st, "eps", [NP, 1])
            h0 = sbuf(st, "h0", [NP, NT, D])
            base_ps = psum(st, "base_ps", [P, 512])
            far_ps = psum(st, "far_ps", [P, 512])
            coef_ps = psum(st, "coef_ps", [P, CHUNKS, 2, 512])

            idx_in = sem(st, "idx_in")
            x_in = sem(st, "x_in")
            type_in = [sem(st, f"type_in{i}") for i in range(CHUNKS)]
            made = sem(st, "made")
            pads = sem(st, "pads")
            consts = sem(st, "consts")
            base_done = sem(st, "base_done")
            base_at = sem(st, "base_at")
            check = sem(st, "check")
            far_t = sem(st, "far_t")
            flag_at = sem(st, "flag_at")
            hot = sem(st, "hot")
            coef_mm = sem(st, "coef_mm")
            wc_in = sem(st, "wc_in")
            stat = sem(st, "stat")
            std_at = sem(st, "std_at")
            norm_at = sem(st, "norm_at")
            h_at = sem(st, "h_at")
            h_out = sem(st, "h_out")
            with nc.Block() as block:
                @block.sync
                def _(eng):
                    eng.dma_start(dst_idx[:, :], dst_t).then_inc(idx_in, 16)
                    eng.dma_start(x1[:, :, :], x_v).then_inc(x_in, 16)
                    eng.dma_start(src_idx[:, :], src_t).then_inc(idx_in, 16)
                    eng.dma_start(norm_sb[:, :], norm_t).then_inc(idx_in, 16)
                    types = etype.rearrange("(c j q e) -> c q j e", c=CHUNKS, q=QT, e=P)
                    for c in range(CHUNKS):
                        for q in range(QT):
                            eng.dma_start(etype_b[q * R:(q + 1) * R, c, :].rearrange("p (j e) -> p j e", e=P),
                                          types[c, q].partition_broadcast(R)).then_inc(type_in[c], 16)
                    for t in range(0, NT, 2):
                        eng.wait_ge(h_at, t + 2)
                        eng.dma_start(h0_v[:, t:t + 2, :], h0[:, t:t + 2, :]).then_inc(h_out, 16)
                    eng.wait_ge(h_out, 16 * (NT // 2))

                @block.gpsimd
                def _(eng):
                    eng.memset(ident[:, :], 0.0).then_inc(made, 1)
                    eng.wait_ge(made, 1)
                    eng.affine_select(out=ident[:, :], in_=ident[:, :], compare_op=ALU.not_equal,
                                      fill=1.0, base=0, pattern=[[-1, P]], channel_multiplier=1)\
                        .then_inc(made, 1)
                    eng.iota(iota[:, :], [[1, WN]], base=0, channel_multiplier=0,
                             allow_small_or_imprecise_dtypes=True).then_inc(made, 1)
                    eng.iota(rel_id_i[:, :], [[0, 1]], base=0, channel_multiplier=1).then_inc(made, 1)
                    eng.iota(half_i[:, :], [[0, 1]], base=0, channel_multiplier=1).then_inc(made, 1)

                @block.vector
                def _(eng):
                    eng.memset(ones[:, :], 1.0).then_inc(consts, 1)
                    eng.memset(dst_rel[:, T:T + TG], -1.0).then_inc(consts, 1)
                    eng.memset(coef[:, T:T + TG, :], 0.0).then_inc(consts, 1)
                    eng.memset(far[:, :], 0.0).then_inc(consts, 1)
                    eng.memset(eps[:, :], EPS).then_inc(consts, 1)
                    eng.memset(wc[:, :, :], 0.0).then_inc(consts, 1)
                    eng.wait_ge(idx_in, 48)
                    eng.tensor_scalar(dst_row[:, :], dst_idx[:, :], 0.0, None, ALU.max)\
                        .then_inc(base_done, 1)
                    eng.wait_ge(base_done, 1)
                    eng.tensor_copy(base_f[:, :], dst_row[0:1, :]).then_inc(base_done, 1)
                    eng.wait_ge(made, 5)
                    eng.tensor_scalar(rel_id_i[:, :], rel_id_i[:, :], R - 1, None, ALU.bitwise_and)\
                        .then_inc(base_done, 1)
                    eng.wait_ge(base_done, 3)
                    eng.tensor_copy(rel_id[:, :], rel_id_i[:, :]).then_inc(base_done, 1)
                    eng.tensor_scalar(half_i[:, :], half_i[:, :], 1, None, ALU.logical_shift_right)\
                        .then_inc(base_done, 1)
                    eng.wait_ge(base_done, 5)
                    eng.tensor_copy(half_f[:, :], half_i[:, :]).then_inc(base_done, 1)
                    eng.wait_ge(x_in, 16)
                    for t in range(NT):
                        eng.bn_stats(stats[:, t, :], x1[:, t, :]).then_inc(stat, 1)
                    for t in range(NT):
                        eng.wait_ge(stat, t + 1)
                        eng.bn_aggr(mv[:, t, :], stats[:, t, :]).then_inc(stat, 1)
                    eng.wait_ge(base_at, 1)
                    eng.tensor_tensor(dst_rel[:, 0:T], dst_idx[:, :], base_ps[:, 0:T], ALU.subtract)\
                        .then_inc(check, 1)
                    eng.wait_ge(base_done, 6)
                    eng.tensor_scalar(win_node[BR:BR + 2 * WN, :], base_ps[BR:BR + 2 * WN, 0:T],
                                      half_f[BR:BR + 2 * WN, :], -BR / 2, ALU.add, ALU.add)\
                        .then_inc(base_done, 1)
                    eng.wait_ge(check, 1)
                    eng.tensor_scalar(off[:, :], dst_rel[:, 0:T], -(WN - 1) / 2, None, ALU.add)\
                        .then_inc(check, 1)
                    eng.wait_ge(check, 2)
                    eng.tensor_tensor(off[:, :], off[:, :], off[:, :], ALU.mult).then_inc(check, 1)
                    eng.wait_ge(check, 3)
                    eng.wait_ge(consts, 5)
                    eng.reduce_max(far[:, 0:1], off[:, 0:FULL], axis=AX_X).then_inc(check, 1)
                    if REST:
                        eng.reduce_max(far[0:REST, 1:2], off[0:REST, FULL:FULL + 1], axis=AX_X)\
                            .then_inc(check, 1)
                    eng.wait_ge(check, 4 + (REST > 0))
                    eng.reduce_max(far1[:, :], far[:, :], axis=AX_X).then_inc(check, 1)
                    eng.wait_ge(far_t, 1)
                    eng.reduce_max(wide_f[:, 0:1], far_ps[0:1, 0:P], axis=AX_X).then_inc(flag_at, 1)
                    eng.wait_ge(flag_at, 1)
                    eng.tensor_scalar(wide[:, :], wide_f[:, 0:1], (WN / 2) ** 2, None, ALU.is_ge)\
                        .then_inc(flag_at, 1)
                    for c in range(CHUNKS):
                        eng.wait_ge(type_in[c], 16 * QT)
                        eng.tensor_scalar(type_hot[:, c, :], etype_b[:, c, :], rel_id[:, :], None,
                                          ALU.is_equal).then_inc(hot, 1)
                    eng.wait_ge(std_at, 1)
                    eng.reciprocal(rstd[:, :], std[:, :]).then_inc(norm_at, 1)
                    eng.wait_ge(norm_at, 1)
                    for t in range(NT):
                        eng.tensor_scalar(h0[:, t, :], x1[:, t, :], mv[:, t, 0:1], rstd[:, t:t + 1],
                                          ALU.subtract, ALU.mult).then_inc(norm_at, 1)
                    for t in range(NT):
                        eng.wait_ge(norm_at, 2 + t)
                        eng.tensor_scalar(h0[:, t, :], h0[:, t, :], 0.0, None, ALU.max)\
                            .then_inc(h_at, 1)
                    for c in range(CHUNKS):
                        for h in range(2):
                            g0, g1 = (0, HALF) if h == 0 else (HALF, TCH)
                            t0 = (c * TCH + g0) * QT
                            n = (g1 - g0) * QT
                            eng.wait_ge(coef_mm, 2 * c + h + 1)
                            eng.tensor_tensor(
                                coef[:, t0:t0 + n, :],
                                coef_ps[:, c, h, 0:n * NB].rearrange("p (t b) -> p t b", b=NB),
                                norm_sb[:, t0:t0 + n].unsqueeze(2).to_broadcast([P, n, NB]),
                                ALU.mult)

                @block.tensor
                def _(eng):
                    eng.wait_ge(base_done, 2)
                    eng.wait_ge(consts, 1)
                    eng.matmul(base_ps[:, 0:T], ones[:, :], base_f[:, :], start=True, stop=True)\
                        .then_inc(base_at, 1)
                    eng.wait_ge(check, 5 + (REST > 0))
                    eng.wait_ge(made, 2)
                    eng.transpose(far_ps[0:1, 0:P], far1[:, :], ident[:, :]).then_inc(far_t, 1)
                    eng.wait_ge(wc_in, 16 * QT)
                    for c in range(CHUNKS):
                        eng.wait_ge(hot, c + 1)
                        for g in range(TCH):
                            h, col = divmod(g, HALF)
                            mm = eng.matmul(coef_ps[:, c, h, col * QT * NB:(col + 1) * QT * NB],
                                            type_hot[:, c, g * P:(g + 1) * P],
                                            wc[:, :, :].rearrange("p q b -> p (q b)"),
                                            start=True, stop=True)
                            if g in (HALF - 1, TCH - 1):
                                mm.then_inc(coef_mm, 1)

                @block.scalar
                def _(eng):
                    eng.wait_ge(consts, 6)
                    for q in range(QT):
                        eng.dma_start(wc[q * R:(q + 1) * R, q, :], w_comp).then_inc(wc_in, 16)
                    eng.wait_ge(stat, 2 * NT)
                    eng.activation(std[:, :], mv[:, :, 1:2].squeeze(2), ACT.Sqrt, bias=eps[:, :])\
                        .then_inc(std_at, 1)

        with ExitStack() as st:
            G = sbuf(st, "G", [P, KC, NB, NPAD])
            with ExitStack() as st2:
                scatter_layer0(nc, st2, sbuf, psum, sem, G, h0_rows, src_idx, dst_idx, dst_row,
                               dst_rel, coef, iota, wide)
            with ExitStack() as st2:
                apply_bases(nc, st2, sbuf, psum, sem, G, bases, h_bias, x1)
        layer0.close()

        with ExitStack() as st:
            h1 = sbuf(st, "h1", [NP, NT, D])
            h1t = sbuf(st, "h1t", [P, KC, N])
            with ExitStack() as st2:
                node_products(nc, st2, sbuf, psum, sem, x1, h1, h1t, ident, w1, b1, xa_v, xb_v,
                              xb_parts)
            aggt = sbuf(st, "aggt", [P, KC, NPAD])
            with ExitStack() as st2:
                edge_mlp(nc, st2, sbuf, psum, sem, aggt, xa_rows, xb_parts, edge_attr, w1, w2, b2,
                         src_idx, dst_idx, dst_e, dst_row, dst_rel, win_node, iota, ident, wide)
            with ExitStack() as st2:
                node_mlp(nc, st2, sbuf, psum, sem, x1, h1, h1t, aggt, ident, w3, b3, w4, b4, gamma,
                         beta, out_v)


def scatter_layer0(nc, st, sbuf, psum, sem, G, h0_rows, src_idx, dst_idx, dst_row, dst_rel, coef,
                   iota, wide):
    rows = sbuf(st, "rows", [P, ROWS, D])
    idx = sbuf(st, "l0_idx", [P, ROWS], I32)
    S = sbuf(st, "S", [P, ROWS, NB, WN])
    ps = psum(st, "l0_ps", [P, BANKS, KC * NB * WN])
    rows_in = [sem(st, f"rows_in{i}") for i in range(ROWS)]
    idx_at = sem(st, "l0_idx_at")
    s_at = sem(st, "s_at")
    mm_done = sem(st, "mm_done")
    added = sem(st, "added")
    w_s = sem(st, "w_s")
    w_mm = sem(st, "w_mm")
    w_add = sem(st, "w_add")
    w_node = sem(st, "w_node")
    pool_turns = sem(st, "l0_pool_turns")
    pe_turns = sem(st, "l0_pe_turns")
    zero = sbuf(st, "zero", [P, 1])
    zero_at = sem(st, "zero_at")
    g_zero = sem(st, "g_zero")
    node = sbuf(st, "l0_node", [P, 1])

    def gather(eng, i, q, rows_free, per_tile, carry):
        if q % TG == 0:
            half = slice(q, q + TG)
            for k in range(q, q + TG):
                wait(eng, rows_in[k], 16 * i)
            eng.tensor_copy(idx[:, half], src_idx[:, bass.ds(ROWS * i + q, TG)]).then_inc(idx_at, 1)
            eng.wait_ge(idx_at, 2 * i + q // TG + 1)
        eng.wait_ge(rows_free, (ROWS * i + q + 1) * per_tile)
        carry()
        eng.indirect_dma_start(rows[:, q, :], None, h0_rows,
                               bass.IndirectOffsetOnAxis(ap=idx[:, q:q + 1], axis=0))\
            .then_inc(rows_in[q], 16)

    def gathers(eng, rows_free, per_tile):
        carry = carrier(eng, pool_turns)
        for q in range(ROWS):
            gather(eng, 0, q, rows_free, per_tile, carry)
        with eng.Fori(1, T // ROWS, 1) as i:
            for q in range(ROWS):
                gather(eng, i, q, rows_free, per_tile, carry)

    def products(eng, q, bank):
        for c in range(KC):
            mm = eng.matmul(ps[:, bank, c * NB * WN:(c + 1) * NB * WN],
                            rows[:, q, c * P:(c + 1) * P],
                            S[:, q, :, :].rearrange("p b n -> p (b n)"), start=True, stop=True)
        return mm

    def build_s(eng, t, q, node):
        return eng.scalar_tensor_tensor(
            S[:, q, :, :], iota[:, :].unsqueeze(1).to_broadcast([P, NB, WN]), node,
            coef[:, bass.ds(t, 1), :].squeeze(1).unsqueeze(2).to_broadcast([P, NB, WN]),
            ALU.is_equal, ALU.mult)

    def zero_part(part):
        half = slice(part * KC // 2, (part + 1) * KC // 2)
        return G[:, half, :, :].rearrange("p c b n -> p (c b n)")

    def add_to_g(eng, base, bank):
        window = G[:, :, :, bass.ds(base, WN)].rearrange("p c b n -> p (c b) n")
        return eng.tensor_tensor(window, window,
                                 ps[:, bank, :].rearrange("p (m n) -> p m n", n=WN), ALU.add)

    with nc.Block() as block:
        @block.gpsimd
        def _(eng):
            general = eng.value_load(wide[0:1, 0:1], min_val=0, max_val=1)
            with eng.If(general == 0):
                gathers(eng, mm_done, 1)
            with eng.Else():
                gathers(eng, w_mm, WINDOWS)

        @block.scalar
        def _(eng):
            eng.wait_ge(zero_at, 1)
            part = zero_part(1)
            n = part.shape[1]
            eng.activation(part, zero[:, :].to_broadcast([P, n]), ACT.Copy).then_inc(g_zero, 1)

        @block.tensor
        def _(eng):
            general = eng.value_load(wide[0:1, 0:1], min_val=0, max_val=1)
            with eng.If(general == 0):
                eng.sem_inc(mm_done, ROWS)
                with eng.Fori(0, T // ROWS, 1) as i:
                    for q in range(ROWS):
                        t = ROWS * i + q
                        eng.wait_ge(rows_in[q], 16 * i + 16)
                        eng.wait_ge(s_at, t + 1)
                        eng.wait_ge(added, t + 1)
                        products(eng, q, q % BANKS).then_inc(mm_done, 1)
            with eng.Else():
                eng.sem_inc(w_mm, ROWS * WINDOWS)
                carry = carrier(eng, pe_turns)
                with eng.Fori(0, T // ROWS, 1) as i:
                    for q in range(ROWS):
                        eng.wait_ge(rows_in[q], 16 * i + 16)
                        carry()
                        with eng.Fori(0, WINDOWS, 1) as w:
                            n = (ROWS * i + q) * WINDOWS + w
                            eng.wait_ge(w_s, n + 1)
                            eng.wait_ge(w_add, n + 1)
                            products(eng, q, 0).then_inc(w_mm, 1)

        @block.vector
        def _(eng):
            eng.memset(zero[:, :], 0.0).then_inc(zero_at, 1)
            general = eng.value_load(wide[0:1, 0:1], min_val=0, max_val=1)
            with eng.If(general == 0):
                starts = [eng.alloc_register(f"l0_start{k}") for k in range(TG)]
                eng.memset(zero_part(0), 0.0).then_inc(g_zero, 1)
                for k in range(TG):
                    build_s(eng, k, k, dst_rel[:, k:k + 1]).then_inc(s_at, 1)
                eng.wait_ge(g_zero, 2)
                eng.sem_inc(added, BANKS)
                with eng.Fori(0, T // ROWS, 1) as i:
                    for half in range(2):
                        t0 = ROWS * i + half * TG
                        eng.reg_load(starts, dst_row[0:1, bass.ds(t0, TG)])
                        eng.wait_ge(mm_done, ROWS + t0)
                        for k in range(TG):
                            t = t0 + TG + k
                            build_s(eng, t, (1 - half) * TG + k, dst_rel[:, bass.ds(t, 1)])\
                                .then_inc(s_at, 1)
                        for k in range(TG):
                            eng.wait_ge(mm_done, ROWS + t0 + k + 1)
                            eng.wait_ge(added, BANKS + t0 + k)
                            start = eng.snap(starts[k], min_val=0, max_val=N - 1)
                            add_to_g(eng, start, k).then_inc(added, 1)
            with eng.Else():
                eng.memset(zero_part(0), 0.0).then_inc(g_zero, 1)
                eng.wait_ge(g_zero, 2)
                eng.sem_inc(w_add, 1)
                with eng.Fori(0, T // ROWS, 1) as i:
                    for q in range(ROWS):
                        t = ROWS * i + q
                        eng.wait_ge(w_add, t * WINDOWS + 1)
                        eng.tensor_copy(node[:, :], dst_idx[:, bass.ds(t, 1)]).then_inc(w_node, 1)
                        with eng.Fori(0, WINDOWS, 1) as w:
                            n = t * WINDOWS + w
                            eng.wait_ge(w_node, n + t + 1)
                            build_s(eng, t, q, node[:, :]).then_inc(w_s, 1)
                            eng.wait_ge(w_s, n + 1)
                            eng.tensor_scalar(node[:, :], node[:, :], -float(WN), None, ALU.add)\
                                .then_inc(w_node, 1)
                            eng.wait_ge(w_mm, ROWS * WINDOWS + n + 1)
                            add_to_g(eng, w * WN, 0).then_inc(w_add, 1)


def apply_bases(nc, st, sbuf, psum, sem, G, bases, h_bias, x1):
    RING = 4
    ROUND = NT // 2
    wb = sbuf(st, "wb", [P, RING, D])
    bias = sbuf(st, "bias0", [NP, D])
    ps = psum(st, "b_ps", [P, 8, D])
    wb_in = [sem(st, f"wb_in{i}") for i in range(RING)]
    bias_in = sem(st, "bias0_in")
    used = sem(st, "wb_used")
    summed = sem(st, "summed")
    got = sem(st, "got")
    x1_at = sem(st, "x1_at")
    pieces = NB * KC
    with nc.Block() as block:
        @block.sync
        def _(eng):
            for m in range(2 * pieces):
                b, c = divmod(m % pieces, KC)
                wait(eng, used, m - RING + 1)
                eng.dma_start(wb[:, m % RING, :], bases[b, c * P:(c + 1) * P, :])\
                    .then_inc(wb_in[m % RING], 16)

        @block.scalar
        def _(eng):
            eng.dma_start(bias[:, :], h_bias.partition_broadcast(NP)).then_inc(bias_in, 16)

        @block.tensor
        def _(eng):
            for m in range(2 * pieces):
                r = m // pieces
                b, c = divmod(m % pieces, KC)
                eng.wait_ge(wb_in[m % RING], 16 * (m // RING + 1))
                for k in range(ROUND):
                    t = r * ROUND + k
                    if m % pieces == 0 and t >= 8:
                        eng.wait_ge(got, t - 8 + 1)
                    mm = eng.matmul(ps[0:NP, t % 8, :], G[:, c, b, t * NP:(t + 1) * NP],
                                    wb[:, m % RING, :], start=(m % pieces == 0),
                                    stop=(m % pieces == pieces - 1))
                mm.then_inc(used, 1)

        @block.vector
        def _(eng):
            eng.wait_ge(bias_in, 16)
            for t in range(NT):
                eng.wait_ge(used, pieces * (t // ROUND + 1))
                eng.tensor_tensor(x1[:, t, :], x1[:, t, :], ps[0:NP, t % 8, :], ALU.add)\
                    .then_inc(got, 1)
                eng.wait_ge(got, t + 1)
                eng.tensor_tensor(x1[:, t, :], x1[:, t, :], bias[:, :], ALU.add).then_inc(x1_at, 1)


def node_products(nc, st, sbuf, psum, sem, x1, h1, h1t, ident, w1, b1, xa_v, xb_v, xb_parts):
    w1ab = sbuf(st, "w1ab", [P, 2, KC, D])
    b1b = sbuf(st, "b1b", [NP, D])
    stats = sbuf(st, "stats1", [NP, NT, 6])
    mv = sbuf(st, "mv1", [NP, NT, 2])
    std = sbuf(st, "std1", [NP, NT])
    rstd = sbuf(st, "rstd1", [NP, NT])
    eps = sbuf(st, "eps1", [NP, 1])
    rows_a = sbuf(st, "rows_a", [NP, 2, D])
    rows_b = sbuf(st, "rows_b", [NP, 2, D])
    parts_b = sbuf(st, "parts_b", [NP, 2, 2, D], F32R)
    pad_b = sbuf(st, "pad_b", [WN, 2, D], F32R)
    tp = psum(st, "tp1", [P, 2, D])
    ps = psum(st, "ab_ps", [P, 4, D])
    w_in = sem(st, "w1_in")
    eps_at = sem(st, "eps1_at")
    stat = sem(st, "stat1")
    std_at = sem(st, "std1_at")
    norm_at = sem(st, "norm1_at")
    h_at = sem(st, "h1_at")
    tp_done = sem(st, "tp1_done")
    ht_at = sem(st, "h1t_at")
    ab_mm = sem(st, "ab_mm")
    ab_at = sem(st, "ab_at")
    parts_at = sem(st, "parts_at")
    pad_at = sem(st, "pad_at")
    pad_out = sem(st, "pad_out")
    ab_out = [sem(st, f"ab_out{i}") for i in range(2)]
    with nc.Block() as block:
        @block.sync
        def _(eng):
            for a in range(2):
                eng.dma_start(w1ab[:, a, :, :],
                              w1[a * D:(a + 1) * D, :].rearrange("(c p) n -> p c n", p=P))\
                    .then_inc(w_in, 16)
            eng.dma_start(b1b[:, :], b1.partition_broadcast(NP)).then_inc(w_in, 16)
            eng.wait_ge(pad_at, 2)
            eng.dma_start(xb_parts[N:NPAD, :, :], pad_b[:, :, :].bitcast(F32)).then_inc(pad_out, 16)
            for t in range(NT):
                eng.wait_ge(ab_at, 2 * t + 1)
                eng.dma_start(xa_v[:, t, :], rows_a[:, t % 2, :]).then_inc(ab_out[t % 2], 16)
                eng.wait_ge(parts_at, 2 * t + 2)
                eng.dma_start(xb_v[:, t, :, :], parts_b[:, t % 2, :, :].bitcast(F32))\
                    .then_inc(ab_out[t % 2], 16)
            eng.wait_ge(pad_out, 16)
            for s in range(2):
                eng.wait_ge(ab_out[s], 32 * (NT // 2))

        @block.vector
        def _(eng):
            eng.memset(eps[:, :], EPS).then_inc(eps_at, 1)
            for t in range(NT):
                eng.bn_stats(stats[:, t, :], x1[:, t, :]).then_inc(stat, 1)
            for t in range(NT):
                eng.wait_ge(stat, t + 1)
                eng.bn_aggr(mv[:, t, :], stats[:, t, :]).then_inc(stat, 1)
            eng.wait_ge(std_at, 1)
            eng.reciprocal(rstd[:, :], std[:, :]).then_inc(norm_at, 1)
            eng.wait_ge(norm_at, 1)
            for t in range(NT):
                eng.tensor_scalar(h1[:, t, :], x1[:, t, :], mv[:, t, 0:1], rstd[:, t:t + 1],
                                  ALU.subtract, ALU.mult).then_inc(norm_at, 1)
                eng.wait_ge(norm_at, 2 + t)
                eng.tensor_scalar(h1[:, t, :], h1[:, t, :], 0.0, None, ALU.max).then_inc(h_at, 1)
            eng.wait_ge(w_in, 48)
            eng.memset(rows_b[:, 0, :], 0.0).then_inc(pad_at, 1)
            eng.wait_ge(pad_at, 1)
            eng.tensor_copy(pad_b[:, :, :], rows_b[0:WN, 0, :].unsqueeze(1).to_broadcast([WN, 2, D]))\
                .then_inc(pad_at, 1)
            eng.wait_ge(pad_at, 2)
            for t in range(NT):
                eng.wait_ge(ab_mm, 2 * t + 2)
                if t >= 2:
                    eng.wait_ge(ab_out[t % 2], 32 * (t // 2))
                eng.tensor_copy(rows_a[:, t % 2, :], ps[0:NP, 2 * (t % 2), :]).then_inc(ab_at, 1)
                wait(eng, parts_at, 2 * (t - 1))
                eng.tensor_tensor(rows_b[:, t % 2, :], ps[0:NP, 2 * (t % 2) + 1, :], b1b[:, :],
                                  ALU.add).then_inc(ab_at, 1)
                eng.wait_ge(parts_at, 2 * t + 1)
                eng.tensor_tensor(parts_b[:, t % 2, 1, :], rows_b[:, t % 2, :],
                                  parts_b[:, t % 2, 0, :].bitcast(F32), ALU.subtract)\
                    .then_inc(parts_at, 1)

        @block.scalar
        def _(eng):
            def high_part(t):
                eng.wait_ge(ab_at, 2 * t + 2)
                if t >= 2:
                    eng.wait_ge(ab_out[t % 2], 32 * (t // 2))
                eng.activation(parts_b[:, t % 2, 0, :], rows_b[:, t % 2, :], ACT.Copy)\
                    .then_inc(parts_at, 1)

            eng.wait_ge(stat, 2 * NT)
            eng.wait_ge(eps_at, 1)
            eng.activation(std[:, :], mv[:, :, 1:2].squeeze(2), ACT.Sqrt, bias=eps[:, :])\
                .then_inc(std_at, 1)
            for t in range(NT):
                eng.wait_ge(tp_done, t + 1)
                eng.activation(h1t[:, :, t * NP:(t + 1) * NP],
                               tp[:, t % 2, 0:KC * P].rearrange("p (c n) -> p c n", c=KC)[:, :, 0:NP],
                               ACT.Copy).then_inc(ht_at, 1)
                if t > 0:
                    high_part(t - 1)
            high_part(NT - 1)

        @block.tensor
        def _(eng):
            def transposes(t):
                eng.wait_ge(h_at, t + 1)
                wait(eng, ht_at, t - 1)
                for c in range(KC):
                    mm = eng.transpose(tp[:, t % 2, c * P:c * P + NP], h1[:, t, c * P:(c + 1) * P],
                                       ident[0:NP, 0:NP])
                mm.then_inc(tp_done, 1)

            transposes(0)
            eng.wait_ge(w_in, 48)
            for t in range(NT):
                if t + 1 < NT:
                    transposes(t + 1)
                eng.wait_ge(ht_at, t + 1)
                for a in range(2):
                    if a == 0:
                        wait(eng, ab_at, 2 * (t - 1))
                    for c in range(KC):
                        mm = eng.matmul(ps[0:NP, 2 * (t % 2) + a, :], h1t[:, c, t * NP:(t + 1) * NP],
                                        w1ab[:, a, c, :], start=(c == 0), stop=(c == KC - 1))
                    mm.then_inc(ab_mm, 1)


def edge_mlp(nc, st, sbuf, psum, sem, aggt, xa_rows, xb_parts, edge_attr, w1, w2, b2, src_idx,
             dst_idx, dst_e, dst_row, dst_rel, win_node, iota, ident, wide):
    GF = TG * D
    X = sbuf(st, "X", [P, 2, GF])
    XB = sbuf(st, "XB", [P, 2, D])
    U1 = sbuf(st, "U1", [P, 2, GF])
    X2 = sbuf(st, "X2", [P, 2, GF])
    U2 = sbuf(st, "U2", [P, 2, GF])
    h_hi = sbuf(st, "h_hi", [P, 2, D], F32R)
    h_lo = sbuf(st, "h_lo", [P, 2, D], F32R)
    w2_hi = sbuf(st, "w2_hi", [P, KC, D], F32R)
    w2_lo = sbuf(st, "w2_lo", [P, KC, D], F32R)
    wc_hi = sbuf(st, "wc_hi", [P, D], F32R)
    ea = sbuf(st, "ea", [P, 2, TG * P])
    ea_hl = sbuf(st, "ea_hl", [P, 2, TG * P], F32R)
    ea_n = sbuf(st, "ea_n", [P, 2, TG * P], F32R)
    dst_b = sbuf(st, "dst_b", [P, 2, TG * P], I32)
    wx = sbuf(st, "wx", [P, TG, D], F32R)
    b2b = sbuf(st, "b2b", [P, D])
    one = sbuf(st, "one", [P, 2, TG, WN])
    idx_a = sbuf(st, "idx_a", [P, 2, TG], I32)
    idx_b = sbuf(st, "idx_b", [P, 1], I32)
    pz1 = psum(st, "pz1", [P, 2, D])
    pt = psum(st, "pt", [P, 2, D])
    pz2 = psum(st, "pz2", [P, 2, D])
    pg = psum(st, "pg", [P, 2, D])

    w_in = sem(st, "w2_in")
    w_split = sem(st, "w_split")
    ea_in = [sem(st, f"ea_in{i}") for i in range(2)]
    a_in = [sem(st, f"a_in{i}") for i in range(2)]
    b_in = sem(st, "b_in")
    ia_at = sem(st, "ia_at")
    ib_at = sem(st, "ib_at")
    wx_in = [sem(st, f"wx_in{i}") for i in range(TG)]
    ea_at = sem(st, "ea_at")
    hot_at = sem(st, "hot_at")
    xb_at = sem(st, "xb_at")
    x_at = sem(st, "x_at")
    z1_mm = sem(st, "z1_mm")
    z1_at = sem(st, "z1_at")
    exp1 = sem(st, "exp1")
    cut1 = sem(st, "cut1")
    ln1 = sem(st, "ln1")
    tanh1 = sem(st, "tanh1")
    hid = sem(st, "hid")
    exp2 = sem(st, "exp2")
    cut2 = sem(st, "cut2")
    ln2 = sem(st, "ln2")
    tanh2 = sem(st, "tanh2")
    msg = sem(st, "msg")
    t_mm = sem(st, "t_mm")
    hi_at = sem(st, "hi_at")
    lo_at = sem(st, "lo_at")
    z2_mm = sem(st, "z2_mm")
    z2_at = sem(st, "z2_at")
    one_at = sem(st, "one_at")
    sum_mm = sem(st, "sum_mm")
    sum_at = sem(st, "sum_at")
    g_one = sem(st, "g_one")
    g_mm = sem(st, "g_mm")
    g_at = sem(st, "g_at")
    g_node = sem(st, "g_node")
    pool_turns = sem(st, "l1_pool_turns")
    pe_turns = sem(st, "l1_pe_turns")
    node = sbuf(st, "l1_node", [P, 1])

    def grp(i, d):
        return 2 * i + d

    def tile(i, d, k):
        return 2 * TG * i + TG * d + k

    def count(i, d, per=16):
        return per * i + per * (d // 2 + 1)

    def steps(eng, step, first, last):
        lo, hi = 4, GROUPS - 4
        hi -= (hi - lo + 1) % 2
        for j in range(first, lo):
            step(0, j, j)
        with eng.Fori(0, (hi - lo + 1) // 2, 1) as i:
            for p in range(2):
                step(i, lo + p, None)
        for j in range(hi + 1, last + 1):
            step(0, j, j)

    def there(j, d):
        return j is None or 0 <= j + d < GROUPS

    def pe_program(eng, general):
        carry = carrier(eng, pe_turns)

        def edge_products(i, d, k):
            s = d % 2
            if k == 0:
                eng.wait_ge(ea_at, 3 * grp(i, d) + 3)
                if not general:
                    eng.wait_ge(hot_at, grp(i, d) + 1)
            wait(eng, z1_at, tile(i, d, k) - 1)
            eng.matmul(pz1[:, k % 2, :], ea_hl[:, s, k * P:(k + 1) * P], wc_hi[:, :], start=True,
                       stop=False)
            eng.wait_ge(wx_in[k], 16 * grp(i, d) + 16)
            rows = ED if general else BR + 2 * WN
            eng.matmul(pz1[:, k % 2, :], ea_n[0:rows, s, k * P:(k + 1) * P], wx[0:rows, k, :],
                       start=False, stop=True).then_inc(z1_mm, 1)

        def transposes(i, d, k):
            if k == 0:
                eng.wait_ge(hid, grp(i, d) + 1)
            wait(eng, lo_at, tile(i, d, k) - 1)
            for c in range(KC):
                mm = eng.transpose(pt[:, k % 2, c * P:(c + 1) * P],
                                   U1[:, d % 2, k * D + c * P:k * D + (c + 1) * P], ident[:, :])
            mm.then_inc(t_mm, 1)

        def hidden_products(i, d, k):
            eng.wait_ge(lo_at, tile(i, d, k) + 1)
            wait(eng, z2_at, tile(i, d, k) - 1)
            n = 0
            for c in range(KC):
                for part, w in ((h_hi, w2_hi), (h_hi, w2_lo), (h_lo, w2_hi)):
                    mm = eng.matmul(pz2[:, k % 2, :], part[:, k % 2, c * P:(c + 1) * P], w[:, c, :],
                                    start=(n == 0), stop=(n == 3 * KC - 1))
                    n += 1
            mm.then_inc(z2_mm, 1)

        def window_products(s, k):
            for c in range(KC):
                mm = eng.matmul(pg[:, k % 2, c * WN:(c + 1) * WN], U2[:, s, k * D + c * P:k * D + (c + 1) * P],
                                one[:, s, k, :], start=True, stop=True)
            return mm

        def sum_products(i, d, k):
            if k == 0:
                eng.wait_ge(msg, grp(i, d) + 1)
            t = tile(i, d, k)
            if not general:
                eng.wait_ge(one_at, t + 1)
                eng.wait_ge(sum_at, t + 1)
                window_products(d % 2, k).then_inc(sum_mm, 1)
            else:
                carry()
                with eng.Fori(0, WINDOWS, 1) as w:
                    eng.wait_ge(g_one, t * WINDOWS + w + 1)
                    window_products(d % 2, k).then_inc(g_mm, 1)

        def step(i, d, j):
            if there(j, -2):
                sum_products(i, d - 2, 0)
                sum_products(i, d - 2, 1)
                sum_products(i, d - 2, 2)
            if there(j, 1):
                transposes(i, d + 1, 0)
            if there(j, 0):
                hidden_products(i, d, 2)
            if there(j, 3):
                edge_products(i, d + 3, 0)
            if there(j, 1):
                transposes(i, d + 1, 1)
            if there(j, -2):
                sum_products(i, d - 2, 3)
            if there(j, 3):
                edge_products(i, d + 3, 1)
            if there(j, 0):
                hidden_products(i, d, 3)
            if there(j, 3):
                edge_products(i, d + 3, 2)
            if there(j, 1):
                transposes(i, d + 1, 2)
            if there(j, 3):
                edge_products(i, d + 3, 3)
            if there(j, 1):
                hidden_products(i, d + 1, 0)
                hidden_products(i, d + 1, 1)
                transposes(i, d + 1, 3)

        eng.wait_ge(w_split, 7)
        steps(eng, step, -3, GROUPS + 1)

    def act_program(eng, general):
        def act(func, u, d, source=None, bias=0.0):
            return eng.activation(u[:, d % 2, :], (u if source is None else source)[:, d % 2, :], func,
                                  bias=bias)

        def exp_1(i, d):
            eng.wait_ge(z1_at, tile(i, d, TG))
            wait(eng, t_mm, tile(i, d - 1, 0))
            act(ACT.Exp, U1, d, X).then_inc(exp1, 1)

        def exp_2(i, d):
            eng.wait_ge(z2_at, tile(i, d, TG))
            wait(eng, sum_mm, tile(i, d - 1, 0))
            act(ACT.Exp, U2, d, X2).then_inc(exp2, 1)

        def ln(u, i, d, cut, done):
            eng.wait_ge(cut, grp(i, d) + 1)
            act(ACT.Ln, u, d, bias=1.0).then_inc(done, 1)

        def tanh(u, i, d, ln, done):
            eng.wait_ge(ln, grp(i, d) + 1)
            act(ACT.Tanh, u, d).then_inc(done, 1)

        def hi_part(i, d, k):
            t = tile(i, d, k)
            eng.wait_ge(t_mm, t + 1)
            wait(eng, z2_mm, t - 1)
            eng.activation(h_hi[:, k % 2, :], pt[:, k % 2, :], ACT.Copy).then_inc(hi_at, 1)

        def step(i, d, j):
            if there(j, 1):
                tanh(U1, i, d + 1, ln1, tanh1)
            if there(j, -1):
                exp_2(i, d - 1)
            if there(j, 0):
                hi_part(i, d, 2)
            if there(j, 2):
                exp_1(i, d + 2)
            if there(j, 0):
                hi_part(i, d, 3)
            if there(j, -1):
                ln(U2, i, d - 1, cut2, ln2)
            if there(j, 1):
                hi_part(i, d + 1, 0)
            if there(j, 2):
                ln(U1, i, d + 2, cut1, ln1)
            if there(j, -1):
                tanh(U2, i, d - 1, ln2, tanh2)
            if there(j, 1):
                hi_part(i, d + 1, 1)

        steps(eng, step, -2, GROUPS)

    def dve_program(eng, general):
        starts = [eng.alloc_register(f"l1_start{general}{k}") for k in range(TG)]

        def window_rows(i, d):
            s = d % 2
            eng.wait_ge(ea_in[s], count(i, d, 48))
            wait(eng, z1_mm, tile(i, d - 1, 0))
            hot = slice(BR, BR + 2 * WN)
            for k in range(TG):
                cols = slice(k * P, (k + 1) * P)
                op = eng.tensor_scalar(ea_n[hot, s, cols], dst_b[hot, s, cols],
                                       win_node[hot, bass.ds(tile(i, d, k), 1)], None,
                                       ALU.is_equal)
            op.then_inc(hot_at, 1)

        def preactivation(i, d, k):
            if k == 0 and general:
                eng.wait_ge(x_at, grp(i, d) + 1)
            if k == 0 and not general:
                eng.wait_ge(a_in[d % 2], count(i, d, 64))
            eng.wait_ge(z1_mm, tile(i, d, k) + 1)
            own = X[:, d % 2, k * D:(k + 1) * D]
            eng.tensor_tensor(own, own, pz1[:, k % 2, :], ALU.add).then_inc(z1_at, 1)

        def cut(u, i, d, exp, done):
            eng.wait_ge(exp, grp(i, d) + 1)
            eng.tensor_scalar(u[:, d % 2, :], u[:, d % 2, :], U_MAX, None, ALU.min).then_inc(done, 1)

        def times(u, z, i, d, tanh, done):
            eng.wait_ge(tanh, grp(i, d) + 1)
            eng.tensor_tensor(u[:, d % 2, :], u[:, d % 2, :], z[:, d % 2, :], ALU.mult)\
                .then_inc(done, 1)

        def lo_part(i, d, k):
            eng.wait_ge(hi_at, tile(i, d, k) + 1)
            eng.tensor_tensor(h_lo[:, k % 2, :], pt[:, k % 2, :], h_hi[:, k % 2, :].bitcast(F32),
                              ALU.subtract).then_inc(lo_at, 1)

        def second_preactivation(i, d, k):
            t = tile(i, d, k)
            if k == 0:
                wait(eng, msg, grp(i, d - 1))
            eng.wait_ge(z2_mm, t + 1)
            eng.tensor_tensor(X2[:, d % 2, k * D:(k + 1) * D], pz2[:, k % 2, :], b2b[:, :], ALU.add)\
                .then_inc(z2_at, 1)

        def one_hots(i, d):
            if general:
                return
            wait(eng, sum_mm, tile(i, d - 1, 0))
            for k in range(TG):
                t = tile(i, d, k)
                eng.tensor_scalar(one[:, d % 2, k, :], iota[:, :], dst_rel[:, bass.ds(t, 1)],
                                  None, ALU.is_equal).then_inc(one_at, 1)

        def add_window(k, base):
            window = aggt[:, :, bass.ds(base, WN)]
            return eng.tensor_tensor(window, window,
                                     pg[:, k % 2, 0:KC * WN].rearrange("p (c n) -> p c n", c=KC),
                                     ALU.add)

        def sum_up(i, d, k):
            t = tile(i, d, k)
            s = d % 2
            if not general:
                eng.wait_ge(sum_mm, t + 1)
                eng.wait_ge(sum_at, 2 + t)
                start = eng.snap(starts[k], min_val=0, max_val=N - 1)
                add_window(k, start).then_inc(sum_at, 1)
            else:
                eng.wait_ge(g_at, t * WINDOWS + 1)
                eng.tensor_copy(node[:, :], dst_idx[:, bass.ds(t, 1)]).then_inc(g_node, 1)
                with eng.Fori(0, WINDOWS, 1) as w:
                    n = t * WINDOWS + w
                    eng.wait_ge(g_node, n + t + 1)
                    eng.tensor_scalar(one[:, s, k, :], iota[:, :], node[:, :], None,
                                      ALU.is_equal).then_inc(g_one, 1)
                    eng.wait_ge(g_one, n + 1)
                    eng.tensor_scalar(node[:, :], node[:, :], -float(WN), None, ALU.add)\
                        .then_inc(g_node, 1)
                    eng.wait_ge(g_mm, n + 1)
                    add_window(k, w * WN).then_inc(g_at, 1)
                eng.sem_inc(sum_mm, 1)

        def step(i, d, j):
            if there(j, -2) and not general:
                eng.reg_load(starts, dst_row[0:1, bass.ds(tile(i, d - 2, 0), TG)])
            if there(j, -1):
                second_preactivation(i, d - 1, 2)
            if there(j, -2):
                one_hots(i, d - 2)
            if there(j, 2):
                preactivation(i, d + 2, 0)
            if there(j, 3):
                window_rows(i, d + 3)
            if there(j, 2):
                preactivation(i, d + 2, 1)
            if there(j, -1):
                second_preactivation(i, d - 1, 3)
            if there(j, 2):
                preactivation(i, d + 2, 2)
                preactivation(i, d + 2, 3)
            if there(j, 0):
                lo_part(i, d, 1)
            if there(j, -2):
                times(U2, X2, i, d - 2, tanh2, msg)
            if there(j, 1):
                times(U1, X, i, d + 1, tanh1, hid)
            if there(j, -2):
                sum_up(i, d - 2, 0)
            if there(j, 0):
                lo_part(i, d, 2)
                second_preactivation(i, d, 0)
            if there(j, -1):
                cut(U2, i, d - 1, exp2, cut2)
            if there(j, -2):
                sum_up(i, d - 2, 1)
            if there(j, 0):
                lo_part(i, d, 3)
            if there(j, 2):
                cut(U1, i, d + 2, exp1, cut1)
            if there(j, 0):
                second_preactivation(i, d, 1)
            if there(j, -2):
                sum_up(i, d - 2, 2)
            if there(j, 1):
                lo_part(i, d + 1, 0)
            if there(j, -2):
                sum_up(i, d - 2, 3)

        eng.memset(aggt[:, :, :].rearrange("p c n -> p (c n)"), 0.0)\
            .then_inc(g_at if general else sum_at, 1 if general else 2)
        eng.wait_ge(w_in, 64)
        raw2 = U2[:, 0, :].rearrange("p (c n) -> p c n", c=KC)
        rawc = U2[:, 1, 0:D]
        eng.tensor_copy(w2_hi[:, :, :], raw2).then_inc(w_split, 1)
        eng.tensor_copy(wc_hi[:, :], rawc).then_inc(w_split, 1)
        eng.wait_ge(w_split, 2)
        eng.tensor_tensor(w2_lo[:, :, :], raw2, w2_hi[:, :, :].bitcast(F32), ALU.subtract)\
            .then_inc(w_split, 2)
        for k in range(TG):
            low = eng.tensor_tensor(wx[0:ED, k, :], rawc[0:ED, :], wc_hi[0:ED, :].bitcast(F32),
                                    ALU.subtract)
        low.then_inc(w_split, 3)
        steps(eng, step, -4, GROUPS + 1)

    def pool_program(eng, general):
        carry = carrier(eng, pool_turns)
        xb_rows = xb_parts.rearrange("n h f -> n (h f)")

        def rows_of_edges(i, d):
            s = d % 2
            if d >= 2:
                eng.wait_ge(a_in[s], count(i, d - 2, 64))
            eng.tensor_copy(idx_a[:, s, :], src_idx[:, bass.ds(tile(i, d, 0), TG)]).then_inc(ia_at, 1)
            eng.wait_ge(ia_at, grp(i, d) + 1)
            wait(eng, hid, grp(i, d) - 1)
            carry()
            for k in range(TG):
                eng.indirect_dma_start(X[:, s, k * D:(k + 1) * D], None, xa_rows,
                                       bass.IndirectOffsetOnAxis(ap=idx_a[:, s, k:k + 1], axis=0))\
                    .then_inc(a_in[s], 16)
            if general:
                add_rows_of_nodes(i, d)

        def add_rows_of_nodes(i, d):
            s = d % 2
            eng.wait_ge(a_in[s], count(i, d, 64))
            for k in range(TG):
                t = tile(i, d, k)
                eng.tensor_copy(idx_b[:, :], dst_row[:, bass.ds(t, 1)]).then_inc(ib_at, 1)
                eng.wait_ge(ib_at, t + 1)
                carry()
                eng.indirect_dma_start(XB[:, :, :].rearrange("p h f -> p (h f)"), None, xb_rows,
                                       bass.IndirectOffsetOnAxis(ap=idx_b[:, :], axis=0))\
                    .then_inc(b_in, 16)
                eng.wait_ge(b_in, 16 * t + 16)
                own = X[:, s, k * D:(k + 1) * D]
                for h in range(2):
                    eng.tensor_tensor(own, own, XB[:, h, :], ALU.add).then_inc(xb_at, 1)
                    eng.wait_ge(xb_at, 2 * t + h + 1)
            eng.sem_inc(x_at, 1)

        def left_sides(i, d):
            s = d % 2
            eng.wait_ge(ea_in[s], count(i, d, 48))
            wait(eng, z1_mm, tile(i, d - 1, 0))
            carry()
            eng.tensor_copy(ea_hl[:, s, :], ea[:, s, :]).then_inc(ea_at, 1)
            eng.tensor_copy(ea_n[0:ED, s, :], ea[0:ED, s, :]).then_inc(ea_at, 1)
            eng.wait_ge(ea_at, 3 * grp(i, d) + 2)
            eng.tensor_tensor(ea_hl[0:ED, s, :], ea[0:ED, s, :], ea_n[0:ED, s, :].bitcast(F32),
                              ALU.subtract).then_inc(ea_at, 1)

        def step(i, d):
            rows_of_edges(i, d)
            left_sides(i, d + 1)

        left_sides(0, 0)
        for d in range(3):
            step(0, d)
        with eng.Fori(0, (GROUPS - 4) // 2, 1) as i:
            step(i, 3)
            step(i, 4)
        rows_of_edges(0, GROUPS - 1)

    def branch(eng, program):
        general = eng.value_load(wide[0:1, 0:1], min_val=0, max_val=1)
        with eng.If(general == 0):
            program(eng, 0)
        with eng.Else():
            program(eng, 1)

    with nc.Block() as block:
        @block.sync
        def _(eng):
            eng.dma_start(U2[:, 0, :].rearrange("p (c n) -> p c n", c=KC),
                          w2.rearrange("(c p) n -> p c n", p=P)).then_inc(w_in, 16)
            eng.dma_start(b2b[:, :], b2.partition_broadcast(P)).then_inc(w_in, 16)
            for half in range(2):
                eng.dma_start(U2[half * ED:(half + 1) * ED, 1, 0:D], w1[2 * D:2 * D + ED, :])\
                    .then_inc(w_in, 16)

            starts = [eng.alloc_register(f"wx_start{k}") for k in range(TG)]

            def attributes(i, d):
                s = d % 2
                wait(eng, ea_at, 3 * grp(i, d - 1))
                wait(eng, hot_at, grp(i, d - 1))
                cols = bass.ds(tile(i, d, 0) * P, TG * P)
                for half in range(2):
                    eng.dma_start(ea[half * ED:(half + 1) * ED, s, :], edge_attr[:, cols])\
                        .then_inc(ea_in[s], 16)
                eng.dma_start(dst_b[BR:BR + 2 * WN, s, :], dst_e[cols].partition_broadcast(2 * WN))\
                    .then_inc(ea_in[s], 16)

            def windows(i, d):
                eng.reg_load(starts, dst_row[0:1, bass.ds(tile(i, d, 0), TG)])
                for k in range(TG):
                    wait(eng, z1_mm, tile(i, d - 1, k) + 1)
                    start = eng.snap(starts[k], min_val=0, max_val=N - 1)
                    eng.dma_start(wx[BR:BR + 2 * WN, k, :].bitcast(F32),
                                  xb_parts[bass.ds(start, WN), :, :].rearrange("n h f -> (n h) f"))\
                        .then_inc(wx_in[k], 16)

            attributes(0, 0)
            attributes(0, 1)
            for d in range(2):
                windows(0, d)
            with eng.Fori(0, GROUPS // 2 - 1, 1) as i:
                for d in (2, 3):
                    attributes(i, d)
                    windows(i, d)

        @block.gpsimd
        def _(eng):
            branch(eng, pool_program)

        @block.tensor
        def _(eng):
            branch(eng, pe_program)

        @block.scalar
        def _(eng):
            act_program(eng, 0)

        @block.vector
        def _(eng):
            branch(eng, dve_program)


def node_mlp(nc, st, sbuf, psum, sem, x1, h1, h1t, aggt, ident, w3, b3, w4, b4, gamma, beta, out_v):
    w3s = sbuf(st, "w3s", [P, 2 * KC, D])
    w4s = sbuf(st, "w4s", [P, KC, D])
    rows = sbuf(st, "rows5", [NP, 4, D])
    Z = sbuf(st, "Z", [NP, 2, D])
    U = sbuf(st, "U", [NP, 2, D])
    ut = sbuf(st, "ut", [P, 2, D])
    stats = sbuf(st, "stats2", [NP, NT, 6])
    mv = sbuf(st, "mv2", [NP, NT, 2])
    std = sbuf(st, "std2", [NP, NT])
    rstd = sbuf(st, "rstd2", [NP, NT])
    eps = sbuf(st, "eps2", [NP, 1])
    p3 = psum(st, "p3", [P, 2, D])
    pt = psum(st, "pt3", [P, 2, D])
    p4 = psum(st, "p4", [P, 2, D])
    w_in = sem(st, "w34_in")
    eps_at = sem(st, "eps2_at")
    mm3 = sem(st, "mm3")
    z_at = sem(st, "z_at")
    e_at = sem(st, "e_at")
    cut = sem(st, "cut")
    l_at = sem(st, "l_at")
    t_at = sem(st, "t_at")
    u_at = sem(st, "u_at")
    tp = sem(st, "tp3")
    ut_at = sem(st, "ut_at")
    mm4 = sem(st, "mm4")
    y_a = sem(st, "y_a")
    y_at = sem(st, "y_at")
    stat = sem(st, "stat2")
    std_at = sem(st, "std2_at")
    r_at = sem(st, "r_at")
    f1 = sem(st, "f1")
    f2 = sem(st, "f2")
    f3 = sem(st, "f3")
    f4 = sem(st, "f4")
    stored = sem(st, "stored")
    with nc.Block() as block:
        @block.sync
        def _(eng):
            eng.dma_start(w3s[:, :, :], w3.rearrange("(c p) n -> p c n", p=P)).then_inc(w_in, 16)
            eng.dma_start(w4s[:, :, :], w4.rearrange("(c p) n -> p c n", p=P)).then_inc(w_in, 16)
            for n, v in enumerate((b3, b4, gamma, beta)):
                eng.dma_start(rows[:, n, :], v.partition_broadcast(NP)).then_inc(w_in, 16)
            for t in range(NT):
                eng.wait_ge(f4, t + 1)
                eng.dma_start(out_v[:, t, :], x1[:, t, :]).then_inc(stored, 16)
            eng.wait_ge(stored, 16 * NT)

        @block.tensor
        def _(eng):
            eng.wait_ge(w_in, 96)

            def first(t):
                wait(eng, z_at, t - 1)
                for c in range(2 * KC):
                    lhs = (h1t if c < KC else aggt)[:, c % KC, t * NP:(t + 1) * NP]
                    mm = eng.matmul(p3[0:NP, t % 2, :], lhs, w3s[:, c, :], start=(c == 0),
                                    stop=(c == 2 * KC - 1))
                mm.then_inc(mm3, 1)

            def second(t):
                eng.wait_ge(u_at, t + 1)
                wait(eng, ut_at, t - 1)
                for c in range(KC):
                    mm = eng.transpose(pt[:, t % 2, c * P:c * P + NP],
                                       U[:, t % 2, c * P:(c + 1) * P], ident[0:NP, 0:NP])
                mm.then_inc(tp, 1)
                eng.wait_ge(ut_at, t + 1)
                wait(eng, y_a, t - 1)
                for c in range(KC):
                    mm = eng.matmul(p4[0:NP, t % 2, :], ut[:, t % 2, c * P:c * P + NP], w4s[:, c, :],
                                    start=(c == 0), stop=(c == KC - 1))
                mm.then_inc(mm4, 1)

            first(0)
            for t in range(NT):
                if t + 1 < NT:
                    first(t + 1)
                second(t)

        @block.scalar
        def _(eng):
            for t in range(NT):
                s = t % 2
                eng.wait_ge(z_at, t + 1)
                wait(eng, tp, t - 1)
                eng.activation(U[:, s, :], Z[:, s, :], ACT.Exp).then_inc(e_at, 1)
                eng.wait_ge(cut, t + 1)
                eng.activation(U[:, s, :], U[:, s, :], ACT.Ln, bias=1.0).then_inc(l_at, 1)
                eng.wait_ge(l_at, t + 1)
                eng.activation(U[:, s, :], U[:, s, :], ACT.Tanh).then_inc(t_at, 1)
                eng.wait_ge(tp, t + 1)
                wait(eng, mm4, t - 1)
                view = "p (c n) -> p c n"
                eng.activation(ut[:, s, :].rearrange(view, c=KC)[:, :, 0:NP],
                               pt[:, s, :].rearrange(view, c=KC)[:, :, 0:NP], ACT.Copy)\
                    .then_inc(ut_at, 1)
            eng.wait_ge(stat, 2 * NT)
            eng.wait_ge(eps_at, 1)
            eng.activation(std[:, :], mv[:, :, 1:2].squeeze(2), ACT.Sqrt, bias=eps[:, :])\
                .then_inc(std_at, 1)

        @block.vector
        def _(eng):
            eng.memset(eps[:, :], EPS).then_inc(eps_at, 1)
            eng.wait_ge(w_in, 96)

            def z_part(t):
                s = t % 2
                eng.wait_ge(mm3, t + 1)
                wait(eng, u_at, t - 1)
                eng.tensor_tensor(Z[:, s, :], p3[0:NP, s, :], rows[:, 0, :], ALU.add)\
                    .then_inc(z_at, 1)
                eng.wait_ge(e_at, t + 1)
                eng.tensor_scalar(U[:, s, :], U[:, s, :], U_MAX, None, ALU.min).then_inc(cut, 1)

            def y_part(t):
                eng.wait_ge(mm4, t + 1)
                eng.tensor_tensor(h1[:, t, :], h1[:, t, :], p4[0:NP, t % 2, :], ALU.add)\
                    .then_inc(y_a, 1)
                eng.wait_ge(y_a, t + 1)
                eng.tensor_tensor(h1[:, t, :], h1[:, t, :], rows[:, 1, :], ALU.add)\
                    .then_inc(y_at, 1)
                eng.wait_ge(y_at, t + 1)
                eng.bn_stats(stats[:, t, :], h1[:, t, :]).then_inc(stat, 1)

            for t in range(NT):
                z_part(t)
                if t > 0:
                    y_part(t - 1)
                eng.wait_ge(t_at, t + 1)
                eng.tensor_tensor(U[:, t % 2, :], U[:, t % 2, :], Z[:, t % 2, :], ALU.mult)\
                    .then_inc(u_at, 1)
            y_part(NT - 1)
            for t in range(NT):
                eng.wait_ge(stat, t + 1)
                eng.bn_aggr(mv[:, t, :], stats[:, t, :]).then_inc(stat, 1)
            eng.wait_ge(std_at, 1)
            eng.reciprocal(rstd[:, :], std[:, :]).then_inc(r_at, 1)
            eng.wait_ge(r_at, 1)
            for t in range(NT):
                eng.tensor_scalar(h1[:, t, :], h1[:, t, :], mv[:, t, 0:1], rstd[:, t:t + 1],
                                  ALU.subtract, ALU.mult).then_inc(f1, 1)
                eng.wait_ge(f1, t + 1)
                eng.tensor_tensor(h1[:, t, :], h1[:, t, :], rows[:, 2, :], ALU.mult).then_inc(f2, 1)
                eng.tensor_tensor(x1[:, t, :], x1[:, t, :], rows[:, 3, :], ALU.add).then_inc(f3, 1)
                eng.wait_ge(f2, t + 1)
                eng.wait_ge(f3, t + 1)
                eng.tensor_tensor(x1[:, t, :], x1[:, t, :], h1[:, t, :], ALU.add).then_inc(f4, 1)


def kernel(x, src, dst, edge_attr_64, edge_type_32, edge_weight1, L0_gnn_bases, L0_gnn_w_comp,
           L0_gnn_h_bias, L1_gnn_W1, L1_gnn_b1, L1_gnn_W2, L1_gnn_b2, L1_gnn_W3, L1_gnn_b3,
           L1_gnn_W4, L1_gnn_b4, L1_gnn_gamma, L1_gnn_beta):
    import numpy as np
    import concourse.bacc as bacc
    from concourse.bass_utils import run_bass_kernel_spmd

    def padded(a, fill):
        a = np.asarray(a).reshape(E)
        return np.concatenate([a, np.full(EPAD - E, fill, a.dtype)])

    def by_tile(a, fill):
        return np.ascontiguousarray(padded(a, fill).reshape(T, P).T)

    attr = np.zeros((ED, EPAD), np.asarray(edge_attr_64).dtype)
    attr[:, :E] = np.asarray(edge_attr_64).T
    given = {
        "x": x, "src_t": by_tile(src, 0), "dst_t": by_tile(dst, -1), "dst_e": padded(dst, -1), "etype": padded(edge_type_32, 0),
        "norm_t": by_tile(edge_weight1, 0), "edge_attr": attr, "bases": L0_gnn_bases,
        "w_comp": L0_gnn_w_comp, "h_bias": L0_gnn_h_bias, "w1": L1_gnn_W1, "b1": L1_gnn_b1,
        "w2": L1_gnn_W2, "b2": L1_gnn_b2, "w3": L1_gnn_W3, "b3": L1_gnn_b3, "w4": L1_gnn_W4,
        "b4": L1_gnn_b4, "gamma": L1_gnn_gamma, "beta": L1_gnn_beta,
    }
    nc = bacc.Bacc("TRN2", target_bir_lowering=False, num_devices=1)
    arrays, args = {}, []
    for name, a in given.items():
        a = np.ascontiguousarray(a)
        arrays[f"in_{name}"] = a
        args.append(nc.dram_tensor(f"in_{name}", a.shape, mybir.dt.from_np(a.dtype),
                                   kind="ExternalInput").ap())
    args.append(nc.dram_tensor("out_0", (N, D), F32, kind="ExternalOutput").ap())
    gnn_kernel(nc, *args)
    r = run_bass_kernel_spmd(nc, [arrays], core_ids=[0])
    return r.results[0]["out_0"]
```

```python
from contextlib import ExitStack

import concourse.bass as bass
from concourse import mybir

F32 = mybir.dt.float32
F32R = mybir.dt.float32r
I32 = mybir.dt.int32
ALU = mybir.AluOpType
ACT = mybir.ActivationFunctionType
AX_X = mybir.AxisListType.X

P = 128
N = 1250
E = 21250
D = 512
KC = D // P
ED = 64
R = 32
NB = 8
NP = 125
NT = N // NP
TG = 4
GROUPS = -(-E // (P * TG * 2)) * 2
T = GROUPS * TG
EPAD = T * P
FULL = E // P
REST = E - FULL * P
WN = 16
WINDOWS = -(-N // WN)
NPAD = N + WN
BR = ED
ROWS = 8
BANKS = 8
QT = P // R
TQ = T // QT
TCH = 21
CHUNKS = TQ // TCH
HALF = 512 // (QT * NB)
U_MAX = 1e18
EPS = 1e-5


def wait(eng, sem, value):
    if not (isinstance(value, int) and value <= 0):
        eng.wait_ge(sem, value)


def carrier(eng, turns):
    return lambda: eng.sem_inc(turns, 1)


def gnn_kernel(nc, x, src_t, dst_t, dst_e, etype, norm_t, edge_attr, bases, w_comp, h_bias, w1, b1,
               w2, b2, w3, b3, w4, b4, gamma, beta, out):
    h0_rows = nc.dram_tensor("h0_rows", [N, D], F32, kind="Internal").ap()
    xa_rows = nc.dram_tensor("xa_rows", [N, D], F32, kind="Internal").ap()
    xb_parts = nc.dram_tensor("xb_parts", [NPAD, 2, D], F32, kind="Internal").ap()
    by_tile = "(t p) f -> p t f"
    x_v = x.rearrange(by_tile, p=NP)
    out_v = out.rearrange(by_tile, p=NP)
    h0_v = h0_rows.rearrange(by_tile, p=NP)
    xa_v = xa_rows.rearrange(by_tile, p=NP)
    xb_v = xb_parts[0:N, :, :].rearrange("(t p) h f -> p t h f", p=NP)

    with ExitStack() as whole:
        def sbuf(stack, name, shape, dt=F32):
            return stack.enter_context(nc.sbuf_tensor(name, shape, dt))

        def psum(stack, name, shape):
            return stack.enter_context(nc.psum_tensor(name, shape, F32))

        def sem(stack, name):
            return stack.enter_context(nc.semaphore(name))

        src_idx = sbuf(whole, "src_idx", [P, T], I32)
        dst_idx = sbuf(whole, "dst_idx", [P, T], I32)
        dst_row = sbuf(whole, "dst_row", [P, T], I32)
        dst_rel = sbuf(whole, "dst_rel", [P, T + ROWS])
        wide = sbuf(whole, "wide", [1, 1], I32)
        win_node = sbuf(whole, "win_node", [P, T])
        iota = sbuf(whole, "iota", [P, WN])
        ident = sbuf(whole, "ident", [P, P])
        x1 = sbuf(whole, "x1", [NP, NT, D])

        layer0 = whole.enter_context(ExitStack())
        coef = sbuf(layer0, "coef", [P, T + ROWS, NB])
        with ExitStack() as st:
            norm_sb = sbuf(st, "norm_sb", [P, T])
            wc = sbuf(st, "wc", [P, QT, NB])
            etype_b = sbuf(st, "etype_b", [P, CHUNKS, TCH * P], I32)
            type_hot = sbuf(st, "type_hot", [P, CHUNKS, TCH * P])
            rel_id_i = sbuf(st, "rel_id_i", [P, 1], I32)
            rel_id = sbuf(st, "rel_id", [P, 1])
            half_i = sbuf(st, "half_i", [P, 1], I32)
            half_f = sbuf(st, "half_f", [P, 1])
            ones = sbuf(st, "ones", [1, P])
            base_f = sbuf(st, "base_f", [1, T])
            off = sbuf(st, "off", [P, T])
            far = sbuf(st, "far", [P, 2])
            far1 = sbuf(st, "far1", [P, 1])
            wide_f = sbuf(st, "wide_f", [1, 2])
            stats = sbuf(st, "stats", [NP, NT, 6])
            mv = sbuf(st, "mv", [NP, NT, 2])
            std = sbuf(st, "std", [NP, NT])
            rstd = sbuf(st, "rstd", [NP, NT])
            eps = sbuf(st, "eps", [NP, 1])
            h0 = sbuf(st, "h0", [NP, NT, D])
            base_ps = psum(st, "base_ps", [P, 512])
            far_ps = psum(st, "far_ps", [P, 512])
            coef_ps = psum(st, "coef_ps", [P, CHUNKS, 2, 512])

            idx_in = sem(st, "idx_in")
            x_in = sem(st, "x_in")
            type_in = [sem(st, f"type_in{i}") for i in range(CHUNKS)]
            made = sem(st, "made")
            pads = sem(st, "pads")
            consts = sem(st, "consts")
            base_done = sem(st, "base_done")
            base_at = sem(st, "base_at")
            check = sem(st, "check")
            far_t = sem(st, "far_t")
            flag_at = sem(st, "flag_at")
            hot = sem(st, "hot")
            coef_mm = sem(st, "coef_mm")
            wc_in = sem(st, "wc_in")
            stat = sem(st, "stat")
            std_at = sem(st, "std_at")
            norm_at = sem(st, "norm_at")
            h_at = sem(st, "h_at")
            h_out = sem(st, "h_out")
            with nc.Block() as block:
                @block.sync
                def _(eng):
                    eng.dma_start(dst_idx[:, :], dst_t).then_inc(idx_in, 16)
                    eng.dma_start(x1[:, :, :], x_v).then_inc(x_in, 16)
                    eng.dma_start(src_idx[:, :], src_t).then_inc(idx_in, 16)
                    eng.dma_start(norm_sb[:, :], norm_t).then_inc(idx_in, 16)
                    types = etype.rearrange("(c j q e) -> c q j e", c=CHUNKS, q=QT, e=P)
                    for c in range(CHUNKS):
                        for q in range(QT):
                            rows = etype_b[q * R:(q + 1) * R, c, :].rearrange("p (j e) -> p j e", e=P)
                            eng.dma_start(rows, types[c, q].partition_broadcast(R))\
                                .then_inc(type_in[c], 16)
                    for t in range(0, NT, 2):
                        eng.wait_ge(h_at, t + 2)
                        eng.dma_start(h0_v[:, t:t + 2, :], h0[:, t:t + 2, :]).then_inc(h_out, 16)
                    eng.wait_ge(h_out, 16 * (NT // 2))

                @block.gpsimd
                def _(eng):
                    eng.memset(ident[:, :], 0.0).then_inc(made, 1)
                    eng.wait_ge(made, 1)
                    eng.affine_select(out=ident[:, :], in_=ident[:, :], compare_op=ALU.not_equal,
                                      fill=1.0, base=0, pattern=[[-1, P]], channel_multiplier=1)\
                        .then_inc(made, 1)
                    eng.iota(iota[:, :], [[1, WN]], base=0, channel_multiplier=0,
                             allow_small_or_imprecise_dtypes=True).then_inc(made, 1)
                    eng.iota(rel_id_i[:, :], [[0, 1]], base=0, channel_multiplier=1).then_inc(made, 1)
                    eng.iota(half_i[:, :], [[0, 1]], base=0, channel_multiplier=1).then_inc(made, 1)

                @block.vector
                def _(eng):
                    eng.memset(ones[:, :], 1.0).then_inc(consts, 1)
                    eng.memset(dst_rel[:, T:T + ROWS], -1.0).then_inc(consts, 1)
                    eng.memset(coef[:, T:T + ROWS, :], 0.0).then_inc(consts, 1)
                    eng.memset(far[:, :], 0.0).then_inc(consts, 1)
                    eng.memset(eps[:, :], EPS).then_inc(consts, 1)
                    eng.memset(wc[:, :, :], 0.0).then_inc(consts, 1)
                    eng.wait_ge(idx_in, 48)
                    eng.tensor_scalar(dst_row[:, :], dst_idx[:, :], 0.0, None, ALU.max)\
                        .then_inc(base_done, 1)
                    eng.wait_ge(base_done, 1)
                    eng.tensor_copy(base_f[:, :], dst_row[0:1, :]).then_inc(base_done, 1)
                    eng.wait_ge(made, 5)
                    eng.tensor_scalar(rel_id_i[:, :], rel_id_i[:, :], R - 1, None, ALU.bitwise_and)\
                        .then_inc(base_done, 1)
                    eng.wait_ge(base_done, 3)
                    eng.tensor_copy(rel_id[:, :], rel_id_i[:, :]).then_inc(base_done, 1)
                    eng.tensor_scalar(half_i[:, :], half_i[:, :], 1, None, ALU.logical_shift_right)\
                        .then_inc(base_done, 1)
                    eng.wait_ge(base_done, 5)
                    eng.tensor_copy(half_f[:, :], half_i[:, :]).then_inc(base_done, 1)
                    eng.wait_ge(x_in, 16)
                    for t in range(NT):
                        eng.bn_stats(stats[:, t, :], x1[:, t, :]).then_inc(stat, 1)
                    for t in range(NT):
                        eng.wait_ge(stat, t + 1)
                        eng.bn_aggr(mv[:, t, :], stats[:, t, :]).then_inc(stat, 1)
                    eng.wait_ge(base_at, 1)
                    eng.tensor_tensor(dst_rel[:, 0:T], dst_idx[:, :], base_ps[:, 0:T], ALU.subtract)\
                        .then_inc(check, 1)
                    eng.wait_ge(base_done, 6)
                    eng.tensor_scalar(win_node[BR:BR + 2 * WN, :], base_ps[BR:BR + 2 * WN, 0:T],
                                      half_f[BR:BR + 2 * WN, :], -BR / 2, ALU.add, ALU.add)\
                        .then_inc(base_done, 1)
                    eng.wait_ge(check, 1)
                    eng.tensor_scalar(off[:, :], dst_rel[:, 0:T], -(WN - 1) / 2, None, ALU.add)\
                        .then_inc(check, 1)
                    eng.wait_ge(check, 2)
                    eng.tensor_tensor(off[:, :], off[:, :], off[:, :], ALU.mult).then_inc(check, 1)
                    eng.wait_ge(check, 3)
                    eng.wait_ge(consts, 5)
                    eng.reduce_max(far[:, 0:1], off[:, 0:FULL], axis=AX_X).then_inc(check, 1)
                    if REST:
                        eng.reduce_max(far[0:REST, 1:2], off[0:REST, FULL:FULL + 1], axis=AX_X)\
                            .then_inc(check, 1)
                    eng.wait_ge(check, 4 + (REST > 0))
                    eng.reduce_max(far1[:, :], far[:, :], axis=AX_X).then_inc(check, 1)
                    eng.wait_ge(far_t, 1)
                    eng.reduce_max(wide_f[:, 0:1], far_ps[0:1, 0:P], axis=AX_X).then_inc(flag_at, 1)
                    eng.wait_ge(flag_at, 1)
                    eng.tensor_scalar(wide[:, :], wide_f[:, 0:1], (WN / 2) ** 2, None, ALU.is_ge)\
                        .then_inc(flag_at, 1)
                    for c in range(CHUNKS):
                        eng.wait_ge(type_in[c], 16 * QT)
                        eng.tensor_scalar(type_hot[:, c, :], etype_b[:, c, :], rel_id[:, :], None,
                                          ALU.is_equal).then_inc(hot, 1)
                    eng.wait_ge(std_at, 1)
                    eng.reciprocal(rstd[:, :], std[:, :]).then_inc(norm_at, 1)
                    eng.wait_ge(norm_at, 1)
                    for t in range(NT):
                        eng.tensor_scalar(h0[:, t, :], x1[:, t, :], mv[:, t, 0:1], rstd[:, t:t + 1],
                                          ALU.subtract, ALU.mult).then_inc(norm_at, 1)
                    for t in range(NT):
                        eng.wait_ge(norm_at, 2 + t)
                        eng.tensor_scalar(h0[:, t, :], h0[:, t, :], 0.0, None, ALU.max)\
                            .then_inc(h_at, 1)
                    for c in range(CHUNKS):
                        for h in range(2):
                            g0, g1 = (0, HALF) if h == 0 else (HALF, TCH)
                            t0 = (c * TCH + g0) * QT
                            n = (g1 - g0) * QT
                            eng.wait_ge(coef_mm, 2 * c + h + 1)
                            eng.tensor_tensor(
                                coef[:, t0:t0 + n, :],
                                coef_ps[:, c, h, 0:n * NB].rearrange("p (t b) -> p t b", b=NB),
                                norm_sb[:, t0:t0 + n].unsqueeze(2).to_broadcast([P, n, NB]),
                                ALU.mult)

                @block.tensor
                def _(eng):
                    eng.wait_ge(base_done, 2)
                    eng.wait_ge(consts, 1)
                    eng.matmul(base_ps[:, 0:T], ones[:, :], base_f[:, :], start=True, stop=True)\
                        .then_inc(base_at, 1)
                    eng.wait_ge(check, 5 + (REST > 0))
                    eng.wait_ge(made, 2)
                    eng.transpose(far_ps[0:1, 0:P], far1[:, :], ident[:, :]).then_inc(far_t, 1)
                    eng.wait_ge(wc_in, 16 * QT)
                    for c in range(CHUNKS):
                        eng.wait_ge(hot, c + 1)
                        for g in range(TCH):
                            h, col = divmod(g, HALF)
                            mm = eng.matmul(coef_ps[:, c, h, col * QT * NB:(col + 1) * QT * NB],
                                            type_hot[:, c, g * P:(g + 1) * P],
                                            wc[:, :, :].rearrange("p q b -> p (q b)"),
                                            start=True, stop=True)
                            if g in (HALF - 1, TCH - 1):
                                mm.then_inc(coef_mm, 1)

                @block.scalar
                def _(eng):
                    eng.wait_ge(consts, 6)
                    for q in range(QT):
                        eng.dma_start(wc[q * R:(q + 1) * R, q, :], w_comp).then_inc(wc_in, 16)
                    eng.wait_ge(stat, 2 * NT)
                    eng.activation(std[:, :], mv[:, :, 1:2].squeeze(2), ACT.Sqrt, bias=eps[:, :])\
                        .then_inc(std_at, 1)

        with ExitStack() as st:
            G = sbuf(st, "G", [P, KC, NB, NPAD])
            with ExitStack() as st2:
                scatter_layer0(nc, st2, sbuf, psum, sem, G, h0_rows, src_idx, dst_idx, dst_row,
                               dst_rel, coef, iota, wide)
            with ExitStack() as st2:
                apply_bases(nc, st2, sbuf, psum, sem, G, bases, h_bias, x1, coef)
        layer0.close()

        with ExitStack() as st:
            h1 = sbuf(st, "h1", [NP, NT, D])
            h1t = sbuf(st, "h1t", [P, KC, N])
            aggt = sbuf(st, "aggt", [P, KC, NPAD])
            with ExitStack() as edge_st:
                w2_hi = sbuf(edge_st, "w2_hi", [P, KC, D], F32R)
                w2_lo = sbuf(edge_st, "w2_lo", [P, KC, D], F32R)
                wc_hi = sbuf(edge_st, "wc_hi", [P, D], F32R)
                wx = sbuf(edge_st, "wx", [P, TG, D], F32R)
                b2b = sbuf(edge_st, "b2b", [P, D])
                edge_weights = (w2_hi, w2_lo, wc_hi, wx, b2b)
                with ExitStack() as st2:
                    node_products(nc, st2, sbuf, psum, sem, x1, h1, h1t, aggt, edge_weights, ident,
                                  w1, b1, w2, b2, xa_v, xb_v, xb_parts)
                with ExitStack() as st2:
                    edge_mlp(nc, st2, sbuf, psum, sem, aggt, edge_weights, xa_rows, xb_parts,
                             edge_attr, src_idx, dst_idx, dst_e, dst_row, dst_rel, win_node, iota, ident, wide)
            with ExitStack() as st2:
                node_mlp(nc, st2, sbuf, psum, sem, x1, h1, h1t, aggt, ident, w3, b3, w4, b4, gamma,
                         beta, out_v)


def scatter_layer0(nc, st, sbuf, psum, sem, G, h0_rows, src_idx, dst_idx, dst_row, dst_rel, coef,
                   iota, wide):
    rows = sbuf(st, "rows", [P, ROWS, D])
    idx = sbuf(st, "l0_idx", [P, ROWS], I32)
    S = sbuf(st, "S", [P, ROWS, NB, WN])
    ps = psum(st, "l0_ps", [P, BANKS, KC * NB * WN])
    rows_in = [sem(st, f"rows_in{i}") for i in range(ROWS)]
    idx_at = sem(st, "l0_idx_at")
    s_at = sem(st, "s_at")
    mm_done = sem(st, "mm_done")
    added = sem(st, "added")
    w_s = sem(st, "w_s")
    w_mm = sem(st, "w_mm")
    w_add = sem(st, "w_add")
    w_node = sem(st, "w_node")
    pool_turns = sem(st, "l0_pool_turns")
    pe_turns = sem(st, "l0_pe_turns")
    zero = sbuf(st, "zero", [P, 1])
    zero_at = sem(st, "zero_at")
    g_zero = sem(st, "g_zero")
    node = sbuf(st, "l0_node", [P, 1])

    def gather(eng, i, q, rows_free, per_tile, carry):
        if q % TG == 0:
            half = slice(q, q + TG)
            for k in range(q, q + TG):
                wait(eng, rows_in[k], 16 * i)
            eng.tensor_copy(idx[:, half], src_idx[:, bass.ds(ROWS * i + q, TG)]).then_inc(idx_at, 1)
            eng.wait_ge(idx_at, 2 * i + q // TG + 1)
        eng.wait_ge(rows_free, (ROWS * i + q + 1) * per_tile)
        carry()
        eng.indirect_dma_start(rows[:, q, :], None, h0_rows,
                               bass.IndirectOffsetOnAxis(ap=idx[:, q:q + 1], axis=0))\
            .then_inc(rows_in[q], 16)

    def gathers(eng, rows_free, per_tile):
        carry = carrier(eng, pool_turns)
        for q in range(ROWS):
            gather(eng, 0, q, rows_free, per_tile, carry)
        eng.memset(zero_part(2), 0.0).then_inc(g_zero, 1)
        with eng.Fori(1, T // ROWS, 1) as i:
            for q in range(ROWS):
                gather(eng, i, q, rows_free, per_tile, carry)

    def products(eng, q, bank):
        for c in range(KC):
            mm = eng.matmul(ps[:, bank, c * NB * WN:(c + 1) * NB * WN],
                            rows[:, q, c * P:(c + 1) * P],
                            S[:, q, :, :].rearrange("p b n -> p (b n)"), start=True, stop=True)
        return mm

    def build_s(eng, t, q, node):
        return eng.scalar_tensor_tensor(
            S[:, q, :, :], iota[:, :].unsqueeze(1).to_broadcast([P, NB, WN]), node,
            coef[:, bass.ds(t, 1), :].squeeze(1).unsqueeze(2).to_broadcast([P, NB, WN]),
            ALU.is_equal, ALU.mult)

    def zero_part(part):
        cuts = [0, KC * NB * 3 // 8, KC * NB * 3 // 4, KC * NB]
        return G[:, :, :, :].rearrange("p c b n -> p (c b) n")[:, cuts[part]:cuts[part + 1], :]\
            .rearrange("p m n -> p (m n)")

    def add_to_g(eng, base, bank):
        window = G[:, :, :, bass.ds(base, WN)].rearrange("p c b n -> p (c b) n")
        return eng.tensor_tensor(window, window,
                                 ps[:, bank, :].rearrange("p (m n) -> p m n", n=WN), ALU.add)

    with nc.Block() as block:
        @block.gpsimd
        def _(eng):
            general = eng.value_load(wide[0:1, 0:1], min_val=0, max_val=1)
            with eng.If(general == 0):
                gathers(eng, mm_done, 1)
            with eng.Else():
                gathers(eng, w_mm, WINDOWS)

        @block.scalar
        def _(eng):
            eng.wait_ge(zero_at, 1)
            part = zero_part(1)
            n = part.shape[1]
            eng.activation(part, zero[:, :].to_broadcast([P, n]), ACT.Copy).then_inc(g_zero, 1)

        @block.tensor
        def _(eng):
            general = eng.value_load(wide[0:1, 0:1], min_val=0, max_val=1)
            with eng.If(general == 0):
                eng.sem_inc(mm_done, ROWS)
                with eng.Fori(0, T // ROWS, 1) as i:
                    for q in range(ROWS):
                        t = ROWS * i + q
                        eng.wait_ge(rows_in[q], 16 * i + 16)
                        eng.wait_ge(s_at, t + 1)
                        eng.wait_ge(added, t + 1)
                        products(eng, q, q % BANKS).then_inc(mm_done, 1)
            with eng.Else():
                eng.sem_inc(w_mm, ROWS * WINDOWS)
                carry = carrier(eng, pe_turns)
                with eng.Fori(0, T // ROWS, 1) as i:
                    for q in range(ROWS):
                        eng.wait_ge(rows_in[q], 16 * i + 16)
                        carry()
                        with eng.Fori(0, WINDOWS, 1) as w:
                            n = (ROWS * i + q) * WINDOWS + w
                            eng.wait_ge(w_s, n + 1)
                            eng.wait_ge(w_add, n + 1)
                            products(eng, q, 0).then_inc(w_mm, 1)

        @block.vector
        def _(eng):
            eng.memset(zero[:, :], 0.0).then_inc(zero_at, 1)
            general = eng.value_load(wide[0:1, 0:1], min_val=0, max_val=1)
            with eng.If(general == 0):
                starts = [eng.alloc_register(f"l0_start{k}") for k in range(TG)]
                eng.sem_inc(added, BANKS)
                for k in range(ROWS):
                    build_s(eng, k, k, dst_rel[:, k:k + 1]).then_inc(s_at, 1)
                eng.memset(zero_part(0), 0.0).then_inc(g_zero, 1)
                eng.wait_ge(g_zero, 3)
                with eng.Fori(0, T // ROWS, 1) as i:
                    for half in range(2):
                        t0 = ROWS * i + half * TG
                        eng.reg_load(starts, dst_row[0:1, bass.ds(t0, TG)])
                        for k in range(TG):
                            eng.wait_ge(mm_done, ROWS + t0 + k + 1)
                            eng.wait_ge(added, BANKS + t0 + k)
                            start = eng.snap(starts[k], min_val=0, max_val=N - 1)
                            add_to_g(eng, start, half * TG + k).then_inc(added, 1)
                        for k in range(TG):
                            t = t0 + ROWS + k
                            build_s(eng, t, half * TG + k, dst_rel[:, bass.ds(t, 1)])\
                                .then_inc(s_at, 1)
            with eng.Else():
                eng.memset(zero_part(0), 0.0).then_inc(g_zero, 1)
                eng.wait_ge(g_zero, 3)
                eng.sem_inc(w_add, 1)
                with eng.Fori(0, T // ROWS, 1) as i:
                    for q in range(ROWS):
                        t = ROWS * i + q
                        eng.wait_ge(w_add, t * WINDOWS + 1)
                        eng.tensor_copy(node[:, :], dst_idx[:, bass.ds(t, 1)]).then_inc(w_node, 1)
                        with eng.Fori(0, WINDOWS, 1) as w:
                            n = t * WINDOWS + w
                            eng.wait_ge(w_node, n + t + 1)
                            build_s(eng, t, q, node[:, :]).then_inc(w_s, 1)
                            eng.wait_ge(w_s, n + 1)
                            eng.tensor_scalar(node[:, :], node[:, :], -float(WN), None, ALU.add)\
                                .then_inc(w_node, 1)
                            eng.wait_ge(w_mm, ROWS * WINDOWS + n + 1)
                            add_to_g(eng, w * WN, 0).then_inc(w_add, 1)


def apply_bases(nc, st, sbuf, psum, sem, G, bases, h_bias, x1, coef):
    ROUNDS = 2
    TR = NT // ROUNDS
    W = TR * NP
    wb = coef[:, :, :].rearrange("p t b -> p (t b)")[:, 0:2 * D].rearrange("p (s n) -> p s n", s=2)
    wb_hi = sbuf(st, "wb_hi", [P, 2, D], F32R)
    wb_lo = sbuf(st, "wb_lo", [P, 2, D], F32R)
    g_hi = sbuf(st, "g_hi", [P, 2, W], F32R)
    g_lo = sbuf(st, "g_lo", [P, 2, W], F32R)
    bias = sbuf(st, "bias0", [NP, D])
    bias_in = sem(st, "bias0_in")
    biased = sem(st, "biased")
    ps = psum(st, "b_ps", [P, TR, D])
    wb_in = [sem(st, f"wb_in{i}") for i in range(2)]
    hi_at = sem(st, "bases_hi_at")
    lo_at = sem(st, "bases_lo_at")
    used = sem(st, "wb_used")
    got = sem(st, "got")
    pieces = NB * KC

    def rounds(eng, body):
        with eng.Fori(0, ROUNDS, 1) as r:
            body(r)

    def g_part(r, m):
        b, c = divmod(m, KC)
        return G[:, c, b, bass.ds(r * W, W)]

    with nc.Block() as block:
        @block.sync
        def _(eng):
            def body(r):
                for m in range(pieces):
                    b, c = divmod(m, KC)
                    eng.wait_ge(lo_at, 2 * (r * pieces + m) + 2)
                    eng.dma_start(wb[:, m % 2, :], bases[b, c * P:(c + 1) * P, :])\
                        .then_inc(wb_in[m % 2], 16)
            eng.dma_start(bias[:, :], h_bias.partition_broadcast(NP)).then_inc(bias_in, 16)
            rounds(eng, body)

        @block.gpsimd
        def _(eng):
            eng.wait_ge(bias_in, 16)
            for t in range(NT):
                eng.tensor_tensor(x1[:, t, :], x1[:, t, :], bias[:, :], ALU.add).then_inc(biased, 1)

        @block.scalar
        def _(eng):
            def body(r):
                for m in range(pieces):
                    s = m % 2
                    eng.wait_ge(used, r * pieces + m + 1)
                    eng.activation(g_hi[:, s, :], g_part(r, m), ACT.Copy).then_inc(hi_at, 1)
                    eng.wait_ge(wb_in[s], 16 * (r * (pieces // 2) + m // 2 + 1))
                    eng.activation(wb_hi[:, s, :], wb[:, s, :], ACT.Copy).then_inc(hi_at, 1)
            rounds(eng, body)

        @block.tensor
        def _(eng):
            eng.sem_inc(used, 2)

            def body(r):
                for m in range(pieces):
                    s = m % 2
                    eng.wait_ge(lo_at, 2 * (r * pieces + m) + 6)
                    for k in range(TR):
                        if m == 0:
                            eng.wait_ge(got, r * TR + k + 1)
                        cols = slice(k * NP, (k + 1) * NP)
                        for n, (g, w) in enumerate(((g_hi, wb_hi), (g_hi, wb_lo), (g_lo, wb_hi))):
                            mm = eng.matmul(ps[0:NP, k, :], g[:, s, cols], w[:, s, :],
                                            start=(m == 0 and n == 0),
                                            stop=(m == pieces - 1 and n == 2))
                    mm.then_inc(used, 1)
            rounds(eng, body)

        @block.vector
        def _(eng):
            eng.sem_inc(lo_at, 4)
            eng.sem_inc(got, TR)

            def body(r):
                for m in range(pieces):
                    s = m % 2
                    eng.wait_ge(hi_at, 2 * (r * pieces + m) + 1)
                    eng.tensor_tensor(g_lo[:, s, :], g_part(r, m), g_hi[:, s, :].bitcast(F32),
                                      ALU.subtract).then_inc(lo_at, 1)
                    eng.wait_ge(hi_at, 2 * (r * pieces + m) + 2)
                    eng.tensor_tensor(wb_lo[:, s, :], wb[:, s, :], wb_hi[:, s, :].bitcast(F32),
                                      ALU.subtract).then_inc(lo_at, 1)
                eng.wait_ge(used, (r + 1) * pieces + 2)
                eng.wait_ge(biased, NT)
                for k in range(TR):
                    own = x1[:, bass.ds(r * TR + k, 1), :].squeeze(1)
                    eng.tensor_tensor(own, own, ps[0:NP, k, :], ALU.add).then_inc(got, 1)
            rounds(eng, body)


def node_products(nc, st, sbuf, psum, sem, x1, h1, h1t, aggt, edge_weights, ident, w1, b1, w2, b2,
                  xa_v, xb_v, xb_parts):
    w2_hi, w2_lo, wc_hi, wx, b2b = edge_weights
    CH = 2 * KC
    w1ab = sbuf(st, "w1ab", [P, CH, D])
    w1_hi = sbuf(st, "w1_hi", [P, CH, D], F32R)
    w1_lo = sbuf(st, "w1_lo", [P, CH, D], F32R)
    raw2 = sbuf(st, "raw2", [P, KC, D])
    rawc = sbuf(st, "rawc", [P, D])
    ht_hi = sbuf(st, "ht_hi", [P, 2, D], F32R)
    ht_lo = sbuf(st, "ht_lo", [P, 2, D], F32R)
    b1b = sbuf(st, "b1b", [NP, D])
    stats = sbuf(st, "stats1", [NP, NT, 6])
    mv = sbuf(st, "mv1", [NP, NT, 2])
    std = sbuf(st, "std1", [NP, NT])
    rstd = sbuf(st, "rstd1", [NP, NT])
    eps = sbuf(st, "eps1", [NP, 1])
    rows_a = sbuf(st, "rows_a", [NP, 2, D])
    rows_b = sbuf(st, "rows_b", [NP, 2, D])
    parts_b = sbuf(st, "parts_b", [NP, 2, 2, D], F32R)
    pad_b = sbuf(st, "pad_b", [WN, 2, D], F32R)
    tp = psum(st, "tp1", [P, 2, D])
    ps = psum(st, "ab_ps", [P, 4, D])
    w1_in = [sem(st, f"w1_in{a}") for a in range(2)]
    b1_in = sem(st, "b1_in")
    edge_in = sem(st, "edge_in")
    edge_hi = sem(st, "edge_hi")
    eps_at = sem(st, "eps1_at")
    stat = sem(st, "stat1")
    std_at = sem(st, "std1_at")
    norm_at = sem(st, "norm1_at")
    h_at = sem(st, "h1_at")
    w1_hi_at = sem(st, "w1_hi_at")
    w1_lo_at = sem(st, "w1_lo_at")
    tp_done = sem(st, "tp1_done")
    ht_at = sem(st, "h1t_at")
    ht_hi_at = sem(st, "ht_hi_at")
    ht_lo_at = sem(st, "ht_lo_at")
    ab_mm = sem(st, "ab_mm")
    ab_at = sem(st, "ab_at")
    parts_at = sem(st, "parts_at")
    pad_at = sem(st, "pad_at")
    pad_out = sem(st, "pad_out")
    ab_out = [sem(st, f"ab_out{i}") for i in range(2)]
    by_chunk = "p (c n) -> p c n"
    with nc.Block() as block:
        @block.sync
        def _(eng):
            for a in range(2):
                eng.dma_start(w1ab[:, a * KC:(a + 1) * KC, :],
                              w1[a * D:(a + 1) * D, :].rearrange("(c p) n -> p c n", p=P))\
                    .then_inc(w1_in[a], 16)
            eng.dma_start(b1b[:, :], b1.partition_broadcast(NP)).then_inc(b1_in, 16)
            eng.dma_start(raw2[:, :, :], w2.rearrange("(c p) n -> p c n", p=P)).then_inc(edge_in, 16)
            eng.dma_start(b2b[:, :], b2.partition_broadcast(P)).then_inc(edge_in, 16)
            for half in range(2):
                eng.dma_start(rawc[half * ED:(half + 1) * ED, :], w1[2 * D:2 * D + ED, :])\
                    .then_inc(edge_in, 16)
            eng.wait_ge(pad_at, 2)
            eng.dma_start(xb_parts[N:NPAD, :, :], pad_b[:, :, :].bitcast(F32)).then_inc(pad_out, 16)
            for t in range(NT):
                eng.wait_ge(ab_at, 2 * t + 1)
                eng.dma_start(xa_v[:, t, :], rows_a[:, t % 2, :]).then_inc(ab_out[t % 2], 16)
                eng.wait_ge(parts_at, 2 * t + 2)
                eng.dma_start(xb_v[:, t, :, :], parts_b[:, t % 2, :, :].bitcast(F32))\
                    .then_inc(ab_out[t % 2], 16)
            eng.wait_ge(pad_out, 16)
            for s in range(2):
                eng.wait_ge(ab_out[s], 32 * (NT // 2))

        @block.vector
        def _(eng):
            def h_part(t):
                eng.tensor_scalar(h1[:, t, :], x1[:, t, :], mv[:, t, 0:1], rstd[:, t:t + 1],
                                  ALU.subtract, ALU.mult).then_inc(norm_at, 1)
                eng.wait_ge(norm_at, 2 + t)
                eng.tensor_scalar(h1[:, t, :], h1[:, t, :], 0.0, None, ALU.max).then_inc(h_at, 1)

            def ht_low(t):
                eng.wait_ge(ht_hi_at, t + 1)
                wait(eng, ab_mm, 2 * (t - 1))
                eng.tensor_tensor(ht_lo[:, t % 2, :].rearrange(by_chunk, c=KC)[:, :, 0:NP],
                                  h1t[:, :, t * NP:(t + 1) * NP],
                                  ht_hi[:, t % 2, :].rearrange(by_chunk, c=KC)[:, :, 0:NP].bitcast(F32),
                                  ALU.subtract).then_inc(ht_lo_at, 1)

            def rows_of(t):
                eng.wait_ge(ab_mm, 2 * t + 2)
                if t >= 2:
                    eng.wait_ge(ab_out[t % 2], 32 * (t // 2))
                eng.tensor_copy(rows_a[:, t % 2, :], ps[0:NP, 2 * (t % 2), :]).then_inc(ab_at, 1)
                wait(eng, parts_at, 2 * (t - 1))
                eng.tensor_tensor(rows_b[:, t % 2, :], ps[0:NP, 2 * (t % 2) + 1, :], b1b[:, :],
                                  ALU.add).then_inc(ab_at, 1)
                eng.wait_ge(parts_at, 2 * t + 1)
                eng.tensor_tensor(parts_b[:, t % 2, 1, :], rows_b[:, t % 2, :],
                                  parts_b[:, t % 2, 0, :].bitcast(F32), ALU.subtract)\
                    .then_inc(parts_at, 1)

            eng.memset(eps[:, :], EPS).then_inc(eps_at, 1)
            for t in range(NT):
                eng.bn_stats(stats[:, t, :], x1[:, t, :]).then_inc(stat, 1)
            for t in range(NT):
                eng.wait_ge(stat, t + 1)
                eng.bn_aggr(mv[:, t, :], stats[:, t, :]).then_inc(stat, 1)
            eng.wait_ge(std_at, 1)
            eng.reciprocal(rstd[:, :], std[:, :]).then_inc(norm_at, 1)
            eng.wait_ge(norm_at, 1)
            h_part(0)
            h_part(1)
            for n in range(CH):
                eng.wait_ge(w1_hi_at, n + 1)
                eng.tensor_tensor(w1_lo[:, n, :], w1ab[:, n, :], w1_hi[:, n, :].bitcast(F32),
                                  ALU.subtract).then_inc(w1_lo_at, 1)
                if n == 1:
                    ht_low(0)
            eng.memset(rows_b[:, 0, :], 0.0).then_inc(pad_at, 1)
            eng.wait_ge(pad_at, 1)
            eng.tensor_copy(pad_b[:, :, :], rows_b[0:WN, 0, :].unsqueeze(1).to_broadcast([WN, 2, D]))\
                .then_inc(pad_at, 1)
            eng.wait_ge(pad_at, 2)
            eng.wait_ge(b1_in, 16)
            for t in range(NT):
                if t + 2 < NT:
                    h_part(t + 2)
                if t + 1 < NT:
                    ht_low(t + 1)
                rows_of(t)
                if t == 4:
                    eng.wait_ge(edge_hi, 2)
                    eng.tensor_tensor(w2_lo[:, :, :], raw2[:, :, :], w2_hi[:, :, :].bitcast(F32),
                                      ALU.subtract)
                if t == 6:
                    for k in range(TG):
                        eng.tensor_tensor(wx[0:ED, k, :], rawc[0:ED, :],
                                          wc_hi[0:ED, :].bitcast(F32), ALU.subtract)

        @block.gpsimd
        def _(eng):
            eng.memset(aggt[:, :, :].rearrange("p c n -> p (c n)"), 0.0)

        @block.scalar
        def _(eng):
            def high_part(t):
                eng.wait_ge(ab_at, 2 * t + 2)
                if t >= 2:
                    eng.wait_ge(ab_out[t % 2], 32 * (t // 2))
                eng.activation(parts_b[:, t % 2, 0, :], rows_b[:, t % 2, :], ACT.Copy)\
                    .then_inc(parts_at, 1)

            for n in range(CH):
                if n % KC == 0:
                    eng.wait_ge(w1_in[n // KC], 16)
                eng.activation(w1_hi[:, n, :], w1ab[:, n, :], ACT.Copy).then_inc(w1_hi_at, 1)
                if n == KC - 1:
                    eng.wait_ge(stat, 2 * NT)
                    eng.wait_ge(eps_at, 1)
                    eng.activation(std[:, :], mv[:, :, 1:2].squeeze(2), ACT.Sqrt, bias=eps[:, :])\
                        .then_inc(std_at, 1)
            for t in range(NT):
                eng.wait_ge(tp_done, t + 1)
                view = tp[:, t % 2, :].rearrange(by_chunk, c=KC)[:, :, 0:NP]
                wait(eng, ab_mm, 2 * (t - 1))
                eng.activation(ht_hi[:, t % 2, :].rearrange(by_chunk, c=KC)[:, :, 0:NP], view,
                               ACT.Copy).then_inc(ht_at, 1)
                eng.activation(h1t[:, :, t * NP:(t + 1) * NP], view, ACT.Copy).then_inc(ht_hi_at, 1)
                if t > 0:
                    high_part(t - 1)
                if t == 2:
                    eng.wait_ge(edge_in, 64)
                    eng.activation(w2_hi[:, :, :], raw2[:, :, :], ACT.Copy).then_inc(edge_hi, 1)
                    eng.activation(wc_hi[:, :], rawc[:, :], ACT.Copy).then_inc(edge_hi, 1)
            high_part(NT - 1)

        @block.tensor
        def _(eng):
            def transposes(t):
                eng.wait_ge(h_at, t + 1)
                wait(eng, ht_hi_at, t - 1)
                for c in range(KC):
                    mm = eng.transpose(tp[:, t % 2, c * P:c * P + NP], h1[:, t, c * P:(c + 1) * P],
                                       ident[0:NP, 0:NP])
                mm.then_inc(tp_done, 1)

            transposes(0)
            for t in range(NT):
                if t + 1 < NT:
                    transposes(t + 1)
                eng.wait_ge(ht_at, t + 1)
                eng.wait_ge(ht_lo_at, t + 1)
                wait(eng, ab_at, 2 * (t - 1))
                for a in range(2):
                    for c in range(KC):
                        n = a * KC + c
                        if t == 0:
                            eng.wait_ge(w1_lo_at, n + 1)
                        for i, (h, w) in enumerate(((ht_hi, w1_hi), (ht_hi, w1_lo), (ht_lo, w1_hi))):
                            mm = eng.matmul(ps[0:NP, 2 * (t % 2) + a, :],
                                            h[:, t % 2, c * P:c * P + NP], w[:, n, :],
                                            start=(c == 0 and i == 0), stop=(c == KC - 1 and i == 2))
                    mm.then_inc(ab_mm, 1)


def edge_mlp(nc, st, sbuf, psum, sem, aggt, edge_weights, xa_rows, xb_parts, edge_attr, src_idx,
             dst_idx, dst_e, dst_row, dst_rel, win_node, iota, ident, wide):
    w2_hi, w2_lo, wc_hi, wx, b2b = edge_weights
    GF = TG * D
    X = sbuf(st, "X", [P, 2, GF])
    XB = sbuf(st, "XB", [P, 2, D])
    U1 = sbuf(st, "U1", [P, 2, GF])
    X2 = sbuf(st, "X2", [P, 2, GF])
    U2 = sbuf(st, "U2", [P, 2, GF])
    h_hi = sbuf(st, "h_hi", [P, 2, D], F32R)
    h_lo = sbuf(st, "h_lo", [P, 2, D], F32R)
    ea = sbuf(st, "ea", [P, 2, TG * P])
    ea_hl = sbuf(st, "ea_hl", [P, 2, TG * P], F32R)
    ea_n = sbuf(st, "ea_n", [P, 2, TG * P], F32R)
    dst_b = sbuf(st, "dst_b", [P, 2, TG * P], I32)
    one = sbuf(st, "one", [P, 2, TG, WN])
    idx_a = sbuf(st, "idx_a", [P, 2, TG], I32)
    idx_b = sbuf(st, "idx_b", [P, 1], I32)
    pz1 = psum(st, "pz1", [P, 2, D])
    pt = psum(st, "pt", [P, 2, D])
    pz2 = psum(st, "pz2", [P, 2, D])
    pg = psum(st, "pg", [P, 2, D])

    ea_in = [sem(st, f"ea_in{i}") for i in range(2)]
    a_in = [sem(st, f"a_in{i}") for i in range(2)]
    b_in = sem(st, "b_in")
    ia_at = sem(st, "ia_at")
    ib_at = sem(st, "ib_at")
    wx_in = [sem(st, f"wx_in{i}") for i in range(TG)]
    ea_at = sem(st, "ea_at")
    hot_at = sem(st, "hot_at")
    xb_at = sem(st, "xb_at")
    x_at = sem(st, "x_at")
    z1_mm = sem(st, "z1_mm")
    z1_at = sem(st, "z1_at")
    exp1 = sem(st, "exp1")
    cut1 = sem(st, "cut1")
    ln1 = sem(st, "ln1")
    tanh1 = sem(st, "tanh1")
    hid = sem(st, "hid")
    exp2 = sem(st, "exp2")
    cut2 = sem(st, "cut2")
    ln2 = sem(st, "ln2")
    tanh2 = sem(st, "tanh2")
    msg = sem(st, "msg")
    t_mm = sem(st, "t_mm")
    hi_at = sem(st, "hi_at")
    lo_at = sem(st, "lo_at")
    z2_mm = sem(st, "z2_mm")
    z2_at = sem(st, "z2_at")
    one_at = sem(st, "one_at")
    sum_mm = sem(st, "sum_mm")
    sum_at = sem(st, "sum_at")
    g_one = sem(st, "g_one")
    g_mm = sem(st, "g_mm")
    g_at = sem(st, "g_at")
    g_node = sem(st, "g_node")
    pool_turns = sem(st, "l1_pool_turns")
    pe_turns = sem(st, "l1_pe_turns")
    node = sbuf(st, "l1_node", [P, 1])

    def grp(i, d):
        return 2 * i + d

    def tile(i, d, k):
        return 2 * TG * i + TG * d + k

    def count(i, d, per=16):
        return per * i + per * (d // 2 + 1)

    def steps(eng, step, first, last):
        lo, hi = 3, GROUPS - 4
        hi -= (hi - lo + 1) % 2
        for j in range(first, lo):
            step(0, j, j)
        with eng.Fori(0, (hi - lo + 1) // 2, 1) as i:
            for p in range(2):
                step(i, lo + p, None)
        for j in range(hi + 1, last + 1):
            step(0, j, j)

    def there(j, d):
        return j is None or 0 <= j + d < GROUPS

    def pe_program(eng, general):
        carry = carrier(eng, pe_turns)

        def edge_products(i, d, k):
            s = d % 2
            if k == 0:
                eng.wait_ge(ea_at, 3 * grp(i, d) + 3)
                if not general:
                    eng.wait_ge(hot_at, grp(i, d) + 1)
            wait(eng, z1_at, tile(i, d, k) - 1)
            eng.matmul(pz1[:, k % 2, :], ea_hl[:, s, k * P:(k + 1) * P], wc_hi[:, :], start=True,
                       stop=False)
            eng.wait_ge(wx_in[k], 16 * grp(i, d) + 16)
            rows = ED if general else BR + 2 * WN
            eng.matmul(pz1[:, k % 2, :], ea_n[0:rows, s, k * P:(k + 1) * P], wx[0:rows, k, :],
                       start=False, stop=True).then_inc(z1_mm, 1)

        def transposes(i, d, k):
            if k == 0:
                eng.wait_ge(hid, grp(i, d) + 1)
            wait(eng, lo_at, tile(i, d, k) - 1)
            for c in range(KC):
                mm = eng.transpose(pt[:, k % 2, c * P:(c + 1) * P],
                                   U1[:, d % 2, k * D + c * P:k * D + (c + 1) * P], ident[:, :])
            mm.then_inc(t_mm, 1)

        def hidden_products(i, d, k):
            eng.wait_ge(lo_at, tile(i, d, k) + 1)
            wait(eng, z2_at, tile(i, d, k) - 1)
            n = 0
            for c in range(KC):
                for part, w in ((h_hi, w2_hi), (h_hi, w2_lo), (h_lo, w2_hi)):
                    mm = eng.matmul(pz2[:, k % 2, :], part[:, k % 2, c * P:(c + 1) * P], w[:, c, :],
                                    start=(n == 0), stop=(n == 3 * KC - 1))
                    n += 1
            mm.then_inc(z2_mm, 1)

        def window_products(s, k):
            for c in range(KC):
                mm = eng.matmul(pg[:, k % 2, c * WN:(c + 1) * WN], U2[:, s, k * D + c * P:k * D + (c + 1) * P],
                                one[:, s, k, :], start=True, stop=True)
            return mm

        def sum_products(i, d, k):
            if k == 0:
                eng.wait_ge(msg, grp(i, d) + 1)
            t = tile(i, d, k)
            if not general:
                eng.wait_ge(one_at, t + 1)
                eng.wait_ge(sum_at, t + 1)
                window_products(d % 2, k).then_inc(sum_mm, 1)
            else:
                carry()
                with eng.Fori(0, WINDOWS, 1) as w:
                    eng.wait_ge(g_one, t * WINDOWS + w + 1)
                    window_products(d % 2, k).then_inc(g_mm, 1)

        def plain_step(i, d, j):
            if there(j, 0):
                for k in range(TG):
                    edge_products(i, d, k)
                for k in range(TG):
                    transposes(i, d, k)
                    hidden_products(i, d, k)
                for k in range(TG):
                    sum_products(i, d, k)

        def step(i, d, j):
            if there(j, 0):
                hidden_products(i, d, 1)
            if there(j, -2):
                sum_products(i, d - 2, 0)
                sum_products(i, d - 2, 1)
            if there(j, 3):
                edge_products(i, d + 3, 0)
            if there(j, 0):
                hidden_products(i, d, 2)
            if there(j, -2):
                sum_products(i, d - 2, 2)
            if there(j, 1):
                transposes(i, d + 1, 0)
                transposes(i, d + 1, 1)
            if there(j, 3):
                edge_products(i, d + 3, 1)
            if there(j, 0):
                hidden_products(i, d, 3)
            if there(j, -2):
                sum_products(i, d - 2, 3)
            if there(j, 1):
                hidden_products(i, d + 1, 0)
            if there(j, 3):
                edge_products(i, d + 3, 2)
            if there(j, 1):
                transposes(i, d + 1, 2)
            if there(j, 3):
                edge_products(i, d + 3, 3)
            if there(j, 1):
                transposes(i, d + 1, 3)

        steps(eng, plain_step if general else step, -3, GROUPS + 1)

    def act_program(eng, general):
        def act(func, u, d, source=None, bias=0.0):
            return eng.activation(u[:, d % 2, :], (u if source is None else source)[:, d % 2, :], func,
                                  bias=bias)

        def exp_1(i, d):
            eng.wait_ge(z1_at, tile(i, d, TG))
            wait(eng, t_mm, tile(i, d - 1, 0))
            act(ACT.Exp, U1, d, X).then_inc(exp1, 1)

        def exp_2(i, d):
            eng.wait_ge(z2_at, tile(i, d, TG))
            wait(eng, sum_mm, tile(i, d - 1, 0))
            act(ACT.Exp, U2, d, X2).then_inc(exp2, 1)

        def ln(u, i, d, cut, done):
            eng.wait_ge(cut, grp(i, d) + 1)
            act(ACT.Ln, u, d, bias=1.0).then_inc(done, 1)

        def tanh(u, i, d, ln, done):
            eng.wait_ge(ln, grp(i, d) + 1)
            act(ACT.Tanh, u, d).then_inc(done, 1)

        def hi_part(i, d, k):
            t = tile(i, d, k)
            eng.wait_ge(t_mm, t + 1)
            wait(eng, z2_mm, t - 1)
            eng.activation(h_hi[:, k % 2, :], pt[:, k % 2, :], ACT.Copy).then_inc(hi_at, 1)

        def plain_step(i, d, j):
            if there(j, 0):
                exp_1(i, d)
                ln(U1, i, d, cut1, ln1)
                tanh(U1, i, d, ln1, tanh1)
                for k in range(TG):
                    hi_part(i, d, k)
                exp_2(i, d)
                ln(U2, i, d, cut2, ln2)
                tanh(U2, i, d, ln2, tanh2)

        def step(i, d, j):
            if there(j, 1):
                ln(U1, i, d + 1, cut1, ln1)
            if there(j, 0):
                hi_part(i, d, 1)
            if there(j, -2):
                tanh(U2, i, d - 2, ln2, tanh2)
            if there(j, 0):
                hi_part(i, d, 2)
            if there(j, -1):
                exp_2(i, d - 1)
            if there(j, 1):
                tanh(U1, i, d + 1, ln1, tanh1)
            if there(j, 2):
                exp_1(i, d + 2)
            if there(j, 0):
                hi_part(i, d, 3)
            if there(j, -1):
                ln(U2, i, d - 1, cut2, ln2)
            if there(j, 1):
                hi_part(i, d + 1, 0)

        steps(eng, plain_step if general else step, -2, GROUPS + 1)

    def dve_program(eng, general):
        starts = [eng.alloc_register(f"l1_start{general}{k}") for k in range(TG)]

        def window_rows(i, d):
            s = d % 2
            eng.wait_ge(ea_in[s], count(i, d, 48))
            wait(eng, z1_mm, tile(i, d - 1, 0))
            hot = slice(BR, BR + 2 * WN)
            for k in range(TG):
                cols = slice(k * P, (k + 1) * P)
                op = eng.tensor_scalar(ea_n[hot, s, cols], dst_b[hot, s, cols],
                                       win_node[hot, bass.ds(tile(i, d, k), 1)], None,
                                       ALU.is_equal)
            op.then_inc(hot_at, 1)

        def preactivation(i, d, k):
            if k == 0 and general:
                eng.wait_ge(x_at, grp(i, d) + 1)
            if k == 0 and not general:
                eng.wait_ge(a_in[d % 2], count(i, d, 64))
            eng.wait_ge(z1_mm, tile(i, d, k) + 1)
            own = X[:, d % 2, k * D:(k + 1) * D]
            eng.tensor_tensor(own, own, pz1[:, k % 2, :], ALU.add).then_inc(z1_at, 1)

        def cut(u, i, d, exp, done):
            eng.wait_ge(exp, grp(i, d) + 1)
            eng.tensor_scalar(u[:, d % 2, :], u[:, d % 2, :], U_MAX, None, ALU.min).then_inc(done, 1)

        def times(u, z, i, d, tanh, done):
            eng.wait_ge(tanh, grp(i, d) + 1)
            eng.tensor_tensor(u[:, d % 2, :], u[:, d % 2, :], z[:, d % 2, :], ALU.mult)\
                .then_inc(done, 1)

        def lo_part(i, d, k):
            eng.wait_ge(hi_at, tile(i, d, k) + 1)
            eng.tensor_tensor(h_lo[:, k % 2, :], pt[:, k % 2, :], h_hi[:, k % 2, :].bitcast(F32),
                              ALU.subtract).then_inc(lo_at, 1)

        def second_preactivation(i, d, k):
            t = tile(i, d, k)
            if k == 0:
                wait(eng, msg, grp(i, d - 1))
            eng.wait_ge(z2_mm, t + 1)
            eng.tensor_tensor(X2[:, d % 2, k * D:(k + 1) * D], pz2[:, k % 2, :], b2b[:, :], ALU.add)\
                .then_inc(z2_at, 1)

        def one_hots(i, d):
            wait(eng, sum_mm, tile(i, d - 1, 0))
            for k in range(TG):
                t = tile(i, d, k)
                eng.tensor_scalar(one[:, d % 2, k, :], iota[:, :], dst_rel[:, bass.ds(t, 1)],
                                  None, ALU.is_equal).then_inc(one_at, 1)

        def add_window(k, base):
            window = aggt[:, :, bass.ds(base, WN)]
            return eng.tensor_tensor(window, window,
                                     pg[:, k % 2, 0:KC * WN].rearrange("p (c n) -> p c n", c=KC),
                                     ALU.add)

        def sum_up(i, d, k):
            t = tile(i, d, k)
            s = d % 2
            if not general:
                eng.wait_ge(sum_mm, t + 1)
                eng.wait_ge(sum_at, 2 + t)
                start = eng.snap(starts[k], min_val=0, max_val=N - 1)
                add_window(k, start).then_inc(sum_at, 1)
            else:
                eng.wait_ge(g_at, t * WINDOWS + 1)
                eng.tensor_copy(node[:, :], dst_idx[:, bass.ds(t, 1)]).then_inc(g_node, 1)
                with eng.Fori(0, WINDOWS, 1) as w:
                    n = t * WINDOWS + w
                    eng.wait_ge(g_node, n + t + 1)
                    eng.tensor_scalar(one[:, s, k, :], iota[:, :], node[:, :], None,
                                      ALU.is_equal).then_inc(g_one, 1)
                    eng.wait_ge(g_one, n + 1)
                    eng.tensor_scalar(node[:, :], node[:, :], -float(WN), None, ALU.add)\
                        .then_inc(g_node, 1)
                    eng.wait_ge(g_mm, n + 1)
                    add_window(k, w * WN).then_inc(g_at, 1)
                eng.sem_inc(sum_mm, 1)

        def plain_step(i, d, j):
            if there(j, 0):
                window_rows(i, d)
                for k in range(TG):
                    preactivation(i, d, k)
                cut(U1, i, d, exp1, cut1)
                times(U1, X, i, d, tanh1, hid)
                for k in range(TG):
                    lo_part(i, d, k)
                    second_preactivation(i, d, k)
                cut(U2, i, d, exp2, cut2)
                times(U2, X2, i, d, tanh2, msg)
                for k in range(TG):
                    sum_up(i, d, k)

        def step(i, d, j):
            if there(j, -2):
                eng.reg_load(starts, dst_row[0:1, bass.ds(tile(i, d - 2, 0), TG)])
            if there(j, 0):
                lo_part(i, d, 1)
            if there(j, 2):
                preactivation(i, d + 2, 0)
                preactivation(i, d + 2, 1)
            if there(j, 3):
                window_rows(i, d + 3)
            if there(j, 2):
                preactivation(i, d + 2, 2)
            if there(j, -2):
                times(U2, X2, i, d - 2, tanh2, msg)
            if there(j, 2):
                preactivation(i, d + 2, 3)
            if there(j, 0):
                lo_part(i, d, 2)
                second_preactivation(i, d, 0)
            if there(j, -2):
                sum_up(i, d - 2, 0)
            if there(j, 1):
                times(U1, X, i, d + 1, tanh1, hid)
            if there(j, -1):
                cut(U2, i, d - 1, exp2, cut2)
            if there(j, 0):
                lo_part(i, d, 3)
                second_preactivation(i, d, 1)
            if there(j, 2):
                cut(U1, i, d + 2, exp1, cut1)
            if there(j, -2):
                sum_up(i, d - 2, 1)
            if there(j, 0):
                second_preactivation(i, d, 2)
            if there(j, 1):
                lo_part(i, d + 1, 0)
            if there(j, -1):
                one_hots(i, d - 1)
            if there(j, 0):
                second_preactivation(i, d, 3)
            if there(j, -2):
                sum_up(i, d - 2, 2)
                sum_up(i, d - 2, 3)

        eng.sem_inc(g_at if general else sum_at, 1 if general else 2)
        steps(eng, plain_step if general else step, -4, GROUPS + 1)

    def pool_program(eng, general):
        carry = carrier(eng, pool_turns)
        xb_rows = xb_parts.rearrange("n h f -> n (h f)")

        def rows_of_edges(i, d):
            s = d % 2
            if d >= 2:
                eng.wait_ge(a_in[s], count(i, d - 2, 64))
            eng.tensor_copy(idx_a[:, s, :], src_idx[:, bass.ds(tile(i, d, 0), TG)]).then_inc(ia_at, 1)
            eng.wait_ge(ia_at, grp(i, d) + 1)
            wait(eng, hid, grp(i, d) - 1)
            carry()
            for k in range(TG):
                eng.indirect_dma_start(X[:, s, k * D:(k + 1) * D], None, xa_rows,
                                       bass.IndirectOffsetOnAxis(ap=idx_a[:, s, k:k + 1], axis=0))\
                    .then_inc(a_in[s], 16)
            if general:
                add_rows_of_nodes(i, d)

        def add_rows_of_nodes(i, d):
            s = d % 2
            eng.wait_ge(a_in[s], count(i, d, 64))
            for k in range(TG):
                t = tile(i, d, k)
                eng.tensor_copy(idx_b[:, :], dst_row[:, bass.ds(t, 1)]).then_inc(ib_at, 1)
                eng.wait_ge(ib_at, t + 1)
                carry()
                eng.indirect_dma_start(XB[:, :, :].rearrange("p h f -> p (h f)"), None, xb_rows,
                                       bass.IndirectOffsetOnAxis(ap=idx_b[:, :], axis=0))\
                    .then_inc(b_in, 16)
                eng.wait_ge(b_in, 16 * t + 16)
                own = X[:, s, k * D:(k + 1) * D]
                for h in range(2):
                    eng.tensor_tensor(own, own, XB[:, h, :], ALU.add).then_inc(xb_at, 1)
                    eng.wait_ge(xb_at, 2 * t + h + 1)
            eng.sem_inc(x_at, 1)

        def left_sides(i, d):
            s = d % 2
            eng.wait_ge(ea_in[s], count(i, d, 48))
            wait(eng, z1_mm, tile(i, d - 1, 0))
            carry()
            eng.tensor_copy(ea_hl[:, s, :], ea[:, s, :]).then_inc(ea_at, 1)
            eng.tensor_copy(ea_n[0:ED, s, :], ea[0:ED, s, :]).then_inc(ea_at, 1)
            eng.wait_ge(ea_at, 3 * grp(i, d) + 2)
            eng.tensor_tensor(ea_hl[0:ED, s, :], ea[0:ED, s, :], ea_n[0:ED, s, :].bitcast(F32),
                              ALU.subtract).then_inc(ea_at, 1)

        def step(i, d):
            rows_of_edges(i, d)
            left_sides(i, d + 1)

        rows_of_edges(0, 0)
        left_sides(0, 0)
        left_sides(0, 1)
        for d in range(1, 3):
            step(0, d)
        with eng.Fori(0, (GROUPS - 4) // 2, 1) as i:
            step(i, 3)
            step(i, 4)
        rows_of_edges(0, GROUPS - 1)

    def branch(eng, program):
        general = eng.value_load(wide[0:1, 0:1], min_val=0, max_val=1)
        with eng.If(general == 0):
            program(eng, 0)
        with eng.Else():
            program(eng, 1)

    with nc.Block() as block:
        @block.sync
        def _(eng):
            starts = [eng.alloc_register(f"wx_start{k}") for k in range(TG)]

            def attributes(i, d):
                s = d % 2
                wait(eng, ea_at, 3 * grp(i, d - 1))
                wait(eng, hot_at, grp(i, d - 1))
                cols = bass.ds(tile(i, d, 0) * P, TG * P)
                for half in range(2):
                    eng.dma_start(ea[half * ED:(half + 1) * ED, s, :], edge_attr[:, cols])\
                        .then_inc(ea_in[s], 16)
                eng.dma_start(dst_b[BR:BR + 2 * WN, s, :], dst_e[cols].partition_broadcast(2 * WN))\
                    .then_inc(ea_in[s], 16)

            def windows(i, d):
                eng.reg_load(starts, dst_row[0:1, bass.ds(tile(i, d, 0), TG)])
                for k in range(TG):
                    wait(eng, z1_mm, tile(i, d - 1, k) + 1)
                    start = eng.snap(starts[k], min_val=0, max_val=N - 1)
                    eng.dma_start(wx[BR:BR + 2 * WN, k, :].bitcast(F32),
                                  xb_parts[bass.ds(start, WN), :, :].rearrange("n h f -> (n h) f"))\
                        .then_inc(wx_in[k], 16)

            attributes(0, 0)
            attributes(0, 1)
            for d in range(2):
                windows(0, d)
            with eng.Fori(0, GROUPS // 2 - 1, 1) as i:
                for d in (2, 3):
                    attributes(i, d)
                    windows(i, d)

        @block.gpsimd
        def _(eng):
            branch(eng, pool_program)

        @block.tensor
        def _(eng):
            branch(eng, pe_program)

        @block.scalar
        def _(eng):
            branch(eng, act_program)

        @block.vector
        def _(eng):
            branch(eng, dve_program)


def node_mlp(nc, st, sbuf, psum, sem, x1, h1, h1t, aggt, ident, w3, b3, w4, b4, gamma, beta, out_v):
    turns = [(t, t + 1) for t in range(0, NT - 2, 2)] + [(NT - 2,), (NT - 1,)]
    NORM_A = 6
    raw = sbuf(st, "raw34", [P, 2 * KC, D])
    w3_hi = sbuf(st, "w3_hi", [P, 2 * KC, D], F32R)
    w3_lo = sbuf(st, "w3_lo", [P, 2 * KC, D], F32R)
    w4_hi = sbuf(st, "w4_hi", [P, KC, D], F32R)
    w4_lo = sbuf(st, "w4_lo", [P, KC, D], F32R)
    in_hi = sbuf(st, "in_hi", [P, 2, 2 * KC, NP], F32R)
    in_lo = sbuf(st, "in_lo", [P, 2, 2 * KC, NP], F32R)
    rows = sbuf(st, "rows5", [NP, 4, D])
    Z = sbuf(st, "Z", [NP, 2, 2, D])
    U = sbuf(st, "U", [NP, 2, 2, D])
    ut_hi = sbuf(st, "ut_hi", [P, 2, D], F32R)
    ut_lo = sbuf(st, "ut_lo", [P, 2, D], F32R)
    stats = sbuf(st, "stats2", [NP, NT, 6])
    mv = sbuf(st, "mv2", [NP, NT, 2])
    std = sbuf(st, "std2", [NP, NT])
    rstd = sbuf(st, "rstd2", [NP, NT])
    eps = sbuf(st, "eps2", [NP, 1])
    p3 = psum(st, "p3", [P, 4, D])
    pt = psum(st, "pt3", [P, 2, D])
    p4 = psum(st, "p4", [P, 2, D])
    w3_in = [sem(st, f"w3_in{c}") for c in range(KC)]
    w4_in = sem(st, "w4_in")
    w_hi_at = sem(st, "w34_hi_at")
    w_lo_at = sem(st, "w34_lo_at")
    in_hi_at = sem(st, "in_hi_at")
    in_lo_at = sem(st, "in_lo_at")
    rows_in = [sem(st, f"rows5_in{n}") for n in range(4)]
    eps_at = sem(st, "eps2_at")
    mm3 = sem(st, "mm3")
    z_at = sem(st, "z_at")
    e_at = sem(st, "e_at")
    cut = sem(st, "cut")
    l_at = sem(st, "l_at")
    t_at = sem(st, "t_at")
    u_at = sem(st, "u_at")
    tp = sem(st, "tp3")
    ut_at = sem(st, "ut_at")
    ut_lo_at = sem(st, "ut_lo_at")
    mm4 = sem(st, "mm4")
    y_a = sem(st, "y_a")
    y_at = sem(st, "y_at")
    stat = sem(st, "stat2")
    aggr = sem(st, "aggr")
    std_at = sem(st, "std2_at")
    r_at = sem(st, "r_at")
    f1 = sem(st, "f1")
    f2 = sem(st, "f2")
    f3 = sem(st, "f3")
    stored = sem(st, "stored")

    def slot(t):
        for g, tiles in enumerate(turns):
            if t in tiles:
                return g % 2, tiles.index(t)

    def input_part(buf, t, c0):
        return buf[:, t % 2, c0:c0 + KC, :]

    view = "p (c n) -> p c n"

    def tiles_of(buf, g):
        return buf[:, g % 2, 0:len(turns[g]), :]

    with nc.Block() as block:
        @block.sync
        def _(eng):
            w3_v = w3.rearrange("(c p) n -> p c n", p=P)
            for c in range(KC):
                eng.dma_start(raw[:, 2 * c:2 * c + 2, :], w3_v[:, 2 * c:2 * c + 2, :])\
                    .then_inc(w3_in[c], 16)
            eng.wait_ge(w_lo_at, 2)
            eng.dma_start(raw[:, 0:KC, :], w4.rearrange("(c p) n -> p c n", p=P)).then_inc(w4_in, 16)
            for t in range(NT):
                eng.wait_ge(f3, t + 1)
                eng.dma_start(out_v[:, t, :], x1[:, t, :]).then_inc(stored, 16)
            eng.wait_ge(stored, 16 * NT)

        @block.tensor
        def _(eng):
            def first(g):
                if g >= 2:
                    eng.wait_ge(z_at, turns[g - 2][-1] + 1)
                for t in turns[g]:
                    s, i = slot(t)
                    eng.wait_ge(in_lo_at, 2 * t + 2)
                    for c in range(2 * KC):
                        if t == 0 and c % 2 == 0:
                            eng.wait_ge(w_lo_at, c // 2 + 1)
                        for n, (h, w) in enumerate(((in_hi, w3_hi), (in_hi, w3_lo), (in_lo, w3_hi))):
                            mm = eng.matmul(p3[0:NP, 2 * s + i, :], h[:, t % 2, c, :], w[:, c, :],
                                            start=(c == 0 and n == 0),
                                            stop=(c == 2 * KC - 1 and n == 2))
                    mm.then_inc(mm3, 1)

            def second(g):
                eng.wait_ge(u_at, g + 1)
                for t in turns[g]:
                    s, i = slot(t)
                    wait(eng, ut_lo_at, t - 1)
                    for c in range(KC):
                        mm = eng.transpose(pt[:, t % 2, c * P:c * P + NP],
                                           U[:, s, i, c * P:(c + 1) * P], ident[0:NP, 0:NP])
                    mm.then_inc(tp, 1)
                for t in turns[g]:
                    eng.wait_ge(ut_lo_at, t + 1)
                    wait(eng, y_a, t - 1)
                    for c in range(KC):
                        for n, (u, w) in enumerate(((ut_hi, w4_hi), (ut_hi, w4_lo), (ut_lo, w4_hi))):
                            mm = eng.matmul(p4[0:NP, t % 2, :], u[:, t % 2, c * P:c * P + NP],
                                            w[:, c, :], start=(c == 0 and n == 0),
                                            stop=(c == KC - 1 and n == 2))
                    mm.then_inc(mm4, 1)

            first(0)
            for g in range(len(turns)):
                if g + 1 < len(turns):
                    first(g + 1)
                if g == 0:
                    eng.wait_ge(w_lo_at, KC + 1)
                second(g)

        @block.scalar
        def _(eng):
            for n, v in enumerate((b3, b4, gamma, beta)):
                eng.dma_start(rows[:, n, :], v.partition_broadcast(NP)).then_inc(rows_in[n], 16)

            def deviations(t0, t1):
                eng.wait_ge(aggr, t1)
                eng.activation(std[:, t0:t1], mv[:, t0:t1, 1:2].squeeze(2), ACT.Sqrt,
                               bias=eps[:, :]).then_inc(std_at, 1)

            def input_high(t):
                if t < NT:
                    wait(eng, mm3, t - 1)
                    nodes = slice(t * NP, (t + 1) * NP)
                    for c0, source in ((0, h1t), (KC, aggt)):
                        eng.activation(input_part(in_hi, t, c0), source[:, :, nodes], ACT.Copy)\
                            .then_inc(in_hi_at, 1)

            input_high(0)
            for c in range(KC):
                eng.wait_ge(w3_in[c], 16)
                eng.activation(w3_hi[:, 2 * c:2 * c + 2, :], raw[:, 2 * c:2 * c + 2, :], ACT.Copy)\
                    .then_inc(w_hi_at, 1)
            input_high(1)
            input_high(2)
            eng.wait_ge(w4_in, 16)
            eng.activation(w4_hi[:, :, :], raw[:, 0:KC, :], ACT.Copy).then_inc(w_hi_at, 1)
            input_high(3)
            eng.wait_ge(eps_at, 1)
            for g, tiles in enumerate(turns):
                eng.wait_ge(z_at, tiles[-1] + 1)
                if g >= 2:
                    eng.wait_ge(tp, turns[g - 2][-1] + 1)
                eng.activation(tiles_of(U, g), tiles_of(Z, g), ACT.Exp).then_inc(e_at, 1)
                eng.wait_ge(cut, g + 1)
                eng.activation(tiles_of(U, g), tiles_of(U, g), ACT.Ln, bias=1.0).then_inc(l_at, 1)
                eng.wait_ge(l_at, g + 1)
                eng.activation(tiles_of(U, g), tiles_of(U, g), ACT.Tanh).then_inc(t_at, 1)
                if g + 2 < len(turns):
                    for t in turns[g + 2]:
                        input_high(t)
                for t in tiles:
                    eng.wait_ge(tp, t + 1)
                    wait(eng, mm4, t - 1)
                    eng.activation(ut_hi[:, t % 2, :].rearrange(view, c=KC)[:, :, 0:NP],
                                   pt[:, t % 2, :].rearrange(view, c=KC)[:, :, 0:NP], ACT.Copy)\
                        .then_inc(ut_at, 1)
                if g == NORM_A // 2:
                    deviations(0, NORM_A)
            deviations(NORM_A, NT)

        @block.gpsimd
        def _(eng):
            for t in range(NT):
                wait(eng, mm3, t - 1)
                nodes = slice(t * NP, (t + 1) * NP)
                for n, (c0, source) in enumerate(((0, h1t), (KC, aggt))):
                    eng.wait_ge(in_hi_at, 2 * t + n + 1)
                    eng.tensor_tensor(input_part(in_lo, t, c0), source[:, :, nodes],
                                      input_part(in_hi, t, c0).bitcast(F32), ALU.subtract)\
                        .then_inc(in_lo_at, 1)
                if t == 0:
                    eng.wait_ge(rows_in[3], 16)
                eng.tensor_tensor(x1[:, t, :], x1[:, t, :], rows[:, 3, :], ALU.add).then_inc(f1, 1)

        @block.vector
        def _(eng):
            def y_part(g):
                for t in turns[g]:
                    eng.wait_ge(mm4, t + 1)
                    eng.tensor_tensor(h1[:, t, :], h1[:, t, :], p4[0:NP, t % 2, :], ALU.add)\
                        .then_inc(y_a, 1)
                    eng.wait_ge(y_a, t + 1)
                    eng.tensor_tensor(h1[:, t, :], h1[:, t, :], rows[:, 1, :], ALU.add)\
                        .then_inc(y_at, 1)
                    eng.wait_ge(y_at, t + 1)
                    eng.bn_stats(stats[:, t, :], h1[:, t, :]).then_inc(stat, 1)

            def aggregate(t0, t1):
                for t in range(t0, t1):
                    eng.wait_ge(stat, t + 1)
                    eng.bn_aggr(mv[:, t, :], stats[:, t, :]).then_inc(aggr, 1)

            def inverse(batch, t0, t1):
                eng.wait_ge(std_at, batch + 1)
                eng.reciprocal(rstd[:, t0:t1], std[:, t0:t1]).then_inc(r_at, 1)
                eng.wait_ge(r_at, batch + 1)

            def normalise(t0, t1):
                for t in range(t0, t1):
                    eng.scalar_tensor_tensor(h1[:, t, :], h1[:, t, :], mv[:, t, 0:1], rows[:, 2, :],
                                             ALU.subtract, ALU.mult).then_inc(f2, 1)
                    eng.wait_ge(f2, t + 1)
                    eng.wait_ge(f1, t + 1)
                    eng.scalar_tensor_tensor(x1[:, t, :], h1[:, t, :], rstd[:, t:t + 1], x1[:, t, :],
                                             ALU.mult, ALU.add).then_inc(f3, 1)

            eng.memset(eps[:, :], EPS).then_inc(eps_at, 1)
            for c in range(KC):
                eng.wait_ge(w_hi_at, c + 1)
                eng.tensor_tensor(w3_lo[:, 2 * c:2 * c + 2, :], raw[:, 2 * c:2 * c + 2, :],
                                  w3_hi[:, 2 * c:2 * c + 2, :].bitcast(F32), ALU.subtract)\
                    .then_inc(w_lo_at, 1)
            eng.wait_ge(w_hi_at, KC + 1)
            eng.tensor_tensor(w4_lo[:, :, :], raw[:, 0:KC, :], w4_hi[:, :, :].bitcast(F32),
                              ALU.subtract).then_inc(w_lo_at, 1)
            for n in range(4):
                eng.wait_ge(rows_in[n], 16)
            for g, tiles in enumerate(turns):
                for t in tiles:
                    s, i = slot(t)
                    eng.wait_ge(mm3, t + 1)
                    if g >= 2:
                        eng.wait_ge(u_at, g - 1)
                    eng.tensor_tensor(Z[:, s, i, :], p3[0:NP, 2 * s + i, :], rows[:, 0, :], ALU.add)\
                        .then_inc(z_at, 1)
                eng.wait_ge(e_at, g + 1)
                eng.tensor_scalar(tiles_of(U, g), tiles_of(U, g), U_MAX, None, ALU.min)\
                    .then_inc(cut, 1)
                eng.wait_ge(t_at, g + 1)
                eng.tensor_tensor(tiles_of(U, g), tiles_of(U, g), tiles_of(Z, g), ALU.mult)\
                    .then_inc(u_at, 1)
                if g > 0:
                    y_part(g - 1)
                if g == NORM_A // 2:
                    aggregate(0, NORM_A)
                if g == NORM_A // 2 + 1:
                    inverse(0, 0, NORM_A)
                    normalise(0, NORM_A // 2)
                if g == NORM_A // 2 + 2:
                    normalise(NORM_A // 2, NORM_A)
                for t in tiles:
                    eng.wait_ge(ut_at, t + 1)
                    eng.tensor_tensor(ut_lo[:, t % 2, :].rearrange(view, c=KC)[:, :, 0:NP],
                                      pt[:, t % 2, :].rearrange(view, c=KC)[:, :, 0:NP],
                                      ut_hi[:, t % 2, :].rearrange(view, c=KC)[:, :, 0:NP]
                                      .bitcast(F32), ALU.subtract).then_inc(ut_lo_at, 1)
            y_part(len(turns) - 1)
            aggregate(NORM_A, NT)
            inverse(1, NORM_A, NT)
            normalise(NORM_A, NT)


def kernel(x, src, dst, edge_attr_64, edge_type_32, edge_weight1, L0_gnn_bases, L0_gnn_w_comp,
           L0_gnn_h_bias, L1_gnn_W1, L1_gnn_b1, L1_gnn_W2, L1_gnn_b2, L1_gnn_W3, L1_gnn_b3,
           L1_gnn_W4, L1_gnn_b4, L1_gnn_gamma, L1_gnn_beta):
    import numpy as np
    import concourse.bacc as bacc
    from concourse.bass_utils import run_bass_kernel_spmd

    def padded(a, fill):
        a = np.asarray(a).reshape(E)
        return np.concatenate([a, np.full(EPAD - E, fill, a.dtype)])

    def by_tile(a, fill):
        return np.ascontiguousarray(padded(a, fill).reshape(T, P).T)

    attr = np.zeros((ED, EPAD), np.asarray(edge_attr_64).dtype)
    attr[:, :E] = np.asarray(edge_attr_64).T
    given = {
        "x": x, "src_t": by_tile(src, 0), "dst_t": by_tile(dst, -1), "dst_e": padded(dst, -1), "etype": padded(edge_type_32, 0),
        "norm_t": by_tile(edge_weight1, 0), "edge_attr": attr, "bases": L0_gnn_bases,
        "w_comp": L0_gnn_w_comp, "h_bias": L0_gnn_h_bias, "w1": L1_gnn_W1, "b1": L1_gnn_b1,
        "w2": L1_gnn_W2, "b2": L1_gnn_b2, "w3": L1_gnn_W3, "b3": L1_gnn_b3, "w4": L1_gnn_W4,
        "b4": L1_gnn_b4, "gamma": L1_gnn_gamma, "beta": L1_gnn_beta,
    }
    nc = bacc.Bacc("TRN2", target_bir_lowering=False, num_devices=1)
    arrays, args = {}, []
    for name, a in given.items():
        a = np.ascontiguousarray(a)
        arrays[f"in_{name}"] = a
        args.append(nc.dram_tensor(f"in_{name}", a.shape, mybir.dt.from_np(a.dtype),
                                   kind="ExternalInput").ap())
    args.append(nc.dram_tensor("out_0", (N, D), F32, kind="ExternalOutput").ap())
    gnn_kernel(nc, *args)
    r = run_bass_kernel_spmd(nc, [arrays], core_ids=[0])
    return r.results[0]["out_0"]
```
